# Optimizing a Trainium2 kernel written in Bass

```python
import numpy as np
import jax
import jax.numpy as jnp

def _softmax(x, axis=-1):
    return jax.nn.softmax(x, axis=axis)

def _gelu(x):
    return jax.nn.gelu(x, approximate=True)

def _silu(x):
    return jax.nn.silu(x)

def _sigmoid(x):
    return jax.nn.sigmoid(x)

def _layernorm(x, axis=-1, eps=1e-05):
    m = jnp.mean(x, axis=axis, keepdims=True)
    v = jnp.var(x, axis=axis, keepdims=True)
    return (x - m) / jnp.sqrt(v + eps)

def _scatter_add(tgt, idx, src, axis=0):
    return tgt.at[idx].add(src)

def _segment_sum(src, seg, n):
    return jax.ops.segment_sum(src, seg, n)
kernel_name = 'mk_gnn_resnorm_d4_gnn_r8_3b2ffe'

def setup_inputs(seed: int=0):
    np.random.seed(seed)
    _w = jnp.asarray

    def _rec_inputs():
        import jax
        import jax.numpy as jnp
        _gk = jax.random.key(seed)
        x = -0.0002117 + 1 * jax.random.normal(jax.random.fold_in(_gk, 1), (6250, 256), jnp.float32)
        src = jax.random.randint(jax.random.fold_in(_gk, 2), (100000,), 0, 6250, jnp.int32)
        dst = jax.random.randint(jax.random.fold_in(_gk, 3), (100000,), 0, 6250, jnp.int32)
        _o = jnp.argsort(dst, stable=True)
        src = src[_o]
        dst = dst[_o]
        edge_type_16 = jax.random.randint(jax.random.fold_in(_gk, 13), (100000,), 0, 16, jnp.int32)
        edge_type_8 = jax.random.randint(jax.random.fold_in(_gk, 14), (100000,), 0, 8, jnp.int32)
        return (x, src, dst, edge_type_16, edge_type_8)
    x, src, dst, edge_type_16, edge_type_8 = _rec_inputs()

    def _L0_gnn_setup():
        import jax, jax.numpy as jnp
        import numpy as np
        N = 12500
        E = 200000
        IN = 256
        HID = 256
        EPS = 1e-05

        def _bn(h, gamma, beta):
            mean = jnp.mean(h, axis=0)
            var = jnp.var(h, axis=0)
            return gamma * (h - mean) * jax.lax.rsqrt(var + EPS) + beta
        key = jax.random.key(seed)
        ks = jax.random.split(key, 12)
        s_in = 1.0 / np.sqrt(IN)
        s_hid = 1.0 / np.sqrt(HID)
        return {'x': jax.random.normal(ks[0], (N, IN), dtype=jnp.float32), 'edge_index': jax.random.randint(ks[1], (2, E), 0, N, dtype=jnp.int64), 'w1': jax.random.uniform(ks[2], (HID, IN), jnp.float32, -s_in, s_in), 'b1': jax.random.uniform(ks[3], (HID,), jnp.float32, -s_in, s_in), 'g1': jnp.ones((HID,), jnp.float32), 'beta1': jnp.zeros((HID,), jnp.float32), 'wr': jax.random.uniform(ks[4], (HID, HID), jnp.float32, -s_hid, s_hid), 'br': jax.random.uniform(ks[5], (HID,), jnp.float32, -s_hid, s_hid), 'wroot': jax.random.uniform(ks[6], (HID, HID), jnp.float32, -s_hid, s_hid), 'w2': jax.random.uniform(ks[7], (IN, HID), jnp.float32, -s_hid, s_hid), 'b2': jax.random.uniform(ks[8], (IN,), jnp.float32, -s_hid, s_hid), 'g2': jnp.ones((IN,), jnp.float32), 'beta2': jnp.zeros((IN,), jnp.float32)}
    _L0_gnn_all = _L0_gnn_setup()
    _L0_gnn_in = {k: v for k, v in _L0_gnn_all.items() if k in ('w1', 'b1', 'g1', 'beta1', 'wr', 'br', 'wroot', 'w2', 'b2', 'g2', 'beta2')}
    del _L0_gnn_all

    def _L1_gnn_setup():
        import jax, jax.numpy as jnp
        import numpy as np
        N, E, D, R, L = (6250, 31250, 256, 8, 3)
        key = jax.random.key(seed)
        k = jax.random.split(key, 7)
        scale = 1.0 / np.sqrt(D)
        x = jax.random.normal(k[0], (N, D), dtype=jnp.float32)
        edge_index = jax.random.randint(k[1], (2, E), 0, N, dtype=jnp.int64)
        edge_type = jax.random.randint(k[2], (E,), 0, R, dtype=jnp.int64)
        W_rel = jax.random.normal(k[3], (L, R, D, D), dtype=jnp.float32) * scale
        W_root = jax.random.normal(k[4], (L, D, D), dtype=jnp.float32) * scale
        bias = jax.random.normal(k[5], (L, D), dtype=jnp.float32) * 0.02
        return {'x': x, 'edge_index': edge_index, 'edge_type': edge_type, 'W_rel': W_rel, 'W_root': W_root, 'bias': bias}
    _L1_gnn_all = _L1_gnn_setup()
    _L1_gnn_in = {k: v for k, v in _L1_gnn_all.items() if k in ('W_rel', 'W_root', 'bias')}
    del _L1_gnn_all

    def _L2_gnn_setup():
        import jax, jax.numpy as jnp
        import numpy as np
        N_NODES = 6250
        N_EDGES = 100000
        HDIM = 256
        NUMRELS = 16

        def _gru_cell(x, h, w_ih, w_hh, b_ih, b_hh):
            gi = x @ w_ih.T + b_ih
            gh = h @ w_hh.T + b_hh
            i_r, i_z, i_n = jnp.split(gi, 3, axis=-1)
            h_r, h_z, h_n = jnp.split(gh, 3, axis=-1)
            r = jax.nn.sigmoid(i_r + h_r)
            z = jax.nn.sigmoid(i_z + h_z)
            n = jnp.tanh(i_n + r * h_n)
            return (1.0 - z) * n + z * h
        key = jax.random.key(seed)
        ks = jax.random.split(key, 9)
        h = jax.random.normal(ks[0], (N_NODES, HDIM), dtype=jnp.float32)
        relvectors = jax.random.normal(ks[1], (NUMRELS, HDIM), dtype=jnp.float32)
        s = 1.0 / np.sqrt(HDIM)
        w_ih = jax.random.uniform(ks[2], (3 * HDIM, HDIM), minval=-s, maxval=s, dtype=jnp.float32)
        w_hh = jax.random.uniform(ks[3], (3 * HDIM, HDIM), minval=-s, maxval=s, dtype=jnp.float32)
        b_ih = jax.random.uniform(ks[4], (3 * HDIM,), minval=-s, maxval=s, dtype=jnp.float32)
        b_hh = jax.random.uniform(ks[5], (3 * HDIM,), minval=-s, maxval=s, dtype=jnp.float32)
        edge_src = jax.random.randint(ks[6], (N_EDGES,), 0, N_NODES, dtype=jnp.int32)
        edge_dst = jax.random.randint(ks[7], (N_EDGES,), 0, N_NODES, dtype=jnp.int32)
        edge_rel = jax.random.randint(ks[8], (N_EDGES,), 0, NUMRELS, dtype=jnp.int32)
        return {'h': h, 'relvectors': relvectors, 'w_ih': w_ih, 'w_hh': w_hh, 'b_ih': b_ih, 'b_hh': b_hh, 'edge_src': edge_src, 'edge_dst': edge_dst, 'edge_rel': edge_rel}
    _L2_gnn_all = _L2_gnn_setup()
    _L2_gnn_in = {k: v for k, v in _L2_gnn_all.items() if k in ('relvectors', 'w_ih', 'w_hh', 'b_ih', 'b_hh')}
    del _L2_gnn_all

    def _L3_gnn_setup():
        import jax, jax.numpy as jnp
        import numpy as np
        N = 6250
        E = 100000
        D = 256
        H = 4
        F = D // H

        def gat_layer(x, src, dst, W, att_src, att_dst, bias):
            n = x.shape[0]
            h = (x @ W).reshape(n, H, F)
            a_src = jnp.sum(h * att_src[None], axis=-1)
            a_dst = jnp.sum(h * att_dst[None], axis=-1)
            e = jax.nn.leaky_relu(a_src[src] + a_dst[dst], 0.2)
            m = jax.ops.segment_max(e, dst, num_segments=n)
            m = jnp.where(jnp.isfinite(m), m, 0.0)
            ex = jnp.exp(e - m[dst])
            denom = jax.ops.segment_sum(ex, dst, num_segments=n)
            alpha = ex / (denom[dst] + 1e-16)
            msg = h[src] * alpha[..., None]
            out = jax.ops.segment_sum(msg, dst, num_segments=n)
            return out.reshape(n, H * F) + bias
        key = jax.random.key(seed)
        ks = jax.random.split(key, 8)
        x = jax.random.normal(ks[0], (N, D), dtype=jnp.float32)
        edge_index = jax.random.randint(ks[1], (2, E), 0, N, dtype=jnp.int32)
        W = jax.random.normal(ks[2], (D, H * F), dtype=jnp.float32) * (1.0 / np.sqrt(D))
        att_src = jax.random.normal(ks[3], (H, F), dtype=jnp.float32) * (1.0 / np.sqrt(F))
        att_dst = jax.random.normal(ks[4], (H, F), dtype=jnp.float32) * (1.0 / np.sqrt(F))
        bias = jnp.zeros((D,), dtype=jnp.float32)
        ln_gamma = jnp.ones((D,), dtype=jnp.float32)
        ln_beta = jnp.zeros((D,), dtype=jnp.float32)
        return {'x': x, 'edge_index': edge_index, 'W': W, 'att_src': att_src, 'att_dst': att_dst, 'bias': bias, 'ln_gamma': ln_gamma, 'ln_beta': ln_beta}
    _L3_gnn_all = _L3_gnn_setup()
    _L3_gnn_in = {k: v for k, v in _L3_gnn_all.items() if k in ('W', 'att_src', 'att_dst', 'bias', 'ln_gamma', 'ln_beta')}
    del _L3_gnn_all
    return {'x': x, 'src': src, 'dst': dst, 'edge_type_16': edge_type_16, 'edge_type_8': edge_type_8, 'L0_gnn_w1': _L0_gnn_in['w1'], 'L0_gnn_b1': _L0_gnn_in['b1'], 'L0_gnn_g1': _L0_gnn_in['g1'], 'L0_gnn_beta1': _L0_gnn_in['beta1'], 'L0_gnn_wr': _L0_gnn_in['wr'], 'L0_gnn_br': _L0_gnn_in['br'], 'L0_gnn_wroot': _L0_gnn_in['wroot'], 'L0_gnn_w2': _L0_gnn_in['w2'], 'L0_gnn_b2': _L0_gnn_in['b2'], 'L0_gnn_g2': _L0_gnn_in['g2'], 'L0_gnn_beta2': _L0_gnn_in['beta2'], 'L1_gnn_W_rel': _L1_gnn_in['W_rel'], 'L1_gnn_W_root': _L1_gnn_in['W_root'], 'L1_gnn_bias': _L1_gnn_in['bias'], 'L2_gnn_relvectors': _L2_gnn_in['relvectors'], 'L2_gnn_w_ih': _L2_gnn_in['w_ih'], 'L2_gnn_w_hh': _L2_gnn_in['w_hh'], 'L2_gnn_b_ih': _L2_gnn_in['b_ih'], 'L2_gnn_b_hh': _L2_gnn_in['b_hh'], 'L3_gnn_W': _L3_gnn_in['W'], 'L3_gnn_att_src': _L3_gnn_in['att_src'], 'L3_gnn_att_dst': _L3_gnn_in['att_dst'], 'L3_gnn_bias': _L3_gnn_in['bias'], 'L3_gnn_ln_gamma': _L3_gnn_in['ln_gamma'], 'L3_gnn_ln_beta': _L3_gnn_in['ln_beta']}

def reference(x, src, dst, edge_type_16, edge_type_8, L0_gnn_w1, L0_gnn_b1, L0_gnn_g1, L0_gnn_beta1, L0_gnn_wr, L0_gnn_br, L0_gnn_wroot, L0_gnn_w2, L0_gnn_b2, L0_gnn_g2, L0_gnn_beta2, L1_gnn_W_rel, L1_gnn_W_root, L1_gnn_bias, L2_gnn_relvectors, L2_gnn_w_ih, L2_gnn_w_hh, L2_gnn_b_ih, L2_gnn_b_hh, L3_gnn_W, L3_gnn_att_src, L3_gnn_att_dst, L3_gnn_bias, L3_gnn_ln_gamma, L3_gnn_ln_beta):
    import jax
    import jax.numpy as jnp

    def _L0_gnn_ref(x, edge_index, w1, b1, g1, beta1, wr, br, wroot, w2, b2, g2, beta2):
        import jax, jax.numpy as jnp
        import numpy as np
        N = 12500
        E = 200000
        IN = 256
        HID = 256
        EPS = 1e-05

        def _bn(h, gamma, beta):
            mean = jnp.mean(h, axis=0)
            var = jnp.var(h, axis=0)
            return gamma * (h - mean) * jax.lax.rsqrt(var + EPS) + beta
        n = x.shape[0]
        h = _bn(x @ w1.T + b1, g1, beta1)
        src, dst = (edge_index[0], edge_index[1])
        agg = jax.ops.segment_sum(h[src], dst, num_segments=n)
        conv = agg @ wr.T + br + h @ wroot.T
        h = jax.nn.gelu(conv, approximate=False)
        out = _bn(h @ w2.T + b2, g2, beta2) + x
        return out

    def _L1_gnn_ref(x, edge_index, edge_type, W_rel, W_root, bias):
        import jax, jax.numpy as jnp
        import numpy as np
        N, E, D, R, L = (6250, 31250, 256, 8, 3)
        src, dst = (edge_index[0], edge_index[1])
        n_layers = W_rel.shape[0]
        for l in range(n_layers):
            xr = jnp.einsum('nd,rde->rne', x, W_rel[l])
            msg = xr[edge_type, src]
            agg = jax.ops.segment_sum(msg, dst, num_segments=x.shape[0])
            x = jax.nn.relu(agg + x @ W_root[l] + bias[l])
        return x

    def _L2_gnn_ref(h, relvectors, w_ih, w_hh, b_ih, b_hh, edge_src, edge_dst, edge_rel):
        import jax, jax.numpy as jnp
        import numpy as np
        N_NODES = 6250
        N_EDGES = 100000
        HDIM = 256
        NUMRELS = 16

        def _gru_cell(x, h, w_ih, w_hh, b_ih, b_hh):
            gi = x @ w_ih.T + b_ih
            gh = h @ w_hh.T + b_hh
            i_r, i_z, i_n = jnp.split(gi, 3, axis=-1)
            h_r, h_z, h_n = jnp.split(gh, 3, axis=-1)
            r = jax.nn.sigmoid(i_r + h_r)
            z = jax.nn.sigmoid(i_z + h_z)
            n = jnp.tanh(i_n + r * h_n)
            return (1.0 - z) * n + z * h
        msg = h[edge_src] + relvectors[edge_rel]
        red = jax.ops.segment_sum(msg, edge_dst, num_segments=h.shape[0])
        return _gru_cell(red, h, w_ih, w_hh, b_ih, b_hh)

    def _L3_gnn_ref(x, edge_index, W, att_src, att_dst, bias, ln_gamma, ln_beta):
        import jax, jax.numpy as jnp
        import numpy as np
        N = 6250
        E = 100000
        D = 256
        H = 4
        F = D // H

        def gat_layer(x, src, dst, W, att_src, att_dst, bias):
            n = x.shape[0]
            h = (x @ W).reshape(n, H, F)
            a_src = jnp.sum(h * att_src[None], axis=-1)
            a_dst = jnp.sum(h * att_dst[None], axis=-1)
            e = jax.nn.leaky_relu(a_src[src] + a_dst[dst], 0.2)
            m = jax.ops.segment_max(e, dst, num_segments=n)
            m = jnp.where(jnp.isfinite(m), m, 0.0)
            ex = jnp.exp(e - m[dst])
            denom = jax.ops.segment_sum(ex, dst, num_segments=n)
            alpha = ex / (denom[dst] + 1e-16)
            msg = h[src] * alpha[..., None]
            out = jax.ops.segment_sum(msg, dst, num_segments=n)
            return out.reshape(n, H * F) + bias
        n = x.shape[0]
        loops = jnp.arange(n, dtype=edge_index.dtype)
        src = jnp.concatenate([edge_index[0], loops])
        dst = jnp.concatenate([edge_index[1], loops])
        h = gat_layer(x, src, dst, W, att_src, att_dst, bias)
        y = h + x
        mu = jnp.mean(y, axis=-1, keepdims=True)
        var = jnp.mean((y - mu) ** 2, axis=-1, keepdims=True)
        y = (y - mu) / jnp.sqrt(var + 1e-05) * ln_gamma + ln_beta
        return jax.nn.relu(y)
    edge_index = jnp.stack([src, dst])
    x = _layernorm(x + _L0_gnn_ref(x, edge_index, L0_gnn_w1, L0_gnn_b1, L0_gnn_g1, L0_gnn_beta1, L0_gnn_wr, L0_gnn_br, L0_gnn_wroot, L0_gnn_w2, L0_gnn_b2, L0_gnn_g2, L0_gnn_beta2), axis=-1)
    x = _layernorm(x + _L1_gnn_ref(x, edge_index, edge_type_8, L1_gnn_W_rel, L1_gnn_W_root, L1_gnn_bias), axis=-1)
    x = _layernorm(x + _L2_gnn_ref(x, L2_gnn_relvectors, L2_gnn_w_ih, L2_gnn_w_hh, L2_gnn_b_ih, L2_gnn_b_hh, src, dst, edge_type_16), axis=-1)
    x = _layernorm(x + _L3_gnn_ref(x, edge_index, L3_gnn_W, L3_gnn_att_src, L3_gnn_att_dst, L3_gnn_bias, L3_gnn_ln_gamma, L3_gnn_ln_beta), axis=-1)
    return x

_drawn_inputs = setup_inputs


def setup_inputs(seed=0):
    import zlib

    import numpy as np

    out = dict(_drawn_inputs(seed))
    spreads = {'L0_gnn_g1': (1.0, 0.2),
     'L0_gnn_beta1': (0.0, 0.1),
     'L0_gnn_g2': (1.0, 0.2),
     'L0_gnn_beta2': (0.0, 0.1),
     'L3_gnn_bias': (0.0, 0.1),
     'L3_gnn_ln_gamma': (1.0, 0.2),
     'L3_gnn_ln_beta': (0.0, 0.1)}
    factors = {'L0_gnn_b1': 8.0,
     'L0_gnn_br': 8.0,
     'L0_gnn_b2': 8.0,
     'L1_gnn_bias': 8.0,
     'L2_gnn_b_ih': 8.0,
     'L2_gnn_b_hh': 8.0,
     'L3_gnn_att_dst': 3.178}
    for name, (base, spread) in spreads.items():
        noise = np.random.default_rng([zlib.crc32(name.encode()), seed]).standard_normal(out[name].shape)
        drawn = base * np.exp(spread * noise) if base else spread * noise
        out[name] = jnp.asarray(drawn.astype(out[name].dtype))
    for name, factor in factors.items():
        out[name] = (out[name] * factor).astype(out[name].dtype)
    return out
```

```python
from contextlib import ExitStack

import concourse.bass as bass
from concourse import mybir

F32 = mybir.dt.float32
BF16 = mybir.dt.bfloat16
I32 = mybir.dt.int32
ALU = mybir.AluOpType
ACT = mybir.ActivationFunctionType
AX = mybir.AxisListType.X

P = 128
N, D, E = 6250, 256, 100000
NT = -(-N // P)
NP = NT * P
LAST = N - (NT - 1) * P
EC = -(-E // P)
ELAST = E - (P - 1) * EC
TU = 7
TI = NT // TU
U = 16
HALF = U // 2
MAXCH = (P * EC + (NT + 1) * (P - 1)) // P
CI = -(-MAXCH // U)
NCH = CI * U
NB = NT + 1
SU = 16
SI = EC // SU
SREST = EC - SI * SU
R1, L1 = 8, 3
R2 = 16
H, F = 4, 64
G3 = 3 * D
KD = D // P
W3 = D + H
EPS = 1e-5
BIG = float(2 ** 100)
BANKS = 4
OHS = 4
RING = 4
RING2 = 8
LAGS = 10
HA = 2
NPH = 8
READY = 4
assert NT == TU * TI and NCH == U * CI
assert all(U * min(t + READY, CI) * NT >= (t + 1) * NCH for t in range(NT)) and CI - READY <= NT


class Link:

    def __init__(self, eng, sem):
        self.eng, self.sem, self.base, self.n = eng, sem, 0, 0

    def __call__(self, ins):
        self.n += 1
        ins.then_inc(self.sem, 1)
        self.eng.wait_ge(self.sem, self.base + self.n)

    def enter(self, i, per_trip):
        self.outer, self.per_trip = self.base + self.n, per_trip
        self.base, self.n = self.outer + per_trip * i, 0

    def leave(self, trips):
        assert self.n == self.per_trip, self.n
        self.base, self.n = self.outer + self.per_trip * trips, 0


def program(nc, a, out):
    ctx = ExitStack()
    with ctx:
        def sb(name, shape, dt=F32):
            return ctx.enter_context(nc.sbuf_tensor(name, shape, dt))

        def sem(name):
            return ctx.enter_context(nc.semaphore(name))

        def dram(name, shape, dt=F32):
            return nc.dram_tensor(name, shape, dt, kind="Internal").ap()

        slots_d = dram("slots_d", [P * NCH, 4], I32)
        rows_d = dram("rows_d", [NP, D])
        rel_d = [dram(f"rel_d{k}", [R1 * NP, D]) for k in range(2)]
        att_d = dram("att_d", [NP, W3])
        src_logit_d = dram("src_logit_d", [NP, H])

        X = sb("X", [P, NT, D])
        A = sb("A", [P, NT, W3])
        Y = sb("Y", [P, NT * D])
        Y3 = Y[:, :].rearrange("p (t d) -> p t d", d=D)
        edges = sb("edges", [P, 4, NCH], I32)
        edges_f = edges[:, :, :].bitcast(F32)
        blank = edges[:, :, :].rearrange("p w c -> p (w c)").rearrange("p (c w) -> p c w", w=4)
        g = sb("g", [P, U, D + R2])
        gflat = g[:, :, :].rearrange("p u d -> p (u d)")
        bucket_of = sb("bucket_of", [1, NCH], I32)
        order_of = sb("order_of", [1, NT], I32)
        wt = sb("wt", [P, 4, KD, D])
        rows0 = sb("rows0", [P, 7, D])
        col = sb("col", [P, P])
        ident = sb("ident", [P, P])
        ones = sb("ones", [P, P])
        big_ident = sb("big_ident", [P, H, P], BF16)
        stage = sb("stage", [P, 2, D])
        turned = sb("turned", [P, 2, D])
        oh = sb("oh", [P, OHS, P])
        idx = sb("idx", [P, U], I32)
        small = sb("small", [P, 64])
        ps = ctx.enter_context(nc.psum_tensor("ps", [P, 8, 512], F32))

        aflat = A[:, :, :].rearrange("p t d -> p (t d)")

        def tmp(k, dt=F32):
            v = aflat[:, k * EC:(k + 1) * EC]
            return v if dt == F32 else v.bitcast(dt)

        payload = gflat[:, 0:4 * EC].rearrange("p (e w) -> p e w", w=4).bitcast(I32)
        payload_f = gflat[:, 0:4 * EC].rearrange("p (e w) -> p e w", w=4)
        loaded = gflat[:, 0:4 * NCH].rearrange("p (c w) -> p c w", w=4).bitcast(I32)
        slot_row = gflat[:, 4 * EC:5 * EC].bitcast(I32)
        at0 = 5 * EC
        sc_idx = gflat[:, at0:at0 + SU].bitcast(I32)
        sc_pay = gflat[:, at0 + SU:at0 + 5 * SU].rearrange("p (u w) -> p u w", w=4).bitcast(I32)
        iota_b = aflat[:, 10 * EC:10 * EC + NB]
        cnt_b, before_b, tot_b, nch_b, end_b, base_b, first_b, key_b, rank_b, order_f = (
            aflat[:, 10 * EC + 64 * k:10 * EC + 64 * k + NB] for k in range(1, 11))
        upper = aflat[:, 10 * EC + 704:10 * EC + 704 + P]
        chunk_no = aflat[:, 12 * EC:12 * EC + NCH]
        bucket_f = aflat[:, 13 * EC + 64:13 * EC + 64 + NCH]
        pairs = aflat[:, 0:NB * NB].rearrange("p (b c) -> p b c", b=NB)
        from_first, from_end = (aflat[0:1, k * NCH:(k + 1) * NCH] for k in range(2))
        pmask = small[:, 60:61]
        prow = small[:, 61:62]

        nat0 = Y[:, 0:4 * KD * D].rearrange("p (w b d) -> p w b d", w=4, b=KD)
        wrel = [Y[:, b * KD * R1 * D:(b + 1) * KD * R1 * D].rearrange(
            "p (k r d) -> p k r d", k=KD, r=R1) for b in range(2)]
        o1 = 2 * KD * R1 * D
        wroot1 = Y[:, o1:o1 + L1 * KD * D].rearrange("p (l k d) -> p l k d", l=L1, k=KD)
        bias1 = Y[:, o1 + L1 * KD * D:o1 + L1 * KD * D + L1 * D].rearrange("p (l d) -> p l d", l=L1)
        rel_out = gflat[:, 0:2 * R1 * D].rearrange("p (s r d) -> p s r d", s=2, r=R1)
        quarter = wt[:, :, :, :].rearrange("p w k d -> p w (k d)")
        nb2 = G3 // P
        nat2 = Y[:, 0:2 * nb2 * D].rearrange("p (w b d) -> p w b d", w=2, b=nb2)
        o2 = 2 * nb2 * D
        wt2 = Y[:, o2:o2 + 2 * KD * G3].rearrange("p (w k d) -> p w k d", w=2, k=KD)
        o2 += 2 * KD * G3
        b_ih, b_hh = Y[:, o2:o2 + G3], Y[:, o2 + G3:o2 + 2 * G3]
        o2 += 2 * G3
        relvec = Y[0:R2, o2:o2 + D]
        o2 += D
        counts = Y[:, o2:o2 + NT * R2].rearrange("p (t r) -> p t r", r=R2)
        o2 += NT * R2
        cstage = Y[:, o2:o2 + 2 * R2].rearrange("p (s r) -> p s r", s=2)
        o2 += 2 * R2
        cturned = Y[0:R2, o2:o2 + 2 * P].rearrange("p (s n) -> p s n", s=2)
        o2 += 2 * P
        stage2 = Y[:, o2:o2 + 2 * D].rearrange("p (s d) -> p s d", s=2)
        o2 += 2 * D
        turned2 = Y[:, o2:o2 + 2 * D].rearrange("p (s d) -> p s d", s=2)
        o2 += 2 * D
        gates = g[:, 0:2, :].rearrange("p s d -> p (s d)")[:, 0:2 * D]
        hn = g[:, 2, 0:D]
        inn = g[:, 3, 0:D]
        nn = g[:, 4, 0:D]
        relvec_t = Y[:, o2:o2 + KD * R2].rearrange("p (k r) -> p k r", k=KD)
        o2 += KD * R2
        rel_gates = Y[0:R2, o2:o2 + G3]
        o2 += G3
        assert o2 <= NT * D
        w3 = Y[:, 0:KD * D].rearrange("p (k d) -> p k d", k=KD)
        o3 = KD * D
        att_s, att_t, bias3, gamma3, beta3 = (Y[:, o3 + k * D:o3 + (k + 1) * D] for k in range(5))
        o3 += 5 * D
        src_l, max_l, t_l, ex_l = (
            Y[:, o3 + k * NT * H:o3 + (k + 1) * NT * H].rearrange("p (t h) -> p t h", h=H) for k in range(4))
        o3 += 4 * NT * H
        dst_max = Y[:, o3:o3 + NT * 2 * H].rearrange("p (t h) -> p t h", h=2 * H)
        o3 += NT * 2 * H
        att_row = Y[:, o3:o3 + 2 * W3].rearrange("p (s d) -> p s d", s=2)
        o3 += 2 * W3
        att_tmp = Y[:, o3:o3 + D]
        o3 += D
        diag = Y[:, o3:o3 + RING * H * P].rearrange("p (s h e) -> p s h e", s=RING, h=H)
        o3 += RING * H * P
        miss = Y[:, o3:o3 + RING2 * P // 2].bitcast(BF16).rearrange("p (s n) -> p s n", s=RING2)
        o3 += RING2 * P // 2
        red = Y[:, o3:o3 + RING * H].rearrange("p (s h) -> p s h", s=RING)
        o3 += RING * H
        ohT = Y[:, o3:o3 + RING * P].rearrange("p (s e) -> p s e", s=RING)
        o3 += RING * P
        lg = Y[:, o3:o3 + RING * 4 * H].rearrange("p (s h) -> p s h", s=RING)
        o3 += RING * 4 * H
        wrow = Y[:, o3:o3 + RING2 * W3].rearrange("p (s d) -> p s d", s=RING2)
        o3 += RING2 * W3
        ohb = Y[:, o3:o3 + U * P].rearrange("p (s n) -> p s n", s=U)
        o3 += U * P
        assert o3 <= NT * D
        sflat = stage[:, :, :].rearrange("p s d -> p (s d)")
        stats = sflat[:, 0:NT * 6].rearrange("p (t s) -> p t s", s=6)
        mv = sflat[:, NT * 6:NT * 8].rearrange("p (t s) -> p t s", s=2)
        mean_b, scale_b = stage[:, 0, :], stage[:, 1, :]
        out0 = oh[:, :, :].rearrange("p (s q) n -> p s (q n)", s=2)

        s_dve = sem("s_dve")
        s_pool = sem("s_pool")
        s_const = sem("s_const")
        s_ident = sem("s_ident")
        s_edge_in = sem("s_edge_in")
        s_edge_pad = sem("s_edge_pad")
        s_x_pad = sem("s_x_pad")
        s_w0 = sem("s_w0")
        s_rows0 = sem("s_rows0")
        s_turn_w = sem("s_turn_w")
        s_wt = sem("s_wt")
        s_cnt = sem("s_cnt")
        s_tot = sem("s_tot")
        s_slot = sem("s_slot")
        s_blank = sem("s_blank")
        s_blank_d = sem("s_blank_d")
        s_sc = [sem(f"s_sc{k}") for k in range(2)]
        s_scat = sem("s_scat")
        s_edges = sem("s_edges")
        s_planes = sem("s_planes")
        s_stage = [sem(f"s_stage{k}") for k in range(NPH)]
        s_turn = [sem(f"s_turn{k}") for k in range(NPH)]
        s_turned = [sem(f"s_turned{k}") for k in range(NPH)]
        s_prod = [sem(f"s_prod{k}") for k in range(NPH)]
        s_evac = [sem(f"s_evac{k}") for k in range(NPH)]
        s_y = sem("s_y")
        s_sum = sem("s_sum")
        s_dev = sem("s_dev")
        s_sq = sem("s_sq")
        s_sq_used = sem("s_sq_used")
        s_h = sem("s_h")
        s_out0 = [sem(f"s_out0{k}") for k in range(2)]
        s_table = sem("s_table")
        s_var = sem("s_var")
        s_root = sem("s_root")
        s_acc0 = sem("s_acc0")
        s_x = sem("s_x")
        s_idx = [sem(f"s_idx{k}") for k in range(2)]
        s_g = [sem(f"s_g{k}") for k in range(U)]
        s_issue = sem("s_issue")
        s_oh = sem("s_oh")
        s_mm = sem("s_mm")
        s_add = sem("s_add")
        s_wrel = [sem(f"s_wrel{k}") for k in range(L1)]
        s_rel_mm = sem("s_rel_mm")
        s_rel_dve = sem("s_rel_dve")
        s_rel_act = sem("s_rel_act")
        s_rel_out = [sem(f"s_rel_out{k}") for k in range(2)]
        s_quarter_mm = sem("s_quarter_mm")
        s_quarter = sem("s_quarter")
        s_quarter_out = [sem(f"s_quarter_out{k}") for k in range(4)]
        s_w2 = sem("s_w2")
        s_turn_w2 = sem("s_turn_w2")
        s_gru_w = sem("s_gru_w")
        s_rz = sem("s_rz")
        s_gates = sem("s_gates")
        s_cand = sem("s_cand")
        s_tanh = sem("s_tanh")
        s_gru = sem("s_gru")
        s_w3 = sem("s_w3")
        s_att_row = sem("s_att_row")
        s_att_out = [sem(f"s_att_out{k}") for k in range(2)]
        s_logit = sem("s_logit")
        s_diag = sem("s_diag")
        s_diag_dve = sem("s_diag_dve")
        s_miss = sem("s_miss")
        s_spread = sem("s_spread")
        s_red = sem("s_red")
        s_maxed = sem("s_maxed")
        s_shift = sem("s_shift")
        s_self = sem("s_self")
        s_ohb = sem("s_ohb")
        s_oht = sem("s_oht")
        s_ohts = sem("s_ohts")
        s_dm = sem("s_dm")
        s_l0 = sem("s_l0")
        s_l1 = sem("s_l1")
        s_e = sem("s_e")
        s_ex = sem("s_ex")
        s_wr = sem("s_wr")
        s_wr_act = sem("s_wr_act")
        s_mm3 = sem("s_mm3")
        s_add3 = sem("s_add3")
        s_out = sem("s_out")

        block = ctx.enter_context(nc.Block())
        edge_in = [a["dst"], a["src"], a["edge_type_8"], a["edge_type_16"]]
        vec0 = ["L0_gnn_b1", "L0_gnn_g1", "L0_gnn_beta1", "L0_gnn_br", "L0_gnn_b2", "L0_gnn_g2", "L0_gnn_beta2"]
        mat0 = ["L0_gnn_w1", "L0_gnn_wr", "L0_gnn_wroot", "L0_gnn_w2"]
        B1, G1, BETA1, BR, B2, G2, BETA2 = (rows0[:, k, :] for k in range(7))
        A2 = A[:, :, 0:D]

        def all_rows(v):
            return v.rearrange("(o d) -> o d", o=1).broadcast_to([P, v.shape[0]])

        def over_tiles(v):
            return v.rearrange("p (o d) -> p o d", o=1).broadcast_to([P, NT, D])

        def tile_at(v, t, width=D):
            return v[:, bass.ds(t, 1), 0:width].rearrange("p o d -> p (o d)")

        def node_rows(table):
            return table.rearrange("(t p) d -> p t d", p=P)

        def before(j):
            return j if j == 0 else j - 1

        out_uses = [TI * ((TU + 1) // 2), TI * (TU // 2)]

        def buckets_of(engine, i):
            _, values = nc.values_load_multi_w_load_instructions(
                bucket_of[0:1, bass.ds(U * i, U)], engines=(engine,), min_val=0, max_val=NT - 1,
                skip_runtime_bounds_check_because="a bucket's number counts which of NT - 1 ends lie before a chunk")
            return values

        def bucket_by_size(engine, t):
            _, values = nc.values_load_multi_w_load_instructions(
                order_of[0:1, bass.ds(t, 1)], engines=(engine,), min_val=0, max_val=NT - 1,
                skip_runtime_bounds_check_because="the buckets' numbers in another order")
            return values[0]

        def beside_sweep(eng, trip, dense):
            with eng.Fori(0, READY) as i:
                trip(i, None)
            with eng.Fori(READY, CI) as i:
                trip(i, i - READY)
            for t in range(CI - READY, NT):
                dense(t)

        def trips(eng, trip):
            trip(0, lambda k, lag: k >= lag, U)
            with eng.Fori(1, CI) as i:
                trip(i, lambda k, lag: True, U)
            trip(CI, lambda k, lag: k < lag, LAGS)

        def lagged_buckets(engine, i, lag):
            first, last = isinstance(i, int) and i == 0, isinstance(i, int) and i == CI
            at, n = (0, U - lag) if first else (U * i - lag, lag if last else U)
            _, values = nc.values_load_multi_w_load_instructions(
                bucket_of[0:1, bass.ds(at, n)], engines=(engine,), min_val=0, max_val=NT - 1,
                skip_runtime_bounds_check_because="a bucket's number counts which of NT - 1 ends lie before a chunk")
            return (0,) * lag + tuple(values) if first else values

        @block.sync
        def _(sp):
            sp.wait_ge(s_edge_pad, 4)
            for k, v in enumerate(edge_in):
                sp.dma_start(tmp(k, I32)[0:P - 1, :], v[0:(P - 1) * EC].rearrange("(p e) -> p e", e=EC))\
                    .then_inc(s_edge_in, 16)
                sp.dma_start(tmp(k, I32)[P - 1:P, 0:ELAST], v[(P - 1) * EC:E].rearrange("(o e) -> o e", o=1))\
                    .then_inc(s_edge_in, 16)
            for k, n in enumerate(mat0):
                sp.dma_start(nat0[:, k], a[n].rearrange("(b p) d -> p b d", p=P)).then_inc(s_w0, 16)
            for k, n in enumerate(vec0):
                sp.dma_start(rows0[:, k, :], all_rows(a[n])).then_inc(s_rows0, 16)
            sp.wait_ge(s_x_pad, 1)
            sp.dma_start(X[:, 0:NT - 1, :], node_rows(a["x"][0:(NT - 1) * P, :])).then_inc(s_out0[0], 16)
            sp.dma_start(X[0:LAST, NT - 1, :], a["x"][(NT - 1) * P:N, :]).then_inc(s_out0[1], 16)
            sp.wait_ge(s_blank, 1)
            sp.dma_start(slots_d.rearrange("(p c) w -> p c w", p=P), blank).then_inc(s_blank_d, 16)
            with sp.Fori(0, TI) as i:
                for j in range(TU):
                    sp.wait_ge(s_evac[1], 1 + TU * i + j + 1)
                    sp.dma_start(rows_d[bass.ds((TU * i + j) * P, P), :], out0[:, j % 2, :])\
                        .then_inc(s_out0[j % 2], 16)
            def sweep_indices(order, word, used, ahead):
                with sp.Fori(0, CI) as i:
                    for h in range(2):
                        sp.wait_ge(used, ahead + U * i + HALF * (h + 1))
                        sp.dma_start(idx[:, HALF * h:HALF * (h + 1)],
                                     edges[:, word, bass.ds(U * i + HALF * h, HALF)]).then_inc(s_idx[h], 16)

            sp.wait_ge(s_planes, 4)
            sweep_indices(0, 0, s_mm, 0)
            sp.wait_ge(s_x, 1)
            sp.dma_start(wroot1, a["L1_gnn_W_root"].rearrange("l (k p) d -> p l k d", p=P)).then_inc(s_rel_out[0], 16)
            sp.dma_start(bias1, a["L1_gnn_bias"].rearrange("(o l) d -> o l d", o=1).broadcast_to([P, L1, D]))\
                .then_inc(s_rel_out[1], 16)

            def load_wrel(layer):
                for k in range(KD):
                    sp.dma_start(wrel[layer % 2][:, k], a["L1_gnn_W_rel"][layer, :, k * P:(k + 1) * P, :]
                                 .rearrange("r p d -> p r d")).then_inc(s_wrel[layer], 16)

            load_wrel(0)
            load_wrel(1)
            with sp.Fori(0, TI) as i:
                for j in range(TU):
                    done = 2 * (TU * i + j + 1)
                    sp.wait_ge(s_rel_dve, 1 + done)
                    sp.wait_ge(s_rel_act, 1 + done)
                    sp.dma_start(rel_d[0].rearrange("(r n) d -> n r d", r=R1)[bass.ds((TU * i + j) * P, P), :, :],
                                 rel_out[:, j % 2]).then_inc(s_rel_out[j % 2], 16)
            sp.wait_ge(s_prod[3], 1 + NT)
            load_wrel(2)
            for layer in range(L1):
                sweep_indices(1 + layer, 1, s_mm, NCH * (1 + layer))
            sp.wait_ge(s_x, 2)
            sp.dma_start(node_rows(rows_d), X[:, :, :]).then_inc(s_table, 16)
            for k, n in enumerate(["L2_gnn_w_ih", "L2_gnn_w_hh"]):
                sp.dma_start(nat2[:, k], a[n].rearrange("(b p) d -> p b d", p=P)).then_inc(s_w2, 16)
            sp.dma_start(b_ih, all_rows(a["L2_gnn_b_ih"])).then_inc(s_w2, 16)
            sp.dma_start(b_hh, all_rows(a["L2_gnn_b_hh"])).then_inc(s_w2, 16)
            sp.dma_start(relvec, a["L2_gnn_relvectors"]).then_inc(s_w2, 16)
            sweep_indices(4, 0, s_mm, NCH * 4)
            sp.wait_ge(s_x, 3)
            sp.dma_start(w3, a["L3_gnn_W"].rearrange("(k p) d -> p k d", p=P)).then_inc(s_att_out[0], 16)
            sp.dma_start(att_s, all_rows(a["L3_gnn_att_src"].rearrange("h f -> (h f)"))).then_inc(s_att_out[1], 16)
            sp.dma_start(att_t, all_rows(a["L3_gnn_att_dst"].rearrange("h f -> (h f)"))).then_inc(s_w3, 16)
            for v, n in ((bias3, "L3_gnn_bias"), (gamma3, "L3_gnn_ln_gamma"), (beta3, "L3_gnn_ln_beta")):
                sp.dma_start(v, all_rows(a[n])).then_inc(s_w3, 16)
            with sp.Fori(0, TI) as i:
                for j in range(TU):
                    sp.wait_ge(s_att_row, TU * i + j + 1)
                    sp.dma_start(att_d[bass.ds((TU * i + j) * P, P), :], att_row[:, j % 2, :])\
                        .then_inc(s_att_out[j % 2], 16)
            sp.wait_ge(s_logit, 1)
            sp.dma_start(node_rows(src_logit_d), src_l).then_inc(s_table, 16)
            for order in (5, 6):
                with sp.Fori(0, CI) as i:
                    for h in range(2):
                        for j in range(HALF * h, HALF * (h + 1)):
                            sp.wait_ge(s_g[j], 16 * (CI * order + i))
                        sp.dma_start(idx[:, HALF * h:HALF * (h + 1)],
                                     edges[:, 0, bass.ds(U * i + HALF * h, HALF)]).then_inc(s_idx[h], 16)
            sp.wait_ge(s_x, 4)
            sp.dma_start(node_rows(out[0:(NT - 1) * P, :]), X[:, 0:NT - 1, :]).then_inc(s_out, 16)
            sp.dma_start(out[(NT - 1) * P:N, :], X[0:LAST, NT - 1, :]).then_inc(s_out, 16)
            sp.wait_ge(s_out, 32)

        @block.gpsimd
        def _(pool):
            link = Link(pool, s_pool)
            pool.memset(tmp(0, I32), NT * P).then_inc(s_edge_pad, 1)
            for k in range(1, 4):
                pool.memset(tmp(k, I32), 0).then_inc(s_edge_pad, 1)
            pool.iota(col[:, :], pattern=[[1, P]], base=0, channel_multiplier=0,
                      allow_small_or_imprecise_dtypes=True).then_inc(s_const, 1)
            pool.iota(prow, pattern=[[1, 1]], base=0, channel_multiplier=1,
                      allow_small_or_imprecise_dtypes=True).then_inc(s_const, 1)
            pool.iota(iota_b, pattern=[[1, NB]], base=0, channel_multiplier=0,
                      allow_small_or_imprecise_dtypes=True).then_inc(s_const, 1)
            pool.iota(chunk_no, pattern=[[1, NCH]], base=0, channel_multiplier=0,
                      allow_small_or_imprecise_dtypes=True).then_inc(s_const, 1)
            pool.memset(ones[:, :], 1.0).then_inc(s_const, 1)
            pool.memset(X[:, NT - 1, :], 0.0).then_inc(s_x_pad, 1)
            link(pool.memset(blank, 0))
            pool.memset(blank.bitcast(F32)[:, :, 2:3], float(P)).then_inc(s_blank, 1)

            pool.wait_ge(s_slot, 1)
            pool.wait_ge(s_blank_d, 16)

            def scatter(k, s):
                pool.indirect_dma_start(
                    out=slots_d, out_offset=bass.IndirectOffsetOnAxis(ap=sc_idx[:, k:k + 1], axis=0),
                    in_=sc_pay[:, k, :], in_offset=None).then_inc(s, 16)

            half = SU // 2

            def stage_edges(at, h):
                link(pool.tensor_copy(sc_idx[:, half * h:half * (h + 1)], slot_row[:, bass.ds(at, half)]))
                link(pool.tensor_copy(sc_pay[:, half * h:half * (h + 1), :], payload[:, bass.ds(at, half), :]))
                pool.sem_inc(s_issue, 1)
                for k in range(half * h, half * (h + 1)):
                    scatter(k, s_sc[h])

            stage_edges(0, 0)
            stage_edges(half, 1)
            with pool.Fori(1, SI) as i:
                link.enter(i - 1, 4)
                for h in range(2):
                    pool.wait_ge(s_sc[h], 16 * half * i)
                    stage_edges(SU * i + half * h, h)
                link.leave(SI - 1)
            for h in range(2):
                pool.wait_ge(s_sc[h], 16 * half * SI)
            link(pool.tensor_copy(sc_idx[:, 0:SREST], slot_row[:, SU * SI:EC]))
            link(pool.tensor_copy(sc_pay[:, 0:SREST, :], payload[:, SU * SI:EC, :]))
            for k in range(SREST):
                scatter(k, s_scat)
            pool.wait_ge(s_scat, 16 * SREST)
            pool.dma_start(loaded, slots_d.rearrange("(p c) w -> p c w", p=P)).then_inc(s_edges, 16)

            def gathers(order, table, width, free, ahead):
                with pool.Fori(0, CI) as i:
                    for j in range(U):
                        if j % HALF == 0:
                            pool.wait_ge(s_idx[j // HALF], 16 * (CI * order + i + 1))
                        pool.wait_ge(free, ahead + U * i + j + 1)
                        pool.sem_inc(s_issue, 1)
                        pool.indirect_dma_start(
                            out=g[:, j, 0:width], out_offset=None, in_=table,
                            in_offset=bass.IndirectOffsetOnAxis(ap=idx[:, j:j + 1], axis=0)).then_inc(s_g[j], 16)

            for b in range(2):
                pool.wait_ge(s_out0[b], 16 * (1 + out_uses[b]))
            gathers(0, rows_d, D, s_mm, 0)
            for b in range(2):
                pool.wait_ge(s_rel_out[b], 16 * (1 + out_uses[b]))
            gathers(1, rel_d[0], D, s_mm, NCH)
            for layer in range(1, L1):
                for q in range(4):
                    pool.wait_ge(s_quarter_out[q], 16 * (1 + NT * layer))
                gathers(1 + layer, rel_d[layer % 2], D, s_mm, NCH * (1 + layer))
            pool.wait_ge(s_table, 16)
            gathers(4, rows_d, D, s_mm, NCH * 4)
            pool.wait_ge(s_table, 32)
            gathers(5, src_logit_d, H, s_spread, 0)
            for b in range(2):
                pool.wait_ge(s_att_out[b], 16 * (1 + out_uses[b]))
            pool.wait_ge(s_spread, U + NCH)
            gathers(6, att_d, W3, s_mm3, 0)

        @block.scalar
        def _(act):
            def copy(o, v):
                return act.activation(o, v, ACT.Copy)

            act.sem_inc(s_ohts, U)
            act.sem_inc(s_ex, U)
            act.sem_inc(s_quarter, 2)
            for s in s_turned + [s_rel_act]:
                act.sem_inc(s, 1)
            for s in s_quarter_out:
                act.sem_inc(s, 16)

            for k in range(4):
                act.wait_ge(s_turn_w, k + 1)
                copy(wt[:, k].rearrange("p k (b o) -> p k b o", b=KD),
                     ps[:, k, :].rearrange("p (b k o) -> p k b o", b=KD, k=KD)).then_inc(s_wt, 1)

            def turn_tiles(ph, staged, extra=None, begin=0):
                def put(i, j):
                    act.wait_ge(s_turn[ph], 1 + TU * i + before(j))
                    staged(j % 2, TU * i + j).then_inc(s_stage[ph], 1)

                with act.Fori(0, TI) as i:
                    put(i, 0)
                    for j in range(TU):
                        if j + 1 < TU:
                            put(i, j + 1)
                        act.wait_ge(s_turn[ph], 1 + TU * i + j + 1)
                        act.wait_ge(s_prod[ph], 1 + TU * i + before(j))
                        copy(turned[:, j % 2, :], ps[:, 6 + j % 2, 0:D]).then_inc(s_turned[ph], 1)
                        if extra:
                            extra(i, j)

            roots = [0]

            def root(v):
                roots[0] += 1
                act.wait_ge(s_var, roots[0])
                act.activation(v, v, ACT.Sqrt).then_inc(s_root, 1)

            def squares(k):
                with act.Fori(0, TI) as i:
                    for j in range(TU):
                        act.wait_ge(s_sq_used, 1 + NT * k + TU * i + before(j))
                        act.activation(turned[:, j % 2, :], tile_at(Y3, TU * i + j), ACT.Square).then_inc(s_sq, 1)

            for b in range(2):
                act.wait_ge(s_out0[b], 16)
            turn_tiles(0, lambda b, t: copy(stage[:, b, :], tile_at(X, t)))
            act.wait_ge(s_dev, 1)
            squares(0)
            root(scale_b)
            act.wait_ge(s_h, 1)
            turn_tiles(1, lambda b, t: copy(stage[:, b, :], tile_at(Y3, t)))
            act.wait_ge(s_edges, 16)
            for w in range(4):
                act.copy(edges[:, w, :], loaded[:, :, w]).then_inc(s_planes, 1)
            act.wait_ge(s_add, U + NCH)
            turn_tiles(2, lambda b, t: act.activation(stage[:, b, :], tile_at(A, t), ACT.Gelu))
            act.wait_ge(s_dev, 2)
            squares(1)
            root(scale_b)
            root(mv[:, :, 1])

            act.wait_ge(s_x, 1)

            def rel_rows(i, j):
                for q in (1, 3):
                    act.wait_ge(s_rel_mm, 4 * (TU * i + j) + q + 1)
                    if q == 1:
                        act.wait_ge(s_rel_out[j % 2], 16 * (
                            1 + ((TU + 1) // 2 if j % 2 == 0 else TU // 2) * i + j // 2))
                    copy(rel_out[:, j % 2, 2 * q:2 * q + 2, :].rearrange("p r d -> p (r d)"), ps[:, q, :])\
                        .then_inc(s_rel_act, 1)

            turn_tiles(3, lambda b, t: copy(stage[:, b, :], tile_at(X, t)), rel_rows)
            act.wait_ge(s_prod[2], 1 + NT)
            for layer in range(1, L1):
                table = rel_d[layer % 2].rearrange("(r n) d -> n r d", r=R1)

                def rel_tile(t):
                    ph, first = 3 + layer, 4 * (NT * (layer - 1) + t)
                    bucket = bucket_by_size(mybir.EngineType.Activation, t)
                    act.wait_ge(s_turn[ph], 1 + t)
                    act.activation(stage[:, 0, :], tile_at(A, bucket), ACT.Relu).then_inc(s_stage[ph], 1)
                    act.wait_ge(s_turn[ph], 1 + t + 1)
                    act.wait_ge(s_prod[ph], 1 + t)
                    copy(turned[:, 0, :], ps[:, 7, 0:D]).then_inc(s_turned[ph], 1)
                    for q in range(4):
                        act.wait_ge(s_quarter_mm, first + q + 1)
                        act.wait_ge(s_quarter_out[q], 16 * (1 + NT * (layer - 1) + t))
                        copy(quarter[:, q, :], ps[:, 4 + q % 2, :]).then_inc(s_quarter, 1)
                        act.wait_ge(s_quarter, 2 + first + q + 1)
                        act.dma_start(table[bass.ds(bucket * P, P), 2 * q:2 * q + 2, :],
                                      quarter[:, q, :].rearrange("p (r d) -> p r d", r=2)).then_inc(s_quarter_out[q], 16)

                with act.Fori(READY, CI) as i:
                    act.wait_ge(s_add, U + NCH * layer + U * i)
                    rel_tile(i - READY)
                act.wait_ge(s_add, U + NCH * (layer + 1))
                for t in range(CI - READY, NT):
                    rel_tile(t)
            root(mv[:, :, 1])
            for k in range(2):
                for h in range(KD):
                    act.wait_ge(s_turn_w2, KD * k + h + 1)
                    copy(wt2[:, k, h, 0:512], ps[:, 2 * h, :])
                    copy(wt2[:, k, h, 512:G3], ps[:, 2 * h + 1, 0:G3 - 512]).then_inc(s_gru_w, 1)
            act.wait_ge(s_turn_w2, 2 * KD + 1)
            copy(relvec_t, ps[:, 4, 0:KD * R2].rearrange("p (k r) -> p k r", k=KD)).then_inc(s_gru_w, 1)
            act.wait_ge(s_turn_w2, 2 * KD + 2)
            copy(rel_gates[:, 0:512], ps[0:R2, 5, :])
            copy(rel_gates[:, 512:G3], ps[0:R2, 6, 0:G3 - 512]).then_inc(s_gru_w, 1)
            act.wait_ge(s_add, U + NCH * 5)

            def put2(i, j):
                act.wait_ge(s_turn[6], 1 + TU * i + before(j))
                copy(stage[:, j % 2, :], tile_at(A, TU * i + j))
                copy(cstage[:, j % 2, :], tile_at(counts, TU * i + j, R2))
                copy(stage2[:, j % 2, :], tile_at(X, TU * i + j)).then_inc(s_stage[6], 1)

            with act.Fori(0, TI) as i:
                put2(i, 0)
                for j in range(TU):
                    if j + 1 < TU:
                        put2(i, j + 1)
                    act.wait_ge(s_turn[6], 1 + TU * i + j + 1)
                    act.wait_ge(s_prod[6], 1 + TU * i + before(j))
                    copy(turned[:, j % 2, :], ps[:, 6 + j % 2, 0:D])
                    copy(turned2[:, j % 2, :], ps[:, 6 + j % 2, D:2 * D])
                    copy(cturned[:, j % 2, :], ps[0:R2, 4 + j % 2, 0:P]).then_inc(s_turned[6], 1)
                    act.wait_ge(s_rz, TU * i + j + 1)
                    act.activation(gates, gates, ACT.Sigmoid).then_inc(s_gates, 1)
                    act.wait_ge(s_cand, TU * i + j + 1)
                    act.activation(nn, inn, ACT.Tanh).then_inc(s_tanh, 1)
            root(mv[:, :, 1])

            act.wait_ge(s_x, 3)
            turn_tiles(7, lambda b, t: copy(stage[:, b, :], tile_at(X, t)))
            with act.Fori(0, CI) as i:
                for j in range(U):
                    act.wait_ge(s_g[j], 16 * (CI * 5 + i + 1))
                    act.wait_ge(s_spread, U + U * i + j - RING + 1)
                    for h in range(H - 1):
                        ins = act.activation(diag[:, j % RING, h, :], ident[:, :], ACT.Copy, scale=g[:, j, h:h + 1])
                    ins.then_inc(s_diag, 1)
            act.wait_ge(s_shift, 1)
            act.activation(ex_l, t_l, ACT.Exp).then_inc(s_self, 1)

            def second_pass(i, due, steps):
                for k in range(steps):
                    if due(k, 0):
                        c, s = U * i + k, k % RING
                        act.wait_ge(s_oht, c + 1)
                        act.wait_ge(s_dm, U + c - RING + 1)
                        copy(ohT[:, s, :], ps[:, 4 + k % 2, 0:P]).then_inc(s_ohts, 1)
                    if due(k, 6):
                        c, s, r = U * i + k - 6, (k - 6) % RING, (k - 6) % RING2
                        act.wait_ge(s_e, U + c + 1)
                        act.wait_ge(s_mm3, U + c - RING2 + 1)
                        act.activation(wrow[:, r, D:W3], lg[:, s, 3 * H:4 * H], ACT.Exp).then_inc(s_ex, 1)
                    if due(k, 7):
                        c, j, r = U * i + k - 7, (k - 7) % U, (k - 7) % RING2
                        act.wait_ge(s_ex, U + c + 1)
                        for h in range(HA):
                            ins = act.activation(wrow[:, r, h * F:(h + 1) * F], g[:, j, h * F:(h + 1) * F], ACT.Copy,
                                                 scale=wrow[:, r, D + h:D + h + 1])
                        ins.then_inc(s_wr_act, 1)

            trips(act, second_pass)
            root(mv[:, :, 1])
            root(mv[:, :, 1])

        @block.tensor
        def _(pe):
            pe.sem_inc(s_mm, U)
            pe.sem_inc(s_spread, U)
            pe.sem_inc(s_dm, U)
            pe.sem_inc(s_mm3, U)
            for s in s_turn + s_prod + [s_sq_used]:
                pe.sem_inc(s, 1)

            pe.wait_ge(s_ident, 1)
            pe.wait_ge(s_w0, 64)
            for w in range(4):
                for b in range(KD):
                    for k in range(KD):
                        at = (b * KD + k) * P
                        ins = pe.transpose(ps[:, w, at:at + P], nat0[:, w, b, k * P:(k + 1) * P], ident[:, :])
                ins.then_inc(s_turn_w, 1)

            def turn_tiles(ph, products):
                def turn(i, j):
                    pe.wait_ge(s_stage[ph], TU * i + j + 1)
                    pe.wait_ge(s_turned[ph], 1 + TU * i + before(j))
                    for k in range(KD):
                        ins = pe.transpose(ps[:, 6 + j % 2, k * P:(k + 1) * P], stage[:, j % 2, k * P:(k + 1) * P],
                                           ident[:, :])
                    ins.then_inc(s_turn[ph], 1)

                with pe.Fori(0, TI) as i:
                    turn(i, 0)
                    for j in range(TU):
                        if j + 1 < TU:
                            turn(i, j + 1)
                        pe.wait_ge(s_turned[ph], 1 + TU * i + j + 1)
                        products(i, j)

            def product(o, b, w):
                for k in range(KD):
                    ins = pe.matmul(o, turned[:, b, k * P:(k + 1) * P], w[:, k, :], start=(k == 0), stop=(k == KD - 1))
                return ins

            def one_product(ph, w):
                def products(i, j):
                    pe.wait_ge(s_evac[ph], 1 + TU * i + before(j))
                    product(ps[:, j % 2, 0:D], j % 2, wt[:, w]).then_inc(s_prod[ph], 1)
                turn_tiles(ph, products)

            def sum_nodes(k):
                pe.wait_ge(s_y, k + 1)
                pe.matmul(ps[:, 4, 0:D], ones[:, :], Y3[:, 0, :], start=True, stop=False, skip_group_check=True)
                with pe.Fori(0, (NT - 1) // 8) as i:
                    for j in range(8):
                        ins = pe.matmul(ps[:, 4, 0:D], ones[:, :], tile_at(Y3, 8 * i + j + 1), start=False,
                                        stop=(j == 7), skip_group_check=True)
                pe.drain().then_inc(s_sum, 1)
                pe.wait_ge(s_sq, NT * k + 1)
                pe.matmul(ps[:, 5, 0:D], ones[:, :], turned[:, 0, :], start=True, stop=False,
                          skip_group_check=True).then_inc(s_sq_used, 1)
                for j in range(1, TU):
                    pe.wait_ge(s_sq, NT * k + j + 1)
                    pe.matmul(ps[:, 5, 0:D], ones[:, :], turned[:, j % 2, :], start=False, stop=(j == TU - 1),
                              skip_group_check=True).then_inc(s_sq_used, 1)
                with pe.Fori(1, TI) as i:
                    for j in range(TU):
                        pe.wait_ge(s_sq, NT * k + TU * i + j + 1)
                        pe.matmul(ps[:, 5, 0:D], ones[:, :], turned[:, j % 2, :], start=False, stop=(j == TU - 1),
                                  skip_group_check=True).then_inc(s_sq_used, 1)
                pe.drain().then_inc(s_sum, 1)

            def sum_chunk(order, width, i, j):
                c = NCH * order + U * i + j
                pe.wait_ge(s_oh, c + 1)
                pe.wait_ge(s_g[j], 16 * (CI * order + i + 1))
                pe.wait_ge(s_add, U + c - BANKS + 1)
                pe.matmul(ps[:, j % BANKS, 0:width], oh[:, j % OHS, :], g[:, j, 0:width],
                          start=True, stop=True).then_inc(s_mm, 1)

            def sums(order, width):
                with pe.Fori(0, CI) as i:
                    for j in range(U):
                        sum_chunk(order, width, i, j)

            pe.wait_ge(s_cnt, 1)
            pe.matmul(ps[:, 5, 0:NB], upper, cnt_b, start=True, stop=True)
            pe.matmul(ps[:, 5, 64:64 + NB], ones[:, :], cnt_b, start=True, stop=True).then_inc(s_tot, 1)

            pe.wait_ge(s_wt, 4)
            one_product(0, 0)
            sum_nodes(0)

            def two_products(i, j):
                pe.wait_ge(s_evac[1], 1 + TU * i + before(j))
                product(ps[:, j % 2, 0:D], j % 2, wt[:, 1])
                product(ps[:, 2 + j % 2, 0:D], j % 2, wt[:, 2]).then_inc(s_prod[1], 1)

            turn_tiles(1, two_products)
            pe.wait_ge(s_evac[1], 1 + NT)
            sums(0, D)
            pe.wait_ge(s_add, U + NCH)
            one_product(2, 3)
            sum_nodes(1)

            pe.wait_ge(s_rel_out[0], 16)
            relations = [v.rearrange("p k r d -> p k (r d)") for v in wrel]

            def rel_products(i, j):
                for q in range(4):
                    if q % 2:
                        pe.wait_ge(s_rel_act, 1 + 2 * (TU * i + j))
                    else:
                        pe.wait_ge(s_rel_dve, 1 + 2 * (TU * i + j))
                    for k in range(KD):
                        ins = pe.matmul(ps[:, q, :], turned[:, j % 2, k * P:(k + 1) * P],
                                        relations[0][:, k, q * 512:(q + 1) * 512], start=(k == 0), stop=(k == KD - 1))
                    ins.then_inc(s_rel_mm, 1)
                pe.wait_ge(s_evac[3], 1 + TU * i + j)
                product(ps[:, 4, 0:D], j % 2, wroot1[:, 0]).then_inc(s_prod[3], 1)

            pe.wait_ge(s_wrel[0], 32)
            turn_tiles(3, rel_products)
            pe.wait_ge(s_rel_act, 1 + 2 * NT)
            pe.wait_ge(s_rel_dve, 1 + 2 * NT)
            pe.wait_ge(s_evac[3], 1 + NT)
            for layer in range(1, L1):
                w, ph = relations[layer % 2], 3 + layer

                def rel_turn(t):
                    pe.wait_ge(s_stage[ph], t + 1)
                    pe.wait_ge(s_turned[ph], 1 + t)
                    for k in range(KD):
                        ins = pe.transpose(ps[:, 7, k * P:(k + 1) * P], stage[:, 0, k * P:(k + 1) * P], ident[:, :])
                    ins.then_inc(s_turn[ph], 1)

                def rel_quarter(t, q):
                    if q == 0:
                        pe.wait_ge(s_turned[ph], 1 + t + 1)
                    pe.wait_ge(s_quarter, 4 * (NT * (layer - 1) + t) + q + 1)
                    for k in range(KD):
                        ins = pe.matmul(ps[:, 4 + q % 2, :], turned[:, 0, k * P:(k + 1) * P],
                                        w[:, k, q * 512:(q + 1) * 512], start=(k == 0), stop=(k == KD - 1))
                    ins.then_inc(s_quarter_mm, 1)

                def rel_root(t):
                    pe.wait_ge(s_evac[ph], 1 + t)
                    product(ps[:, 6, 0:D], 0, wroot1[:, layer]).then_inc(s_prod[ph], 1)

                def trip(i, t):
                    for j in range(U):
                        sum_chunk(layer, D, i, j)
                        if t is not None:
                            if j == 2:
                                rel_turn(t)
                            if j in (5, 8, 11, 13):
                                rel_quarter(t, (5, 8, 11, 13).index(j))
                            if j == U - 1:
                                rel_root(t)

                def dense(t):
                    rel_turn(t)
                    for q in range(4):
                        rel_quarter(t, q)
                    rel_root(t)

                pe.wait_ge(s_wrel[layer], 32)
                beside_sweep(pe, trip, dense)
                pe.wait_ge(s_evac[ph], 1 + NT)
            sums(L1, D)
            pe.wait_ge(s_add, U + NCH * (1 + L1))

            pe.wait_ge(s_w2, 80)
            for w in range(2):
                for k in range(KD):
                    if w:
                        pe.wait_ge(s_gru_w, k + 1)
                    for b in range(nb2):
                        ins = pe.transpose(ps[:, 2 * k + b // 4, b % 4 * P:(b % 4 + 1) * P],
                                           nat2[:, w, b, k * P:(k + 1) * P], ident[:, :])
                    ins.then_inc(s_turn_w2, 1)
            for k in range(KD):
                ins = pe.transpose(ps[:, 4, k * R2:(k + 1) * R2], relvec[:, k * P:(k + 1) * P], ident[0:R2, 0:R2])
            ins.then_inc(s_turn_w2, 1)
            pe.wait_ge(s_gru_w, 2 * KD + 1)
            for o, lo, hi in ((ps[0:R2, 5, :], 0, 512), (ps[0:R2, 6, 0:G3 - 512], 512, G3)):
                for k in range(KD):
                    ins = pe.matmul(o, relvec_t[:, k, :], wt2[:, 0, k, lo:hi], start=(k == 0), stop=(k == KD - 1))
            ins.then_inc(s_turn_w2, 1)
            pe.wait_ge(s_gru_w, 2 * KD + 2)
            sums(4, D + R2)
            pe.wait_ge(s_add, U + NCH * 5)

            def turn2(i, j):
                pe.wait_ge(s_stage[6], TU * i + j + 1)
                pe.wait_ge(s_turned[6], 1 + TU * i + before(j))
                for v, at in ((stage, 0), (stage2, D)):
                    for k in range(KD):
                        pe.transpose(ps[:, 6 + j % 2, at + k * P:at + (k + 1) * P], v[:, j % 2, k * P:(k + 1) * P],
                                     ident[:, :])
                pe.transpose(ps[0:R2, 4 + j % 2, 0:P], cstage[:, j % 2, :], ident[:, :]).then_inc(s_turn[6], 1)

            with pe.Fori(0, TI) as i:
                turn2(i, 0)
                for j in range(TU):
                    if j + 1 < TU:
                        turn2(i, j + 1)
                    b = j % 2
                    pe.wait_ge(s_turned[6], 1 + TU * i + j + 1)
                    pe.wait_ge(s_evac[6], 1 + TU * i + before(j))
                    rz, inp, hid = ps[:, b, :], ps[:, 2 + b, 0:D], ps[:, 2 + b, D:2 * D]
                    for k in range(KD):
                        x_k, h_k = turned[:, b, k * P:(k + 1) * P], turned2[:, b, k * P:(k + 1) * P]
                        pe.matmul(rz, x_k, wt2[:, 0, k, 0:512], start=(k == 0), stop=False)
                        pe.matmul(rz, h_k, wt2[:, 1, k, 0:512], start=False, stop=False)
                    pe.matmul(rz, cturned[:, b, :], rel_gates[:, 0:512], start=False, stop=True)
                    for k in range(KD):
                        pe.matmul(inp, turned[:, b, k * P:(k + 1) * P], wt2[:, 0, k, 512:G3], start=(k == 0), stop=False)
                    pe.matmul(inp, cturned[:, b, :], rel_gates[:, 512:G3], start=False, stop=True)
                    for k in range(KD):
                        ins = pe.matmul(hid, turned2[:, b, k * P:(k + 1) * P], wt2[:, 1, k, 512:G3],
                                        start=(k == 0), stop=(k == KD - 1))
                    ins.then_inc(s_prod[6], 1)

            pe.wait_ge(s_att_out[0], 16)
            pe.wait_ge(s_gru, NT)

            def att_products(i, j):
                pe.wait_ge(s_evac[7], 1 + TU * i + before(j))
                product(ps[:, j % 2, 0:D], j % 2, w3).then_inc(s_prod[7], 1)

            turn_tiles(7, att_products)
            pe.wait_ge(s_evac[7], 1 + NT)
            with pe.Fori(0, CI) as i:
                for j in range(U):
                    c = U * i + j
                    pe.wait_ge(s_diag, c + 1)
                    pe.wait_ge(s_diag_dve, c + 1)
                    pe.wait_ge(s_miss, c + 1)
                    pe.wait_ge(s_red, U + c - 8 + 1)
                    o = ps[:, j % 8, :]
                    pe.matmul(o, ones[:, :], diag[:, j % RING].rearrange("p h e -> p (h e)"), start=True, stop=False)
                    pe.matmul(o, miss[:, j % RING2, :], big_ident[:, :, :].rearrange("p h e -> p (h e)"),
                              start=False, stop=True).then_inc(s_spread, 1)
            pe.wait_ge(s_self, 1)
            pe.wait_ge(s_acc0, 1)

            def second_pass(i, due, steps):
                buckets = lagged_buckets(mybir.EngineType.PE, i, 2)
                for k in range(steps):
                    if due(k, 9):
                        c, j, r = U * i + k - 9, (k - 9) % U, (k - 9) % RING2
                        pe.wait_ge(s_wr, c + 1)
                        pe.wait_ge(s_wr_act, c + 1)
                        pe.wait_ge(s_add3, U + c - BANKS + 1)
                        pe.matmul(ps[:, j % BANKS, 0:W3], ohb[:, j, :], wrow[:, r, :], start=True, stop=True)\
                            .then_inc(s_mm3, 1)
                    if due(k, 0):
                        c = U * i + k
                        pe.wait_ge(s_ohb, c + 1)
                        pe.wait_ge(s_ohts, U + c - 2 + 1)
                        pe.transpose(ps[:, 4 + k % 2, 0:P], ohb[:, k, :], ident[:, :]).then_inc(s_oht, 1)
                    if due(k, 2):
                        c, s = U * i + k - 2, (k - 2) % RING
                        pe.wait_ge(s_ohts, U + c + 1)
                        pe.wait_ge(s_l0, U + c - 2 + 1)
                        pe.matmul(ps[:, 6 + k % 2, 0:2 * H], ohT[:, s, :], tile_at(dst_max, buckets[k], 2 * H),
                                  start=True, stop=True).then_inc(s_dm, 1)

            trips(pe, second_pass)

        @block.vector
        def _(dve):
            link = Link(dve, s_dve)
            dve.sem_inc(s_add, U)
            dve.sem_inc(s_red, U)
            dve.sem_inc(s_e, U)
            dve.sem_inc(s_l0, U)
            dve.sem_inc(s_add3, U)
            dve.sem_inc(s_maxed, U)
            for s in s_evac + [s_rel_dve]:
                dve.sem_inc(s, 1)

            dve.wait_ge(s_const, 5)
            dve.tensor_scalar(upper, col[:, :], prow, None, ALU.is_gt)
            dve.tensor_scalar(pmask, prow, float(LAST), None, ALU.is_lt)
            link(dve.tensor_scalar(ident[:, :], col[:, :], prow, None, ALU.is_equal))
            for h in range(H):
                ins = dve.tensor_scalar(big_ident[:, h, :], ident[:, :], BIG, None, ALU.mult)
            ins.then_inc(s_ident, 1)

            dst_i, src_i, rel_i, typ_i, int_w = (tmp(k, I32) for k in range(5))
            bucket, node, work, rank, pos = (tmp(k) for k in range(5, 10))
            dve.wait_ge(s_edge_in, 16 * 8)
            link(dve.tensor_scalar(int_w, dst_i, 7, None, ALU.logical_shift_right))
            link(dve.tensor_copy(bucket, int_w))
            link(dve.tensor_copy(node, dst_i))
            link(dve.scalar_tensor_tensor(node, bucket, -float(P), node, ALU.mult, ALU.add))
            link(dve.tensor_scalar(work, bucket, float(NT), float(P), ALU.is_equal, ALU.mult))
            link(dve.tensor_tensor(payload_f[:, :, 2], node, work, ALU.add))
            link(dve.tensor_copy(payload[:, :, 0], src_i))
            link(dve.tensor_copy(payload_f[:, :, 3], typ_i))
            link(dve.tensor_copy(node, rel_i))
            link(dve.tensor_copy(work, src_i))
            link(dve.scalar_tensor_tensor(payload[:, :, 1], node, float(NP), work, ALU.mult, ALU.add))
            link(dve.memset(pos, 0.0))
            with dve.Fori(0, NB) as b:
                link.enter(b, 5)
                link(dve.tensor_scalar(work, bucket, iota_b[:, bass.ds(b, 1)], None, ALU.is_equal))
                link(dve.tensor_tensor_scan(rank, work, work, 0.0, ALU.add, ALU.max))
                link(dve.tensor_scalar(cnt_b[:, bass.ds(b, 1)], rank[:, EC - 1:EC], 1.0, None, ALU.mult))
                link(dve.tensor_tensor(rank, rank, work, ALU.mult))
                link(dve.tensor_tensor(pos, pos, rank, ALU.add))
                link.leave(NB)
            dve.sem_inc(s_cnt, 1)
            dve.wait_ge(s_tot, 1)
            before_p, total_p = ps[:, 5, 0:NB], ps[:, 5, 64:64 + NB]

            def by_bucket(v):
                return v.rearrange("p (b o) -> p b o", o=1).broadcast_to([P, NB, NB])

            def by_other(v):
                return v.rearrange("p (o b) -> p o b", o=1).broadcast_to([P, NB, NB])

            int_b, chunks_i = before_b.bitcast(I32), tot_b.bitcast(I32)
            link(dve.tensor_scalar(int_b, total_p, float(P - 1), None, ALU.add))
            link(dve.tensor_scalar(chunks_i, int_b, 7, None, ALU.logical_shift_right))
            link(dve.tensor_copy(nch_b, chunks_i))
            link(dve.scalar_tensor_tensor(key_b, nch_b, 64.0, iota_b, ALU.mult, ALU.add))
            link(dve.memset(key_b[:, NT:NB], 64.0 * (NCH + 1)))
            link(dve.tensor_tensor(pairs, by_other(key_b), by_bucket(key_b), ALU.is_lt))
            link(dve.tensor_reduce(rank_b, pairs, AX, ALU.add))
            link(dve.tensor_tensor(pairs, pairs, by_other(nch_b), ALU.mult))
            link(dve.tensor_reduce(first_b, pairs, AX, ALU.add))
            link(dve.tensor_tensor(end_b, first_b, nch_b, ALU.add))
            link(dve.tensor_scalar(base_b, first_b, float(P), -1.0, ALU.mult, ALU.add))
            link(dve.tensor_tensor(base_b, base_b, before_p, ALU.add))
            with dve.Fori(0, NB) as b:
                link.enter(b, 2)
                link(dve.tensor_scalar(work, bucket, iota_b[:, bass.ds(b, 1)], base_b[:, bass.ds(b, 1)],
                                       ALU.is_equal, ALU.mult))
                link(dve.tensor_tensor(pos, pos, work, ALU.add))
                link.leave(NB)
            link(dve.tensor_copy(int_w, pos))
            link(dve.tensor_scalar(dst_i, int_w, P - 1, None, ALU.bitwise_and))
            link(dve.tensor_scalar(src_i, int_w, 7, None, ALU.logical_shift_right))
            link(dve.tensor_copy(node, dst_i))
            link(dve.tensor_copy(work, src_i))
            dve.scalar_tensor_tensor(slot_row, node, float(NCH), work, ALU.mult, ALU.add).then_inc(s_slot, 1)
            link(dve.tensor_tensor(pairs, by_other(rank_b), by_bucket(iota_b), ALU.is_equal))
            link(dve.tensor_tensor(pairs, pairs, by_other(iota_b), ALU.mult))
            link(dve.tensor_reduce(order_f, pairs, AX, ALU.add))
            link(dve.tensor_copy(order_of[0:1, :], order_f[0:1, 0:NT]))
            bf, cn = bucket_f[0:1, :], chunk_no[0:1, :]
            link(dve.tensor_scalar(bf, cn, first_b[0:1, NT:NB], order_f[0:1, NT - 1:NT], ALU.is_ge, ALU.mult))
            with dve.Fori(1, NT) as b:
                link.enter(b - 1, 3)
                dve.tensor_scalar(from_first, cn, first_b[0:1, bass.ds(b, 1)], iota_b[0:1, bass.ds(b, 1)],
                                  ALU.is_ge, ALU.mult)
                link(dve.tensor_scalar(from_end, cn, end_b[0:1, bass.ds(b, 1)], iota_b[0:1, bass.ds(b, 1)],
                                       ALU.is_ge, ALU.mult))
                link(dve.tensor_tensor(bf, bf, from_first, ALU.add))
                link(dve.tensor_tensor(bf, bf, from_end, ALU.subtract))
                link.leave(NT - 1)
            link(dve.tensor_copy(bucket_of[0:1, :], bf))

            def evacuate(ph, take):
                with dve.Fori(0, TI) as i:
                    for j in range(TU):
                        dve.wait_ge(s_prod[ph], 1 + TU * i + j + 1)
                        take(i, j).then_inc(s_evac[ph], 1)
                dve.wait_ge(s_evac[ph], 1 + NT)

            roots = [0]

            def root(v):
                roots[0] += 1
                dve.sem_inc(s_var, 1)
                dve.wait_ge(s_root, roots[0])
                link(dve.reciprocal(v, v))

            def batch_norm(k, gamma, beta):
                link(dve.tensor_scalar(Y3[:, NT - 1, :], Y3[:, NT - 1, :], pmask, None, ALU.mult))
                dve.sem_inc(s_y, 1)
                dve.wait_ge(s_sum, 2 * k + 1)
                link(dve.tensor_scalar(mean_b, ps[:, 4, 0:D], 1.0 / N, None, ALU.mult))
                link(dve.tensor_tensor(Y3, Y3, over_tiles(mean_b), ALU.subtract))
                link(dve.tensor_scalar(Y3[:, NT - 1, :], Y3[:, NT - 1, :], pmask, None, ALU.mult))
                dve.sem_inc(s_dev, 1)
                dve.wait_ge(s_sum, 2 * k + 2)
                link(dve.tensor_scalar(scale_b, ps[:, 5, 0:D], 1.0 / N, EPS, ALU.mult, ALU.add))
                root(scale_b)
                link(dve.tensor_tensor(scale_b, scale_b, gamma, ALU.mult))
                link(dve.tensor_tensor(Y3, Y3, over_tiles(scale_b), ALU.mult))
                link(dve.tensor_tensor(Y3, Y3, over_tiles(beta), ALU.add))

            def layer_norm(v):
                with dve.Fori(0, TI) as i:
                    link.enter(i, 1)
                    for j in range(TU):
                        ins = dve.bn_stats(tile_at(stats, TU * i + j, 6), tile_at(v, TU * i + j))
                    link(ins)
                    link.leave(TI)
                mean_e, sq_e, mean_o, sq_o = (stats[:, :, n] for n in (1, 2, 4, 5))
                mean, var = mv[:, :, 0], mv[:, :, 1]
                link(dve.tensor_tensor(mean, mean_e, mean_o, ALU.add))
                link(dve.tensor_tensor(mean_e, mean_e, mean_o, ALU.subtract))
                link(dve.tensor_scalar(mean, mean, 0.5, None, ALU.mult))
                link(dve.tensor_tensor(var, sq_e, sq_o, ALU.add))
                link(dve.tensor_tensor(mean_e, mean_e, mean_e, ALU.mult))
                link(dve.scalar_tensor_tensor(var, mean_e, D / 4.0, var, ALU.mult, ALU.add))
                link(dve.tensor_scalar(var, var, 1.0 / D, EPS, ALU.mult, ALU.add))
                root(mv[:, :, 1])
                with dve.Fori(0, TI) as i:
                    link.enter(i, 1)
                    for j in range(TU):
                        t = TU * i + j
                        ins = dve.tensor_scalar(tile_at(v, t), tile_at(v, t), mv[:, bass.ds(t, 1), 0],
                                                mv[:, bass.ds(t, 1), 1], ALU.subtract, ALU.mult)
                    link(ins)
                    link.leave(TI)

            def sums_trip(order, i, with_types=False):
                def one_hot(j):
                    c = NCH * order + U * i + j
                    dve.wait_ge(s_mm, U + c - OHS + 1)
                    if with_types:
                        dve.tensor_scalar(g[:, j, D:D + R2], col[:, 0:R2], edges_f[:, 3, bass.ds(U * i + j, 1)],
                                          None, ALU.is_equal)
                    dve.tensor_scalar(oh[:, j % OHS, :], col[:, :], edges_f[:, 2, bass.ds(U * i + j, 1)],
                                      None, ALU.is_equal).then_inc(s_oh, 1)

                buckets = buckets_of(mybir.EngineType.DVE, i)
                one_hot(0)
                one_hot(1)
                for j in range(U):
                    if j + 2 < U:
                        one_hot(j + 2)
                    c = NCH * order + U * i + j
                    t = buckets[j]
                    dve.wait_ge(s_mm, U + c + 1)
                    dve.wait_ge(s_add, U + c)
                    if with_types:
                        dve.tensor_tensor(tile_at(counts, t, R2), tile_at(counts, t, R2),
                                          ps[:, j % BANKS, D:D + R2], ALU.add)
                    dve.tensor_tensor(tile_at(A, t), tile_at(A, t), ps[:, j % BANKS, 0:D], ALU.add)\
                        .then_inc(s_add, 1)

            def sums(order, with_types=False):
                with dve.Fori(0, CI) as i:
                    sums_trip(order, i, with_types)
                dve.wait_ge(s_add, U + NCH * (order + 1))

            dve.wait_ge(s_rows0, 16 * 7)
            evacuate(0, lambda i, j: dve.tensor_tensor(tile_at(Y3, TU * i + j), ps[:, j % 2, 0:D], B1, ALU.add))
            batch_norm(0, G1, BETA1)
            dve.sem_inc(s_h, 1)

            def take1(i, j):
                dve.tensor_tensor(tile_at(A, TU * i + j), ps[:, 2 + j % 2, 0:D], BR, ALU.add)
                dve.wait_ge(s_out0[j % 2], 16 * (1 + ((TU + 1) // 2 if j % 2 == 0 else TU // 2) * i + j // 2))
                return dve.tensor_copy(out0[:, j % 2, :], ps[:, j % 2, 0:D])

            evacuate(1, take1)
            for b in range(2):
                dve.wait_ge(s_out0[b], 16 * (1 + out_uses[b]))
            dve.wait_ge(s_planes, 4)
            sums(0)
            evacuate(2, lambda i, j: dve.tensor_tensor(tile_at(Y3, TU * i + j), ps[:, j % 2, 0:D], B2, ALU.add))
            batch_norm(1, G2, BETA2)
            link(dve.scalar_tensor_tensor(X[:, :, :], X[:, :, :], 2.0, Y3, ALU.mult, ALU.add))
            layer_norm(X)
            dve.sem_inc(s_x, 1)

            dve.wait_ge(s_rel_out[1], 16)
            def take_rel(i, j):
                for q in (0, 2):
                    dve.wait_ge(s_rel_mm, 4 * (TU * i + j) + q + 1)
                    if q == 0:
                        dve.wait_ge(s_rel_out[j % 2], 16 * (
                            1 + ((TU + 1) // 2 if j % 2 == 0 else TU // 2) * i + j // 2))
                    dve.tensor_copy(rel_out[:, j % 2, 2 * q:2 * q + 2, :].rearrange("p r d -> p (r d)"),
                                    ps[:, q, :]).then_inc(s_rel_dve, 1)
                dve.wait_ge(s_prod[3], 1 + TU * i + j + 1)
                return dve.tensor_tensor(tile_at(A, TU * i + j), ps[:, 4, 0:D], bias1[:, 0, :], ALU.add)

            with dve.Fori(0, TI) as i:
                for j in range(TU):
                    take_rel(i, j).then_inc(s_evac[3], 1)
            dve.wait_ge(s_evac[3], 1 + NT)
            for layer in range(1, L1):
                def take_root(t):
                    bucket = bucket_by_size(mybir.EngineType.DVE, t)
                    dve.wait_ge(s_prod[3 + layer], 1 + t + 1)
                    dve.tensor_tensor(tile_at(A, bucket), ps[:, 6, 0:D], bias1[:, layer, :], ALU.add)\
                        .then_inc(s_evac[3 + layer], 1)

                def trip(i, t):
                    sums_trip(layer, i)
                    if t is not None:
                        take_root(t)

                beside_sweep(dve, trip, take_root)
                dve.wait_ge(s_evac[3 + layer], 1 + NT)
            sums(L1)
            link(dve.scalar_tensor_tensor(X[:, :, :], A2, 0.0, X[:, :, :], ALU.max, ALU.add))
            layer_norm(X)
            link(dve.memset(A2, 0.0))
            link(dve.memset(counts, 0.0))
            dve.sem_inc(s_x, 1)
            sums(4, True)
            dve.wait_ge(s_w2, 80)
            link(dve.tensor_tensor(b_ih[:, 0:512], b_ih[:, 0:512], b_hh[:, 0:512], ALU.add))
            with dve.Fori(0, TI) as i:
                link.enter(i, 4 * TU)
                for j in range(TU):
                    t, b = TU * i + j, j % 2
                    dve.wait_ge(s_prod[6], 1 + t + 1)
                    dve.tensor_tensor(gates, ps[:, b, :], b_ih[:, 0:512], ALU.add).then_inc(s_rz, 1)
                    dve.tensor_tensor(hn, ps[:, 2 + b, D:2 * D], b_hh[:, 512:G3], ALU.add)
                    dve.tensor_tensor(inn, ps[:, 2 + b, 0:D], b_ih[:, 512:G3], ALU.add).then_inc(s_evac[6], 1)
                    dve.wait_ge(s_evac[6], 1 + t + 1)
                    dve.wait_ge(s_gates, t + 1)
                    link(dve.tensor_tensor(hn, hn, gates[:, 0:D], ALU.mult))
                    dve.tensor_tensor(inn, inn, hn, ALU.add).then_inc(s_cand, 1)
                    dve.wait_ge(s_tanh, t + 1)
                    link(dve.tensor_tensor(hn, tile_at(X, t), nn, ALU.subtract))
                    link(dve.tensor_tensor(hn, hn, gates[:, D:2 * D], ALU.mult))
                    link(dve.tensor_tensor(hn, hn, nn, ALU.add))
                    dve.tensor_tensor(tile_at(X, t), tile_at(X, t), hn, ALU.add).then_inc(s_gru, 1)
                    dve.wait_ge(s_gru, t + 1)
                link.leave(TI)
            layer_norm(X)
            dve.sem_inc(s_x, 1)

            dve.wait_ge(s_w3, 64)
            dve.wait_ge(s_att_out[1], 16)
            with dve.Fori(0, TI) as i:
                link.enter(i, 5 * TU)
                for j in range(TU):
                    t, b = TU * i + j, j % 2
                    dve.wait_ge(s_prod[7], 1 + t + 1)
                    dve.wait_ge(s_att_out[b], 16 * (1 + ((TU + 1) // 2 if b == 0 else TU // 2) * i + j // 2))
                    dve.tensor_scalar(tile_at(A, t), ps[:, b, 0:D], 1.0, None, ALU.mult)
                    dve.tensor_copy(att_row[:, b, 0:D], ps[:, b, 0:D])
                    for v, o in ((att_t, dst_max), (att_s, src_l)):
                        link(dve.tensor_tensor(att_tmp, ps[:, b, 0:D], v, ALU.mult))
                        link(dve.tensor_reduce(tile_at(o, t, H), att_tmp.rearrange("p (h f) -> p h f", h=H),
                                               AX, ALU.add))
                    link(dve.tensor_scalar(att_row[:, b, D:W3], tile_at(src_l, t, H), 1.0, None, ALU.mult))
                    dve.sem_inc(s_att_row, 1)
                    dve.sem_inc(s_evac[7], 1)
                link.leave(TI)
            dve.sem_inc(s_logit, 1)
            link(dve.tensor_copy(max_l, src_l))
            def first_pass(i, due, steps):
                buckets = lagged_buckets(mybir.EngineType.DVE, i, 5)
                for k in range(steps):
                    if due(k, 0):
                        c = U * i + k
                        dve.wait_ge(s_spread, U + c - RING2 + 1)
                        dve.tensor_scalar(miss[:, k % RING2, :], col[:, :], edges_f[:, 2, bass.ds(c, 1)], -1.0,
                                          ALU.is_equal, ALU.add).then_inc(s_miss, 1)
                    if due(k, 1):
                        c, j = U * i + k - 1, (k - 1) % U
                        dve.wait_ge(s_g[j], 16 * (CI * 5 + (i if k >= 1 else i - 1) + 1))
                        dve.wait_ge(s_spread, U + c - RING + 1)
                        dve.tensor_scalar(diag[:, j % RING, H - 1, :], ident[:, :], g[:, j, H - 1:H], None, ALU.mult)\
                            .then_inc(s_diag_dve, 1)
                    if due(k, 4):
                        c, j = U * i + k - 4, (k - 4) % U
                        dve.wait_ge(s_spread, U + c + 1)
                        dve.wait_ge(s_maxed, U + c - RING + 1)
                        dve.tensor_reduce(red[:, j % RING, :], ps[:, j % 8, :].rearrange("p (h e) -> p h e", h=H),
                                          AX, ALU.max).then_inc(s_red, 1)
                    if due(k, 5):
                        c, j = U * i + k - 5, (k - 5) % U
                        t = buckets[k]
                        dve.wait_ge(s_red, U + c + 1)
                        dve.wait_ge(s_maxed, U + c)
                        dve.tensor_tensor(tile_at(max_l, t, H), tile_at(max_l, t, H), red[:, j % RING, :], ALU.max)\
                            .then_inc(s_maxed, 1)

            trips(dve, first_pass)
            dve.wait_ge(s_maxed, U + NCH)

            dst_l, m_l = dst_max[:, :, 0:H], dst_max[:, :, H:2 * H]
            link(dve.tensor_tensor(max_l, max_l, dst_l, ALU.add))
            link(dve.scalar_tensor_tensor(m_l, max_l, 0.2, max_l, ALU.mult, ALU.max))
            link(dve.tensor_tensor(t_l, src_l, dst_l, ALU.add))
            link(dve.scalar_tensor_tensor(t_l, t_l, 0.2, t_l, ALU.mult, ALU.max))
            link(dve.tensor_tensor(t_l, t_l, m_l, ALU.subtract))
            dve.sem_inc(s_shift, 1)
            dve.wait_ge(s_self, 1)
            link(dve.tensor_copy(A[:, :, D:W3], ex_l))
            a4 = A2.rearrange("p t (h f) -> p t h f", h=H)
            link(dve.memset(g[:, :, W3:W3 + H], 0.0))

            def by_head(v):
                return v.rearrange("p t (h o) -> p t h o", o=1).broadcast_to([P, NT, H, F])

            link(dve.tensor_tensor(a4, a4, by_head(ex_l), ALU.mult))
            dve.sem_inc(s_acc0, 1)
            def second_pass(i, due, steps):
                buckets = lagged_buckets(mybir.EngineType.DVE, i, 10)
                for k in range(steps):
                    if due(k, 0):
                        c = U * i + k
                        dve.wait_ge(s_mm3, U + c - U + 1)
                        dve.tensor_scalar(ohb[:, k, :], col[:, :], edges_f[:, 2, bass.ds(c, 1)], None,
                                          ALU.is_equal).then_inc(s_ohb, 1)
                    if due(k, 3):
                        c, j, s = U * i + k - 3, (k - 3) % U, (k - 3) % RING
                        dve.wait_ge(s_g[j], 16 * (CI * 6 + (i if k >= 3 else i - 1) + 1))
                        dve.wait_ge(s_dm, U + c + 1)
                        dve.tensor_tensor(lg[:, s, 0:2 * H], ps[:, 6 + s % 2, 0:2 * H], g[:, j, D:D + 2 * H], ALU.add)\
                            .then_inc(s_l0, 1)
                    if due(k, 4):
                        c, s = U * i + k - 4, (k - 4) % RING
                        dve.wait_ge(s_l0, U + c + 1)
                        dve.scalar_tensor_tensor(lg[:, s, 2 * H:3 * H], lg[:, s, 0:H], 0.2, lg[:, s, 0:H],
                                                 ALU.mult, ALU.max).then_inc(s_l1, 1)
                    if due(k, 5):
                        c, s = U * i + k - 5, (k - 5) % RING
                        dve.wait_ge(s_l1, c + 1)
                        dve.wait_ge(s_ex, U + c - RING + 1)
                        dve.tensor_tensor(lg[:, s, 3 * H:4 * H], lg[:, s, 2 * H:3 * H], lg[:, s, H:2 * H],
                                          ALU.subtract).then_inc(s_e, 1)
                    if due(k, 8):
                        c, j, r = U * i + k - 8, (k - 8) % U, (k - 8) % RING2
                        dve.wait_ge(s_ex, U + c + 1)
                        ex = wrow[:, r, D + HA:W3].rearrange("p (h o) -> p h o", o=1).broadcast_to([P, H - HA, F])
                        dve.tensor_tensor(wrow[:, r, HA * F:D].rearrange("p (h f) -> p h f", f=F),
                                          g[:, j, HA * F:D].rearrange("p (h f) -> p h f", f=F), ex, ALU.mult)\
                            .then_inc(s_wr, 1)
                    if due(k, 10):
                        c, j, t = U * i + k - 10, (k - 10) % U, buckets[k]
                        dve.wait_ge(s_mm3, U + c + 1)
                        dve.wait_ge(s_add3, U + c)
                        dve.tensor_tensor(tile_at(A, t, W3), tile_at(A, t, W3), ps[:, j % BANKS, 0:W3], ALU.add)\
                            .then_inc(s_add3, 1)

            trips(dve, second_pass)
            dve.wait_ge(s_add3, U + NCH)
            link(dve.tensor_scalar(A[:, :, D:W3], A[:, :, D:W3], 1e-16, None, ALU.add))
            link(dve.reciprocal(ex_l, A[:, :, D:W3]))
            link(dve.tensor_tensor(a4, a4, by_head(ex_l), ALU.mult))
            link(dve.tensor_tensor(A2, A2, over_tiles(bias3), ALU.add))
            link(dve.tensor_tensor(A2, A2, X[:, :, :], ALU.add))
            layer_norm(A2)
            link(dve.tensor_tensor(A2, A2, over_tiles(gamma3), ALU.mult))
            link(dve.tensor_tensor(A2, A2, over_tiles(beta3), ALU.add))
            link(dve.scalar_tensor_tensor(X[:, :, :], A2, 0.0, X[:, :, :], ALU.max, ALU.add))
            layer_norm(X)
            dve.sem_inc(s_x, 1)


_INS = ["x", "src", "dst", "edge_type_16", "edge_type_8"] + [f"L0_gnn_{n}" for n in (
    "w1", "b1", "g1", "beta1", "wr", "br", "wroot", "w2", "b2", "g2", "beta2")] + [
    "L1_gnn_W_rel", "L1_gnn_W_root", "L1_gnn_bias"] + [f"L2_gnn_{n}" for n in (
        "relvectors", "w_ih", "w_hh", "b_ih", "b_hh")] + [f"L3_gnn_{n}" for n in (
            "W", "att_src", "att_dst", "bias", "ln_gamma", "ln_beta")]


def kernel(**inputs):
    import numpy as np
    import concourse.bacc as bacc
    from concourse.bass_utils import run_bass_kernel_spmd

    nc = bacc.Bacc("TRN2", target_bir_lowering=False, num_devices=1)
    arrays, args = {}, {}
    for name in _INS:
        v = np.ascontiguousarray(inputs[name])
        arrays[f"in_{name}"] = v
        args[name] = nc.dram_tensor(f"in_{name}", v.shape, mybir.dt.from_np(v.dtype), kind="ExternalInput").ap()
    out = nc.dram_tensor("out", (N, D), F32, kind="ExternalOutput").ap()
    program(nc, args, out)
    r = run_bass_kernel_spmd(nc, [arrays], core_ids=[0])
    return r.results[0]["out"]
```

```python
from contextlib import ExitStack

import concourse.bass as bass
from concourse import mybir

F32 = mybir.dt.float32
BF16 = mybir.dt.bfloat16
I32 = mybir.dt.int32
ALU = mybir.AluOpType
ACT = mybir.ActivationFunctionType
AX = mybir.AxisListType.X

P = 128
N, D, E = 6250, 256, 100000
NT = -(-N // P)
NP = NT * P
LAST = N - (NT - 1) * P
EC = -(-E // P)
ELAST = E - (P - 1) * EC
TU = 7
TI = NT // TU
U = 16
HALF = U // 2
MAXCH = (P * EC + (NT + 1) * (P - 1)) // P
CI = -(-MAXCH // U)
NCH = CI * U
NB = NT + 1
SU = 16
SI = EC // SU
SREST = EC - SI * SU
R1, L1 = 8, 3
R2 = 16
RB = R2 + 2
H, F = 4, 64
G3 = 3 * D
KD = D // P
W3 = D + H
EPS = 1e-5
BIG = float(2 ** 100)
BANKS = 4
OHS = 4
RING = 4
RING2 = 8
LAGS = 10
HA = 2
NPH = 8
READY = 4
assert NT == TU * TI and NCH == U * CI
assert all(U * min(t + READY, CI) * NT >= (t + 1) * NCH for t in range(NT)) and CI - READY <= NT


class Link:

    def __init__(self, eng, sem):
        self.eng, self.sem, self.base, self.n = eng, sem, 0, 0

    def __call__(self, ins):
        self.n += 1
        ins.then_inc(self.sem, 1)
        self.eng.wait_ge(self.sem, self.base + self.n)

    def enter(self, i, per_trip):
        self.outer, self.per_trip = self.base + self.n, per_trip
        self.base, self.n = self.outer + per_trip * i, 0

    def leave(self, trips):
        assert self.n == self.per_trip, self.n
        self.base, self.n = self.outer + self.per_trip * trips, 0


def program(nc, a, out):
    ctx = ExitStack()
    with ctx:
        def sb(name, shape, dt=F32):
            return ctx.enter_context(nc.sbuf_tensor(name, shape, dt))

        def sem(name):
            return ctx.enter_context(nc.semaphore(name))

        def dram(name, shape, dt=F32):
            return nc.dram_tensor(name, shape, dt, kind="Internal").ap()

        slots_d = dram("slots_d", [P * NCH, 4], I32)
        rows_d = dram("rows_d", [NP, D])
        rel_d = [dram(f"rel_d{k}", [R1 * NP, D]) for k in range(2)]
        att_d = dram("att_d", [NP, W3])
        src_logit_d = dram("src_logit_d", [NP, H])

        X = sb("X", [P, NT, D])
        A = sb("A", [P, NT, W3])
        Y = sb("Y", [P, NT * D])
        Y3 = Y[:, :].rearrange("p (t d) -> p t d", d=D)
        edges = sb("edges", [P, 4, NCH], I32)
        edges_f = edges[:, :, :].bitcast(F32)
        blank = edges[:, :, :].rearrange("p w c -> p (w c)").rearrange("p (c w) -> p c w", w=4)
        g = sb("g", [P, U, D + R2])
        gflat = g[:, :, :].rearrange("p u d -> p (u d)")
        bucket_of = sb("bucket_of", [1, NCH], I32)
        order_of = sb("order_of", [1, NT], I32)
        wt = sb("wt", [P, 4, KD, D])
        rows0 = sb("rows0", [P, 7, D])
        col = sb("col", [P, P])
        ident = sb("ident", [P, P])
        ones = sb("ones", [P, P])
        big_ident = sb("big_ident", [P, H, P], BF16)
        stage = sb("stage", [P, 2, D])
        turned = sb("turned", [P, 2, D])
        oh = sb("oh", [P, OHS, P])
        idx = sb("idx", [P, U], I32)
        small = sb("small", [P, 64])
        ps = ctx.enter_context(nc.psum_tensor("ps", [P, 8, 512], F32))

        aflat = A[:, :, :].rearrange("p t d -> p (t d)")

        def tmp(k, dt=F32):
            v = aflat[:, k * EC:(k + 1) * EC]
            return v if dt == F32 else v.bitcast(dt)

        payload = gflat[:, 0:4 * EC].rearrange("p (e w) -> p e w", w=4).bitcast(I32)
        payload_f = gflat[:, 0:4 * EC].rearrange("p (e w) -> p e w", w=4)
        loaded = gflat[:, 0:4 * NCH].rearrange("p (c w) -> p c w", w=4).bitcast(I32)
        slot_row = gflat[:, 4 * EC:5 * EC].bitcast(I32)
        at0 = 5 * EC
        sc_idx = gflat[:, at0:at0 + SU].bitcast(I32)
        sc_pay = gflat[:, at0 + SU:at0 + 5 * SU].rearrange("p (u w) -> p u w", w=4).bitcast(I32)
        iota_b = aflat[:, 10 * EC:10 * EC + NB]
        cnt_b, before_b, tot_b, nch_b, end_b, base_b, first_b, key_b, rank_b, order_f = (
            aflat[:, 10 * EC + 64 * k:10 * EC + 64 * k + NB] for k in range(1, 11))
        upper = aflat[:, 10 * EC + 704:10 * EC + 704 + P]
        chunk_no = aflat[:, 12 * EC:12 * EC + NCH]
        bucket_f = aflat[:, 13 * EC + 64:13 * EC + 64 + NCH]
        pairs = aflat[:, 0:NB * NB].rearrange("p (b c) -> p b c", b=NB)
        from_first, from_end = (aflat[0:1, k * NCH:(k + 1) * NCH] for k in range(2))
        pmask = small[:, 60:61]
        prow = small[:, 61:62]

        nat0 = Y[:, 0:4 * KD * D].rearrange("p (w b d) -> p w b d", w=4, b=KD)
        wrel = [Y[:, b * KD * R1 * D:(b + 1) * KD * R1 * D].rearrange(
            "p (k r d) -> p k r d", k=KD, r=R1) for b in range(2)]
        o1 = 2 * KD * R1 * D
        wroot1 = Y[:, o1:o1 + L1 * KD * D].rearrange("p (l k d) -> p l k d", l=L1, k=KD)
        bias1 = Y[:, o1 + L1 * KD * D:o1 + L1 * KD * D + L1 * D].rearrange("p (l d) -> p l d", l=L1)
        rel_out = gflat[:, 0:2 * R1 * D].rearrange("p (s r d) -> p s r d", s=2, r=R1)
        quarter = wt[:, :, :, :].rearrange("p w k d -> p w (k d)")
        nb2 = G3 // P
        nat2 = Y[:, 0:2 * nb2 * D].rearrange("p (w b d) -> p w b d", w=2, b=nb2)
        o2 = 2 * nb2 * D
        wt2 = Y[:, o2:o2 + 2 * KD * G3].rearrange("p (w k d) -> p w k d", w=2, k=KD)
        o2 += 2 * KD * G3
        b_hn = Y[:, o2:o2 + D]
        o2 += D
        relvec = Y[0:R2, o2:o2 + D]
        o2 += D
        counts = Y[:, o2:o2 + NT * R2].rearrange("p (t r) -> p t r", r=R2)
        o2 += NT * R2
        cstage = Y[:, o2:o2 + RB]
        o2 += RB
        cturned = Y[0:RB, o2:o2 + P]
        o2 += P
        stage2 = Y[:, o2:o2 + D]
        o2 += D
        turned2 = Y[:, o2:o2 + D]
        o2 += D
        relvec_t = Y[:, o2:o2 + KD * R2].rearrange("p (k r) -> p k r", k=KD)
        o2 += KD * R2
        rel_gates = Y[0:RB, o2:o2 + G3]
        o2 += G3
        rflat = rows0[:, :, :].rearrange("p k d -> p (k d)")
        gates, hn, inn = rflat[:, 0:2 * D], rflat[:, 2 * D:3 * D], rflat[:, 3 * D:4 * D]
        stats1, mv1 = small[:, 0:6], small[:, 8:10]
        assert o2 <= NT * D
        w3 = Y[:, 0:KD * D].rearrange("p (k d) -> p k d", k=KD)
        o3 = KD * D
        att_st = Y[:, o3:o3 + 2 * D].rearrange("p (s d) -> p s d", s=2)
        o3 += 2 * D
        bias3, gamma3, beta3 = (Y[:, o3 + k * D:o3 + (k + 1) * D] for k in range(3))
        o3 += 3 * D
        max_l, t_l, ex_l = (
            Y[:, o3 + k * NT * H:o3 + (k + 1) * NT * H].rearrange("p (t h) -> p t h", h=H) for k in range(3))
        o3 += 3 * NT * H
        node_l = Y[:, o3:o3 + NT * 3 * H].rearrange("p (t h) -> p t h", h=3 * H)
        o3 += NT * 3 * H
        src_l, dst_l, m_l = (node_l[:, :, k * H:(k + 1) * H] for k in range(3))
        assert o3 <= 2 * nb2 * D
        att_tmp = wt[:, 3].rearrange("p k d -> p (k d)")
        diag = Y[:, o3:o3 + RING * H * P].rearrange("p (s h e) -> p s h e", s=RING, h=H)
        o3 += RING * H * P
        miss = Y[:, o3:o3 + RING2 * P // 2].bitcast(BF16).rearrange("p (s n) -> p s n", s=RING2)
        o3 += RING2 * P // 2
        red = Y[:, o3:o3 + RING * H].rearrange("p (s h) -> p s h", s=RING)
        o3 += RING * H
        ohT = Y[:, o3:o3 + RING * P].rearrange("p (s e) -> p s e", s=RING)
        o3 += RING * P
        lg = Y[:, o3:o3 + RING * 4 * H].rearrange("p (s h) -> p s h", s=RING)
        o3 += RING * 4 * H
        wrow = Y[:, o3:o3 + RING2 * W3].rearrange("p (s d) -> p s d", s=RING2)
        o3 += RING2 * W3
        ohb = Y[:, o3:o3 + U * P].rearrange("p (s n) -> p s n", s=U)
        o3 += U * P
        assert o3 <= NT * D
        sflat = stage[:, :, :].rearrange("p s d -> p (s d)")
        stats = sflat[:, 0:NT * 6].rearrange("p (t s) -> p t s", s=6)
        mv = sflat[:, NT * 6:NT * 8].rearrange("p (t s) -> p t s", s=2)
        mean_b, scale_b = stage[:, 0, :], stage[:, 1, :]
        out0 = oh[:, :, :].rearrange("p (s q) n -> p s (q n)", s=2)

        s_dve = sem("s_dve")
        s_pool = sem("s_pool")
        s_const = sem("s_const")
        s_ident = sem("s_ident")
        s_edge_in = sem("s_edge_in")
        s_edge_pad = sem("s_edge_pad")
        s_x_pad = sem("s_x_pad")
        s_w0 = sem("s_w0")
        s_rows0 = sem("s_rows0")
        s_turn_w = sem("s_turn_w")
        s_wt = sem("s_wt")
        s_cnt = sem("s_cnt")
        s_tot = sem("s_tot")
        s_slot = sem("s_slot")
        s_blank = sem("s_blank")
        s_blank_d = sem("s_blank_d")
        s_sc = [sem(f"s_sc{k}") for k in range(2)]
        s_scat = sem("s_scat")
        s_edges = sem("s_edges")
        s_planes = sem("s_planes")
        s_stage = [sem(f"s_stage{k}") for k in range(NPH)]
        s_turn = [sem(f"s_turn{k}") for k in range(NPH)]
        s_turned = [sem(f"s_turned{k}") for k in range(NPH)]
        s_prod = [sem(f"s_prod{k}") for k in range(NPH)]
        s_evac = [sem(f"s_evac{k}") for k in range(NPH)]
        s_y = sem("s_y")
        s_sum = sem("s_sum")
        s_dev = sem("s_dev")
        s_sq = sem("s_sq")
        s_sq_used = sem("s_sq_used")
        s_h = sem("s_h")
        s_out0 = [sem(f"s_out0{k}") for k in range(2)]
        s_table = sem("s_table")
        s_var = sem("s_var")
        s_root = sem("s_root")
        s_acc0 = sem("s_acc0")
        s_x = sem("s_x")
        s_idx = [sem(f"s_idx{k}") for k in range(2)]
        s_g = [sem(f"s_g{k}") for k in range(U)]
        s_issue = sem("s_issue")
        s_oh = sem("s_oh")
        s_mm = sem("s_mm")
        s_add = sem("s_add")
        s_wrel = [sem(f"s_wrel{k}") for k in range(L1)]
        s_rel_mm = sem("s_rel_mm")
        s_rel_dve = sem("s_rel_dve")
        s_rel_act = sem("s_rel_act")
        s_rel_out = [sem(f"s_rel_out{k}") for k in range(2)]
        s_quarter_mm = sem("s_quarter_mm")
        s_quarter = sem("s_quarter")
        s_quarter_out = [sem(f"s_quarter_out{k}") for k in range(4)]
        s_w2 = sem("s_w2")
        s_turn_w2 = sem("s_turn_w2")
        s_gru_w = sem("s_gru_w")
        s_gates = sem("s_gates")
        s_cand = sem("s_cand")
        s_tanh = sem("s_tanh")
        s_var1 = sem("s_var1")
        s_root1 = sem("s_root1")
        s_norm = sem("s_norm")
        s_w3 = sem("s_w3")
        s_att_row = sem("s_att_row")
        s_att_out = sem("s_att_out")
        s_logit = sem("s_logit")
        s_diag = sem("s_diag")
        s_diag_dve = sem("s_diag_dve")
        s_miss = sem("s_miss")
        s_spread = sem("s_spread")
        s_red = sem("s_red")
        s_maxed = sem("s_maxed")
        s_shift = sem("s_shift")
        s_self = sem("s_self")
        s_ohb = sem("s_ohb")
        s_oht = sem("s_oht")
        s_ohts = sem("s_ohts")
        s_dm = sem("s_dm")
        s_l0 = sem("s_l0")
        s_l1 = sem("s_l1")
        s_e = sem("s_e")
        s_ex = sem("s_ex")
        s_wr = sem("s_wr")
        s_wr_act = sem("s_wr_act")
        s_mm3 = sem("s_mm3")
        s_add3 = sem("s_add3")
        s_out = sem("s_out")

        block = ctx.enter_context(nc.Block())
        edge_in = [a["dst"], a["src"], a["edge_type_8"], a["edge_type_16"]]
        vec0 = ["L0_gnn_b1", "L0_gnn_g1", "L0_gnn_beta1", "L0_gnn_br", "L0_gnn_b2", "L0_gnn_g2", "L0_gnn_beta2"]
        mat0 = ["L0_gnn_w1", "L0_gnn_wr", "L0_gnn_wroot", "L0_gnn_w2"]
        B1, G1, BETA1, BR, B2, G2, BETA2 = (rows0[:, k, :] for k in range(7))
        A2 = A[:, :, 0:D]

        def all_rows(v):
            return v.rearrange("(o d) -> o d", o=1).broadcast_to([P, v.shape[0]])

        def over_tiles(v):
            return v.rearrange("p (o d) -> p o d", o=1).broadcast_to([P, NT, D])

        def tile_at(v, t, width=D):
            return v[:, bass.ds(t, 1), 0:width].rearrange("p o d -> p (o d)")

        def node_rows(table):
            return table.rearrange("(t p) d -> p t d", p=P)

        def before(j):
            return j if j == 0 else j - 1

        out_uses = [TI * ((TU + 1) // 2), TI * (TU // 2)]

        def buckets_of(engine, i):
            _, values = nc.values_load_multi_w_load_instructions(
                bucket_of[0:1, bass.ds(U * i, U)], engines=(engine,), min_val=0, max_val=NT - 1,
                skip_runtime_bounds_check_because="a bucket's number counts which of NT - 1 ends lie before a chunk")
            return values

        def bucket_by_size(engine, t):
            _, values = nc.values_load_multi_w_load_instructions(
                order_of[0:1, bass.ds(t, 1)], engines=(engine,), min_val=0, max_val=NT - 1,
                skip_runtime_bounds_check_because="the buckets' numbers in another order")
            return values[0]

        def beside_sweep(eng, trip, dense):
            with eng.Fori(0, READY) as i:
                trip(i, None)
            with eng.Fori(READY, CI) as i:
                trip(i, i - READY)
            for t in range(CI - READY, NT):
                dense(t)

        def beside_gru(eng, trip, hook):
            with eng.Fori(0, READY) as i:
                trip(i, None, None)
            trip(READY, 0, None)
            with eng.Fori(READY + 1, CI) as i:
                trip(i, i - READY, i - READY - 1)
            for t in range(CI - READY, NT + 1):
                for j in range(U):
                    hook(j, t if t < NT else None, t - 1)

        def trips(eng, trip):
            trip(0, lambda k, lag: k >= lag, U)
            with eng.Fori(1, CI) as i:
                trip(i, lambda k, lag: True, U)
            trip(CI, lambda k, lag: k < lag, LAGS)

        def lagged_buckets(engine, i, lag):
            first, last = isinstance(i, int) and i == 0, isinstance(i, int) and i == CI
            at, n = (0, U - lag) if first else (U * i - lag, lag if last else U)
            _, values = nc.values_load_multi_w_load_instructions(
                bucket_of[0:1, bass.ds(at, n)], engines=(engine,), min_val=0, max_val=NT - 1,
                skip_runtime_bounds_check_because="a bucket's number counts which of NT - 1 ends lie before a chunk")
            return (0,) * lag + tuple(values) if first else values

        @block.sync
        def _(sp):
            sp.wait_ge(s_edge_pad, 4)
            for k, v in enumerate(edge_in):
                sp.dma_start(tmp(k, I32)[0:P - 1, :], v[0:(P - 1) * EC].rearrange("(p e) -> p e", e=EC))\
                    .then_inc(s_edge_in, 16)
                sp.dma_start(tmp(k, I32)[P - 1:P, 0:ELAST], v[(P - 1) * EC:E].rearrange("(o e) -> o e", o=1))\
                    .then_inc(s_edge_in, 16)
            for k, n in enumerate(mat0):
                sp.dma_start(nat0[:, k], a[n].rearrange("(b p) d -> p b d", p=P)).then_inc(s_w0, 16)
            for k, n in enumerate(vec0):
                sp.dma_start(rows0[:, k, :], all_rows(a[n])).then_inc(s_rows0, 16)
            sp.wait_ge(s_x_pad, 1)
            sp.dma_start(X[:, 0:NT - 1, :], node_rows(a["x"][0:(NT - 1) * P, :])).then_inc(s_out0[0], 16)
            sp.dma_start(X[0:LAST, NT - 1, :], a["x"][(NT - 1) * P:N, :]).then_inc(s_out0[1], 16)
            sp.wait_ge(s_blank, 1)
            sp.dma_start(slots_d.rearrange("(p c) w -> p c w", p=P), blank).then_inc(s_blank_d, 16)
            with sp.Fori(0, TI) as i:
                for j in range(TU):
                    sp.wait_ge(s_evac[1], 1 + TU * i + j + 1)
                    sp.dma_start(rows_d[bass.ds((TU * i + j) * P, P), :], out0[:, j % 2, :])\
                        .then_inc(s_out0[j % 2], 16)
            def sweep_indices(order, word, used, ahead):
                with sp.Fori(0, CI) as i:
                    for h in range(2):
                        sp.wait_ge(used, ahead + U * i + HALF * (h + 1))
                        sp.dma_start(idx[:, HALF * h:HALF * (h + 1)],
                                     edges[:, word, bass.ds(U * i + HALF * h, HALF)]).then_inc(s_idx[h], 16)

            sp.wait_ge(s_planes, 4)
            sweep_indices(0, 0, s_mm, 0)
            sp.wait_ge(s_x, 1)
            sp.dma_start(wroot1, a["L1_gnn_W_root"].rearrange("l (k p) d -> p l k d", p=P)).then_inc(s_rel_out[0], 16)
            sp.dma_start(bias1, a["L1_gnn_bias"].rearrange("(o l) d -> o l d", o=1).broadcast_to([P, L1, D]))\
                .then_inc(s_rel_out[1], 16)

            def load_wrel(layer):
                for k in range(KD):
                    sp.dma_start(wrel[layer % 2][:, k], a["L1_gnn_W_rel"][layer, :, k * P:(k + 1) * P, :]
                                 .rearrange("r p d -> p r d")).then_inc(s_wrel[layer], 16)

            load_wrel(0)
            load_wrel(1)
            with sp.Fori(0, TI) as i:
                for j in range(TU):
                    done = 2 * (TU * i + j + 1)
                    sp.wait_ge(s_rel_dve, 1 + done)
                    sp.wait_ge(s_rel_act, 1 + done)
                    sp.dma_start(rel_d[0].rearrange("(r n) d -> n r d", r=R1)[bass.ds((TU * i + j) * P, P), :, :],
                                 rel_out[:, j % 2]).then_inc(s_rel_out[j % 2], 16)
            sp.wait_ge(s_prod[3], 1 + NT)
            load_wrel(2)
            for layer in range(L1):
                sweep_indices(1 + layer, 1, s_mm, NCH * (1 + layer))
            sp.wait_ge(s_x, 2)
            sp.dma_start(node_rows(rows_d), X[:, :, :]).then_inc(s_table, 16)
            for k, n in enumerate(["L2_gnn_w_ih", "L2_gnn_w_hh"]):
                sp.dma_start(nat2[:, k], a[n].rearrange("(b p) d -> p b d", p=P)).then_inc(s_w2, 16)
            sp.dma_start(rel_gates[R2:R2 + 1, :], a["L2_gnn_b_ih"].rearrange("(o d) -> o d", o=1)).then_inc(s_w2, 16)
            sp.dma_start(rel_gates[R2 + 1:RB, 0:2 * D], a["L2_gnn_b_hh"][0:2 * D].rearrange("(o d) -> o d", o=1))\
                .then_inc(s_w2, 16)
            sp.dma_start(b_hn, all_rows(a["L2_gnn_b_hh"][2 * D:G3])).then_inc(s_w2, 16)
            sp.dma_start(relvec, a["L2_gnn_relvectors"]).then_inc(s_w2, 16)
            sp.wait_ge(s_turn_w2, 2 * KD)
            sp.dma_start(w3, a["L3_gnn_W"].rearrange("(k p) d -> p k d", p=P)).then_inc(s_w3, 16)
            for k, n in enumerate(["L3_gnn_att_src", "L3_gnn_att_dst"]):
                sp.dma_start(att_st[:, k, :], all_rows(a[n].rearrange("h f -> (h f)"))).then_inc(s_w3, 16)
            for v, n in ((bias3, "L3_gnn_bias"), (gamma3, "L3_gnn_ln_gamma"), (beta3, "L3_gnn_ln_beta")):
                sp.dma_start(v, all_rows(a[n])).then_inc(s_w3, 16)
            sweep_indices(4, 0, s_mm, NCH * 4)
            sp.wait_ge(s_logit, 1)
            sp.dma_start(node_rows(src_logit_d), src_l).then_inc(s_table, 16)
            for order in (5, 6):
                with sp.Fori(0, CI) as i:
                    for h in range(2):
                        for j in range(HALF * h, HALF * (h + 1)):
                            sp.wait_ge(s_g[j], 16 * (CI * order + i))
                        sp.dma_start(idx[:, HALF * h:HALF * (h + 1)],
                                     edges[:, 0, bass.ds(U * i + HALF * h, HALF)]).then_inc(s_idx[h], 16)
            sp.wait_ge(s_x, 3)
            sp.dma_start(node_rows(out[0:(NT - 1) * P, :]), X[:, 0:NT - 1, :]).then_inc(s_out, 16)
            sp.dma_start(out[(NT - 1) * P:N, :], X[0:LAST, NT - 1, :]).then_inc(s_out, 16)
            sp.wait_ge(s_out, 32)

        @block.gpsimd
        def _(pool):
            link = Link(pool, s_pool)
            pool.memset(tmp(0, I32), NT * P).then_inc(s_edge_pad, 1)
            for k in range(1, 4):
                pool.memset(tmp(k, I32), 0).then_inc(s_edge_pad, 1)
            pool.iota(col[:, :], pattern=[[1, P]], base=0, channel_multiplier=0,
                      allow_small_or_imprecise_dtypes=True).then_inc(s_const, 1)
            pool.iota(prow, pattern=[[1, 1]], base=0, channel_multiplier=1,
                      allow_small_or_imprecise_dtypes=True).then_inc(s_const, 1)
            pool.iota(iota_b, pattern=[[1, NB]], base=0, channel_multiplier=0,
                      allow_small_or_imprecise_dtypes=True).then_inc(s_const, 1)
            pool.iota(chunk_no, pattern=[[1, NCH]], base=0, channel_multiplier=0,
                      allow_small_or_imprecise_dtypes=True).then_inc(s_const, 1)
            pool.memset(ones[:, :], 1.0).then_inc(s_const, 1)
            pool.memset(X[:, NT - 1, :], 0.0).then_inc(s_x_pad, 1)
            link(pool.memset(blank, 0))
            pool.memset(blank.bitcast(F32)[:, :, 2:3], float(P)).then_inc(s_blank, 1)

            pool.wait_ge(s_slot, 1)
            pool.wait_ge(s_blank_d, 16)

            def scatter(k, s):
                pool.indirect_dma_start(
                    out=slots_d, out_offset=bass.IndirectOffsetOnAxis(ap=sc_idx[:, k:k + 1], axis=0),
                    in_=sc_pay[:, k, :], in_offset=None).then_inc(s, 16)

            half = SU // 2

            def stage_edges(at, h):
                link(pool.tensor_copy(sc_idx[:, half * h:half * (h + 1)], slot_row[:, bass.ds(at, half)]))
                link(pool.tensor_copy(sc_pay[:, half * h:half * (h + 1), :], payload[:, bass.ds(at, half), :]))
                pool.sem_inc(s_issue, 1)
                for k in range(half * h, half * (h + 1)):
                    scatter(k, s_sc[h])

            stage_edges(0, 0)
            stage_edges(half, 1)
            with pool.Fori(1, SI) as i:
                link.enter(i - 1, 4)
                for h in range(2):
                    pool.wait_ge(s_sc[h], 16 * half * i)
                    stage_edges(SU * i + half * h, h)
                link.leave(SI - 1)
            for h in range(2):
                pool.wait_ge(s_sc[h], 16 * half * SI)
            link(pool.tensor_copy(sc_idx[:, 0:SREST], slot_row[:, SU * SI:EC]))
            link(pool.tensor_copy(sc_pay[:, 0:SREST, :], payload[:, SU * SI:EC, :]))
            for k in range(SREST):
                scatter(k, s_scat)
            pool.wait_ge(s_scat, 16 * SREST)
            pool.dma_start(loaded, slots_d.rearrange("(p c) w -> p c w", p=P)).then_inc(s_edges, 16)

            def gathers(order, table, width, free, ahead):
                with pool.Fori(0, CI) as i:
                    for j in range(U):
                        if j % HALF == 0:
                            pool.wait_ge(s_idx[j // HALF], 16 * (CI * order + i + 1))
                        pool.wait_ge(free, ahead + U * i + j + 1)
                        pool.sem_inc(s_issue, 1)
                        pool.indirect_dma_start(
                            out=g[:, j, 0:width], out_offset=None, in_=table,
                            in_offset=bass.IndirectOffsetOnAxis(ap=idx[:, j:j + 1], axis=0)).then_inc(s_g[j], 16)

            for b in range(2):
                pool.wait_ge(s_out0[b], 16 * (1 + out_uses[b]))
            gathers(0, rows_d, D, s_mm, 0)
            for b in range(2):
                pool.wait_ge(s_rel_out[b], 16 * (1 + out_uses[b]))
            gathers(1, rel_d[0], D, s_mm, NCH)
            for layer in range(1, L1):
                for q in range(4):
                    pool.wait_ge(s_quarter_out[q], 16 * (1 + NT * layer))
                gathers(1 + layer, rel_d[layer % 2], D, s_mm, NCH * (1 + layer))
            pool.wait_ge(s_table, 16)
            gathers(4, rows_d, D, s_mm, NCH * 4)
            pool.wait_ge(s_table, 32)
            gathers(5, src_logit_d, H, s_spread, 0)
            pool.wait_ge(s_att_out, 16)
            pool.wait_ge(s_spread, U + NCH)
            gathers(6, att_d, W3, s_mm3, 0)

        @block.scalar
        def _(act):
            def copy(o, v):
                return act.activation(o, v, ACT.Copy)

            act.sem_inc(s_ohts, U)
            act.sem_inc(s_ex, U)
            act.sem_inc(s_quarter, 2)
            act.sem_inc(s_gates, 1)
            for s in s_turned + [s_rel_act]:
                act.sem_inc(s, 1)
            for s in s_quarter_out:
                act.sem_inc(s, 16)

            for k in range(4):
                act.wait_ge(s_turn_w, k + 1)
                copy(wt[:, k].rearrange("p k (b o) -> p k b o", b=KD),
                     ps[:, k, :].rearrange("p (b k o) -> p k b o", b=KD, k=KD)).then_inc(s_wt, 1)

            def turn_tiles(ph, staged, extra=None, begin=0):
                def put(i, j):
                    act.wait_ge(s_turn[ph], 1 + TU * i + before(j))
                    staged(j % 2, TU * i + j).then_inc(s_stage[ph], 1)

                with act.Fori(0, TI) as i:
                    put(i, 0)
                    for j in range(TU):
                        if j + 1 < TU:
                            put(i, j + 1)
                        act.wait_ge(s_turn[ph], 1 + TU * i + j + 1)
                        act.wait_ge(s_prod[ph], 1 + TU * i + before(j))
                        copy(turned[:, j % 2, :], ps[:, 6 + j % 2, 0:D]).then_inc(s_turned[ph], 1)
                        if extra:
                            extra(i, j)

            roots = [0]

            def root(v):
                roots[0] += 1
                act.wait_ge(s_var, roots[0])
                act.activation(v, v, ACT.Sqrt).then_inc(s_root, 1)

            def squares(k):
                with act.Fori(0, TI) as i:
                    for j in range(TU):
                        act.wait_ge(s_sq_used, 1 + NT * k + TU * i + before(j))
                        act.activation(turned[:, j % 2, :], tile_at(Y3, TU * i + j), ACT.Square).then_inc(s_sq, 1)

            for b in range(2):
                act.wait_ge(s_out0[b], 16)
            turn_tiles(0, lambda b, t: copy(stage[:, b, :], tile_at(X, t)))
            act.wait_ge(s_dev, 1)
            squares(0)
            root(scale_b)
            act.wait_ge(s_h, 1)
            turn_tiles(1, lambda b, t: copy(stage[:, b, :], tile_at(Y3, t)))
            act.wait_ge(s_edges, 16)
            for w in range(4):
                act.copy(edges[:, w, :], loaded[:, :, w]).then_inc(s_planes, 1)
            act.wait_ge(s_add, U + NCH)
            turn_tiles(2, lambda b, t: act.activation(stage[:, b, :], tile_at(A, t), ACT.Gelu))
            act.wait_ge(s_dev, 2)
            squares(1)
            root(scale_b)
            root(mv[:, :, 1])

            act.wait_ge(s_x, 1)

            def rel_rows(i, j):
                for q in (1, 3):
                    act.wait_ge(s_rel_mm, 4 * (TU * i + j) + q + 1)
                    if q == 1:
                        act.wait_ge(s_rel_out[j % 2], 16 * (
                            1 + ((TU + 1) // 2 if j % 2 == 0 else TU // 2) * i + j // 2))
                    copy(rel_out[:, j % 2, 2 * q:2 * q + 2, :].rearrange("p r d -> p (r d)"), ps[:, q, :])\
                        .then_inc(s_rel_act, 1)

            turn_tiles(3, lambda b, t: copy(stage[:, b, :], tile_at(X, t)), rel_rows)
            act.wait_ge(s_prod[2], 1 + NT)
            for layer in range(1, L1):
                table = rel_d[layer % 2].rearrange("(r n) d -> n r d", r=R1)

                def rel_tile(t):
                    ph, first = 3 + layer, 4 * (NT * (layer - 1) + t)
                    bucket = bucket_by_size(mybir.EngineType.Activation, t)
                    act.wait_ge(s_turn[ph], 1 + t)
                    act.activation(stage[:, 0, :], tile_at(A, bucket), ACT.Relu).then_inc(s_stage[ph], 1)
                    act.wait_ge(s_turn[ph], 1 + t + 1)
                    act.wait_ge(s_prod[ph], 1 + t)
                    copy(turned[:, 0, :], ps[:, 7, 0:D]).then_inc(s_turned[ph], 1)
                    for q in range(4):
                        act.wait_ge(s_quarter_mm, first + q + 1)
                        act.wait_ge(s_quarter_out[q], 16 * (1 + NT * (layer - 1) + t))
                        copy(quarter[:, q, :], ps[:, 4 + q % 2, :]).then_inc(s_quarter, 1)
                        act.wait_ge(s_quarter, 2 + first + q + 1)
                        act.dma_start(table[bass.ds(bucket * P, P), 2 * q:2 * q + 2, :],
                                      quarter[:, q, :].rearrange("p (r d) -> p r d", r=2)).then_inc(s_quarter_out[q], 16)

                with act.Fori(READY, CI) as i:
                    act.wait_ge(s_add, U + NCH * layer + U * i)
                    rel_tile(i - READY)
                act.wait_ge(s_add, U + NCH * (layer + 1))
                for t in range(CI - READY, NT):
                    rel_tile(t)
            root(mv[:, :, 1])
            for k in range(2):
                for h in range(KD):
                    act.wait_ge(s_turn_w2, KD * k + h + 1)
                    copy(wt2[:, k, h, 0:512], ps[:, 2 * h, :])
                    copy(wt2[:, k, h, 512:G3], ps[:, 2 * h + 1, 0:G3 - 512]).then_inc(s_gru_w, 1)
            act.wait_ge(s_turn_w2, 2 * KD + 1)
            copy(relvec_t, ps[:, 4, 0:KD * R2].rearrange("p (k r) -> p k r", k=KD)).then_inc(s_gru_w, 1)
            act.wait_ge(s_turn_w2, 2 * KD + 2)
            copy(rel_gates[0:R2, 0:512], ps[0:R2, 5, :])
            copy(rel_gates[0:R2, 512:G3], ps[0:R2, 6, 0:G3 - 512]).then_inc(s_gru_w, 1)

            def gru_tile(t, u):
                if t is not None:
                    bucket = bucket_by_size(mybir.EngineType.Activation, t)
                    act.wait_ge(s_turn[6], 1 + t)
                    copy(stage[:, 0, :], tile_at(A, bucket))
                    copy(cstage[:, 0:R2], tile_at(counts, bucket, R2))
                    copy(stage2, tile_at(X, bucket)).then_inc(s_stage[6], 1)
                    act.wait_ge(s_turn[6], 1 + t + 1)
                    act.wait_ge(s_prod[6], 1 + t)
                    copy(turned[:, 0, :], ps[:, 6, 0:D])
                    copy(turned2, ps[:, 6, D:2 * D])
                    copy(cturned, ps[0:RB, 7, 0:P]).then_inc(s_turned[6], 1)
                if u is not None:
                    last = bucket_by_size(mybir.EngineType.Activation, u)
                    act.wait_ge(s_var1, u + 1)
                    act.activation(mv1[:, 1:2], mv1[:, 1:2], ACT.Sqrt).then_inc(s_root1, 1)
                    act.wait_ge(s_norm, u + 1)
                    act.wait_ge(s_turn[7], 1 + u)
                    copy(stage[:, 1, :], tile_at(X, last)).then_inc(s_stage[7], 1)
                    act.wait_ge(s_turn[7], 1 + u + 1)
                    act.wait_ge(s_prod[7], 1 + u)
                    copy(turned[:, 1, :], ps[:, 7, 0:D]).then_inc(s_turned[7], 1)
                if t is not None:
                    act.wait_ge(s_prod[6], 1 + t + 1)
                    act.activation(gates, ps[:, 4, :], ACT.Sigmoid).then_inc(s_gates, 1)
                    act.wait_ge(s_cand, 1 + t + 1)
                    act.activation(inn, inn, ACT.Tanh).then_inc(s_tanh, 1)

            act.wait_ge(s_add, U + NCH * 4 + U * READY)
            gru_tile(0, None)
            with act.Fori(READY + 1, CI) as i:
                act.wait_ge(s_add, U + NCH * 4 + U * i)
                gru_tile(i - READY, i - READY - 1)
            act.wait_ge(s_add, U + NCH * 5)
            for t in range(CI - READY, NT + 1):
                gru_tile(t if t < NT else None, t - 1)

            act.wait_ge(s_logit, 1)
            act.dma_start(node_rows(att_d), A[:, :, :]).then_inc(s_att_out, 16)
            with act.Fori(0, CI) as i:
                for j in range(U):
                    act.wait_ge(s_g[j], 16 * (CI * 5 + i + 1))
                    act.wait_ge(s_spread, U + U * i + j - RING + 1)
                    for h in range(H - 1):
                        ins = act.activation(diag[:, j % RING, h, :], ident[:, :], ACT.Copy, scale=g[:, j, h:h + 1])
                    ins.then_inc(s_diag, 1)
            act.wait_ge(s_shift, 1)
            act.activation(ex_l, t_l, ACT.Exp).then_inc(s_self, 1)

            def second_pass(i, due, steps):
                for k in range(steps):
                    if due(k, 0):
                        c, s = U * i + k, k % RING
                        act.wait_ge(s_oht, c + 1)
                        act.wait_ge(s_dm, U + c - RING + 1)
                        copy(ohT[:, s, :], ps[:, 4 + k % 2, 0:P]).then_inc(s_ohts, 1)
                    if due(k, 6):
                        c, s, r = U * i + k - 6, (k - 6) % RING, (k - 6) % RING2
                        act.wait_ge(s_e, U + c + 1)
                        act.wait_ge(s_mm3, U + c - RING2 + 1)
                        act.activation(wrow[:, r, D:W3], lg[:, s, 3 * H:4 * H], ACT.Exp).then_inc(s_ex, 1)
                    if due(k, 7):
                        c, j, r = U * i + k - 7, (k - 7) % U, (k - 7) % RING2
                        act.wait_ge(s_ex, U + c + 1)
                        for h in range(HA):
                            ins = act.activation(wrow[:, r, h * F:(h + 1) * F], g[:, j, h * F:(h + 1) * F], ACT.Copy,
                                                 scale=wrow[:, r, D + h:D + h + 1])
                        ins.then_inc(s_wr_act, 1)

            trips(act, second_pass)
            root(mv[:, :, 1])
            root(mv[:, :, 1])

        @block.tensor
        def _(pe):
            pe.sem_inc(s_mm, U)
            pe.sem_inc(s_spread, U)
            pe.sem_inc(s_dm, U)
            pe.sem_inc(s_mm3, U)
            for s in s_turn + s_prod + [s_sq_used]:
                pe.sem_inc(s, 1)

            pe.wait_ge(s_ident, 1)
            pe.wait_ge(s_w0, 64)
            for w in range(4):
                for b in range(KD):
                    for k in range(KD):
                        at = (b * KD + k) * P
                        ins = pe.transpose(ps[:, w, at:at + P], nat0[:, w, b, k * P:(k + 1) * P], ident[:, :])
                ins.then_inc(s_turn_w, 1)

            def turn_tiles(ph, products):
                def turn(i, j):
                    pe.wait_ge(s_stage[ph], TU * i + j + 1)
                    pe.wait_ge(s_turned[ph], 1 + TU * i + before(j))
                    for k in range(KD):
                        ins = pe.transpose(ps[:, 6 + j % 2, k * P:(k + 1) * P], stage[:, j % 2, k * P:(k + 1) * P],
                                           ident[:, :])
                    ins.then_inc(s_turn[ph], 1)

                with pe.Fori(0, TI) as i:
                    turn(i, 0)
                    for j in range(TU):
                        if j + 1 < TU:
                            turn(i, j + 1)
                        pe.wait_ge(s_turned[ph], 1 + TU * i + j + 1)
                        products(i, j)

            def product(o, b, w):
                for k in range(KD):
                    ins = pe.matmul(o, turned[:, b, k * P:(k + 1) * P], w[:, k, :], start=(k == 0), stop=(k == KD - 1))
                return ins

            def one_product(ph, w):
                def products(i, j):
                    pe.wait_ge(s_evac[ph], 1 + TU * i + before(j))
                    product(ps[:, j % 2, 0:D], j % 2, wt[:, w]).then_inc(s_prod[ph], 1)
                turn_tiles(ph, products)

            def sum_nodes(k):
                pe.wait_ge(s_y, k + 1)
                pe.matmul(ps[:, 4, 0:D], ones[:, :], Y3[:, 0, :], start=True, stop=False, skip_group_check=True)
                with pe.Fori(0, (NT - 1) // 8) as i:
                    for j in range(8):
                        ins = pe.matmul(ps[:, 4, 0:D], ones[:, :], tile_at(Y3, 8 * i + j + 1), start=False,
                                        stop=(j == 7), skip_group_check=True)
                pe.drain().then_inc(s_sum, 1)
                pe.wait_ge(s_sq, NT * k + 1)
                pe.matmul(ps[:, 5, 0:D], ones[:, :], turned[:, 0, :], start=True, stop=False,
                          skip_group_check=True).then_inc(s_sq_used, 1)
                for j in range(1, TU):
                    pe.wait_ge(s_sq, NT * k + j + 1)
                    pe.matmul(ps[:, 5, 0:D], ones[:, :], turned[:, j % 2, :], start=False, stop=(j == TU - 1),
                              skip_group_check=True).then_inc(s_sq_used, 1)
                with pe.Fori(1, TI) as i:
                    for j in range(TU):
                        pe.wait_ge(s_sq, NT * k + TU * i + j + 1)
                        pe.matmul(ps[:, 5, 0:D], ones[:, :], turned[:, j % 2, :], start=False, stop=(j == TU - 1),
                                  skip_group_check=True).then_inc(s_sq_used, 1)
                pe.drain().then_inc(s_sum, 1)

            def sum_chunk(order, width, i, j):
                c = NCH * order + U * i + j
                pe.wait_ge(s_oh, c + 1)
                pe.wait_ge(s_g[j], 16 * (CI * order + i + 1))
                pe.wait_ge(s_add, U + c - BANKS + 1)
                pe.matmul(ps[:, j % BANKS, 0:width], oh[:, j % OHS, :], g[:, j, 0:width],
                          start=True, stop=True).then_inc(s_mm, 1)

            def sums(order, width):
                with pe.Fori(0, CI) as i:
                    for j in range(U):
                        sum_chunk(order, width, i, j)

            pe.wait_ge(s_cnt, 1)
            pe.matmul(ps[:, 5, 0:NB], upper, cnt_b, start=True, stop=True)
            pe.matmul(ps[:, 5, 64:64 + NB], ones[:, :], cnt_b, start=True, stop=True).then_inc(s_tot, 1)

            pe.wait_ge(s_wt, 4)
            one_product(0, 0)
            sum_nodes(0)

            def two_products(i, j):
                pe.wait_ge(s_evac[1], 1 + TU * i + before(j))
                product(ps[:, j % 2, 0:D], j % 2, wt[:, 1])
                product(ps[:, 2 + j % 2, 0:D], j % 2, wt[:, 2]).then_inc(s_prod[1], 1)

            turn_tiles(1, two_products)
            pe.wait_ge(s_evac[1], 1 + NT)
            sums(0, D)
            pe.wait_ge(s_add, U + NCH)
            one_product(2, 3)
            sum_nodes(1)

            pe.wait_ge(s_rel_out[0], 16)
            relations = [v.rearrange("p k r d -> p k (r d)") for v in wrel]

            def rel_products(i, j):
                for q in range(4):
                    if q % 2:
                        pe.wait_ge(s_rel_act, 1 + 2 * (TU * i + j))
                    else:
                        pe.wait_ge(s_rel_dve, 1 + 2 * (TU * i + j))
                    for k in range(KD):
                        ins = pe.matmul(ps[:, q, :], turned[:, j % 2, k * P:(k + 1) * P],
                                        relations[0][:, k, q * 512:(q + 1) * 512], start=(k == 0), stop=(k == KD - 1))
                    ins.then_inc(s_rel_mm, 1)
                pe.wait_ge(s_evac[3], 1 + TU * i + j)
                product(ps[:, 4, 0:D], j % 2, wroot1[:, 0]).then_inc(s_prod[3], 1)

            pe.wait_ge(s_wrel[0], 32)
            turn_tiles(3, rel_products)
            pe.wait_ge(s_rel_act, 1 + 2 * NT)
            pe.wait_ge(s_rel_dve, 1 + 2 * NT)
            pe.wait_ge(s_evac[3], 1 + NT)
            for layer in range(1, L1):
                w, ph = relations[layer % 2], 3 + layer

                def rel_turn(t):
                    pe.wait_ge(s_stage[ph], t + 1)
                    pe.wait_ge(s_turned[ph], 1 + t)
                    for k in range(KD):
                        ins = pe.transpose(ps[:, 7, k * P:(k + 1) * P], stage[:, 0, k * P:(k + 1) * P], ident[:, :])
                    ins.then_inc(s_turn[ph], 1)

                def rel_quarter(t, q):
                    if q == 0:
                        pe.wait_ge(s_turned[ph], 1 + t + 1)
                    pe.wait_ge(s_quarter, 4 * (NT * (layer - 1) + t) + q + 1)
                    for k in range(KD):
                        ins = pe.matmul(ps[:, 4 + q % 2, :], turned[:, 0, k * P:(k + 1) * P],
                                        w[:, k, q * 512:(q + 1) * 512], start=(k == 0), stop=(k == KD - 1))
                    ins.then_inc(s_quarter_mm, 1)

                def rel_root(t):
                    pe.wait_ge(s_evac[ph], 1 + t)
                    product(ps[:, 6, 0:D], 0, wroot1[:, layer]).then_inc(s_prod[ph], 1)

                def trip(i, t):
                    for j in range(U):
                        sum_chunk(layer, D, i, j)
                        if t is not None:
                            if j == 2:
                                rel_turn(t)
                            if j in (5, 8, 11, 13):
                                rel_quarter(t, (5, 8, 11, 13).index(j))
                            if j == U - 1:
                                rel_root(t)

                def dense(t):
                    rel_turn(t)
                    for q in range(4):
                        rel_quarter(t, q)
                    rel_root(t)

                pe.wait_ge(s_wrel[layer], 32)
                beside_sweep(pe, trip, dense)
                pe.wait_ge(s_evac[ph], 1 + NT)
            sums(L1, D)
            pe.wait_ge(s_add, U + NCH * (1 + L1))

            pe.wait_ge(s_w2, 96)
            for w in range(2):
                for k in range(KD):
                    if w:
                        pe.wait_ge(s_gru_w, k + 1)
                    for b in range(nb2):
                        ins = pe.transpose(ps[:, 2 * k + b // 4, b % 4 * P:(b % 4 + 1) * P],
                                           nat2[:, w, b, k * P:(k + 1) * P], ident[:, :])
                    ins.then_inc(s_turn_w2, 1)
            for k in range(KD):
                ins = pe.transpose(ps[:, 4, k * R2:(k + 1) * R2], relvec[:, k * P:(k + 1) * P], ident[0:R2, 0:R2])
            ins.then_inc(s_turn_w2, 1)
            pe.wait_ge(s_gru_w, 2 * KD + 1)
            for o, lo, hi in ((ps[0:R2, 5, :], 0, 512), (ps[0:R2, 6, 0:G3 - 512], 512, G3)):
                for k in range(KD):
                    ins = pe.matmul(o, relvec_t[:, k, :], wt2[:, 0, k, lo:hi], start=(k == 0), stop=(k == KD - 1))
            ins.then_inc(s_turn_w2, 1)
            pe.wait_ge(s_gru_w, 2 * KD + 2)
            pe.wait_ge(s_w3, 96)

            def gru_steps(j, t, u):
                if t is not None and j == 1:
                    pe.wait_ge(s_stage[6], t + 1)
                    pe.wait_ge(s_turned[6], 1 + t)
                    if u is not None:
                        pe.wait_ge(s_evac[7], 1 + u)
                    for v, at in ((stage[:, 0, :], 0), (stage2, D)):
                        for k in range(KD):
                            pe.transpose(ps[:, 6, at + k * P:at + (k + 1) * P], v[:, k * P:(k + 1) * P], ident[:, :])
                    pe.transpose(ps[0:RB, 7, 0:P], cstage, ident[:, :]).then_inc(s_turn[6], 1)
                rz, inp, hid = ps[:, 4, :], ps[:, 5, 0:D], ps[:, 5, D:2 * D]
                if t is not None and j in (3, 5):
                    if j == 3:
                        pe.wait_ge(s_turned[6], 1 + t + 1)
                        pe.wait_ge(s_gates, 1 + t)
                        pe.wait_ge(s_cand, 1 + t)
                    k = (j - 3) // 2
                    pe.matmul(rz, turned[:, 0, k * P:(k + 1) * P], wt2[:, 0, k, 0:2 * D], start=(k == 0), stop=False)
                    pe.matmul(rz, turned2[:, k * P:(k + 1) * P], wt2[:, 1, k, 0:2 * D], start=False, stop=False)
                if u is not None and j == 6:
                    pe.wait_ge(s_stage[7], u + 1)
                    if t is not None:
                        pe.wait_ge(s_turned[6], 1 + t + 1)
                    for k in range(KD):
                        ins = pe.transpose(ps[:, 7, k * P:(k + 1) * P], stage[:, 1, k * P:(k + 1) * P], ident[:, :])
                    ins.then_inc(s_turn[7], 1)
                if t is not None and j == 7:
                    pe.matmul(rz, cturned, rel_gates[:, 0:2 * D], start=False, stop=True)
                    for k in range(KD):
                        pe.matmul(inp, turned[:, 0, k * P:(k + 1) * P], wt2[:, 0, k, 2 * D:G3], start=(k == 0), stop=False)
                    pe.matmul(inp, cturned, rel_gates[:, 2 * D:G3], start=False, stop=True)
                if t is not None and j == 8:
                    for k in range(KD):
                        ins = pe.matmul(hid, turned2[:, k * P:(k + 1) * P], wt2[:, 1, k, 2 * D:G3],
                                        start=(k == 0), stop=(k == KD - 1))
                    ins.then_inc(s_prod[6], 1)
                if u is not None and j == 9:
                    pe.wait_ge(s_turned[7], 1 + u + 1)
                    product(ps[:, 7, D:2 * D], 1, w3).then_inc(s_prod[7], 1)

            def gru_trip(i, t, u):
                for j in range(U):
                    sum_chunk(4, D + R2, i, j)
                    gru_steps(j, t, u)

            beside_gru(pe, gru_trip, gru_steps)
            pe.wait_ge(s_add, U + NCH * 5)
            pe.wait_ge(s_evac[7], 1 + NT)
            with pe.Fori(0, CI) as i:
                for j in range(U):
                    c = U * i + j
                    pe.wait_ge(s_diag, c + 1)
                    pe.wait_ge(s_diag_dve, c + 1)
                    pe.wait_ge(s_miss, c + 1)
                    pe.wait_ge(s_red, U + c - 8 + 1)
                    o = ps[:, j % 8, :]
                    pe.matmul(o, ones[:, :], diag[:, j % RING].rearrange("p h e -> p (h e)"), start=True, stop=False)
                    pe.matmul(o, miss[:, j % RING2, :], big_ident[:, :, :].rearrange("p h e -> p (h e)"),
                              start=False, stop=True).then_inc(s_spread, 1)
            pe.wait_ge(s_self, 1)
            pe.wait_ge(s_acc0, 1)

            def second_pass(i, due, steps):
                buckets = lagged_buckets(mybir.EngineType.PE, i, 2)
                for k in range(steps):
                    if due(k, 9):
                        c, j, r = U * i + k - 9, (k - 9) % U, (k - 9) % RING2
                        pe.wait_ge(s_wr, c + 1)
                        pe.wait_ge(s_wr_act, c + 1)
                        pe.wait_ge(s_add3, U + c - BANKS + 1)
                        pe.matmul(ps[:, j % BANKS, 0:W3], ohb[:, j, :], wrow[:, r, :], start=True, stop=True)\
                            .then_inc(s_mm3, 1)
                    if due(k, 0):
                        c = U * i + k
                        pe.wait_ge(s_ohb, c + 1)
                        pe.wait_ge(s_ohts, U + c - 2 + 1)
                        pe.transpose(ps[:, 4 + k % 2, 0:P], ohb[:, k, :], ident[:, :]).then_inc(s_oht, 1)
                    if due(k, 2):
                        c, s = U * i + k - 2, (k - 2) % RING
                        pe.wait_ge(s_ohts, U + c + 1)
                        pe.wait_ge(s_l0, U + c - 2 + 1)
                        pe.matmul(ps[:, 6 + k % 2, 0:2 * H], ohT[:, s, :], node_l[:, bass.ds(buckets[k], 1), H:3 * H].rearrange("p o h -> p (o h)"),
                                  start=True, stop=True).then_inc(s_dm, 1)

            trips(pe, second_pass)

        @block.vector
        def _(dve):
            link = Link(dve, s_dve)
            dve.sem_inc(s_add, U)
            dve.sem_inc(s_red, U)
            dve.sem_inc(s_e, U)
            dve.sem_inc(s_cand, 1)
            dve.sem_inc(s_l0, U)
            dve.sem_inc(s_add3, U)
            dve.sem_inc(s_maxed, U)
            for s in s_evac + [s_rel_dve]:
                dve.sem_inc(s, 1)

            dve.wait_ge(s_const, 5)
            dve.tensor_scalar(upper, col[:, :], prow, None, ALU.is_gt)
            dve.tensor_scalar(pmask, prow, float(LAST), None, ALU.is_lt)
            link(dve.tensor_scalar(ident[:, :], col[:, :], prow, None, ALU.is_equal))
            for h in range(H):
                ins = dve.tensor_scalar(big_ident[:, h, :], ident[:, :], BIG, None, ALU.mult)
            ins.then_inc(s_ident, 1)

            dst_i, src_i, rel_i, typ_i, int_w = (tmp(k, I32) for k in range(5))
            bucket, node, work, rank, pos = (tmp(k) for k in range(5, 10))
            dve.wait_ge(s_edge_in, 16 * 8)
            link(dve.tensor_scalar(int_w, dst_i, 7, None, ALU.logical_shift_right))
            link(dve.tensor_copy(bucket, int_w))
            link(dve.tensor_copy(node, dst_i))
            link(dve.scalar_tensor_tensor(node, bucket, -float(P), node, ALU.mult, ALU.add))
            link(dve.tensor_scalar(work, bucket, float(NT), float(P), ALU.is_equal, ALU.mult))
            link(dve.tensor_tensor(payload_f[:, :, 2], node, work, ALU.add))
            link(dve.tensor_copy(payload[:, :, 0], src_i))
            link(dve.tensor_copy(payload_f[:, :, 3], typ_i))
            link(dve.tensor_copy(node, rel_i))
            link(dve.tensor_copy(work, src_i))
            link(dve.scalar_tensor_tensor(payload[:, :, 1], node, float(NP), work, ALU.mult, ALU.add))
            link(dve.memset(pos, 0.0))
            with dve.Fori(0, NB) as b:
                link.enter(b, 5)
                link(dve.tensor_scalar(work, bucket, iota_b[:, bass.ds(b, 1)], None, ALU.is_equal))
                link(dve.tensor_tensor_scan(rank, work, work, 0.0, ALU.add, ALU.max))
                link(dve.tensor_scalar(cnt_b[:, bass.ds(b, 1)], rank[:, EC - 1:EC], 1.0, None, ALU.mult))
                link(dve.tensor_tensor(rank, rank, work, ALU.mult))
                link(dve.tensor_tensor(pos, pos, rank, ALU.add))
                link.leave(NB)
            dve.sem_inc(s_cnt, 1)
            dve.wait_ge(s_tot, 1)
            before_p, total_p = ps[:, 5, 0:NB], ps[:, 5, 64:64 + NB]

            def by_bucket(v):
                return v.rearrange("p (b o) -> p b o", o=1).broadcast_to([P, NB, NB])

            def by_other(v):
                return v.rearrange("p (o b) -> p o b", o=1).broadcast_to([P, NB, NB])

            int_b, chunks_i = before_b.bitcast(I32), tot_b.bitcast(I32)
            link(dve.tensor_scalar(int_b, total_p, float(P - 1), None, ALU.add))
            link(dve.tensor_scalar(chunks_i, int_b, 7, None, ALU.logical_shift_right))
            link(dve.tensor_copy(nch_b, chunks_i))
            link(dve.scalar_tensor_tensor(key_b, nch_b, 64.0, iota_b, ALU.mult, ALU.add))
            link(dve.memset(key_b[:, NT:NB], 64.0 * (NCH + 1)))
            link(dve.tensor_tensor(pairs, by_other(key_b), by_bucket(key_b), ALU.is_lt))
            link(dve.tensor_reduce(rank_b, pairs, AX, ALU.add))
            link(dve.tensor_tensor(pairs, pairs, by_other(nch_b), ALU.mult))
            link(dve.tensor_reduce(first_b, pairs, AX, ALU.add))
            link(dve.tensor_tensor(end_b, first_b, nch_b, ALU.add))
            link(dve.tensor_scalar(base_b, first_b, float(P), -1.0, ALU.mult, ALU.add))
            link(dve.tensor_tensor(base_b, base_b, before_p, ALU.add))
            with dve.Fori(0, NB) as b:
                link.enter(b, 2)
                link(dve.tensor_scalar(work, bucket, iota_b[:, bass.ds(b, 1)], base_b[:, bass.ds(b, 1)],
                                       ALU.is_equal, ALU.mult))
                link(dve.tensor_tensor(pos, pos, work, ALU.add))
                link.leave(NB)
            link(dve.tensor_copy(int_w, pos))
            link(dve.tensor_scalar(dst_i, int_w, P - 1, None, ALU.bitwise_and))
            link(dve.tensor_scalar(src_i, int_w, 7, None, ALU.logical_shift_right))
            link(dve.tensor_copy(node, dst_i))
            link(dve.tensor_copy(work, src_i))
            dve.scalar_tensor_tensor(slot_row, node, float(NCH), work, ALU.mult, ALU.add).then_inc(s_slot, 1)
            link(dve.tensor_tensor(pairs, by_other(rank_b), by_bucket(iota_b), ALU.is_equal))
            link(dve.tensor_tensor(pairs, pairs, by_other(iota_b), ALU.mult))
            link(dve.tensor_reduce(order_f, pairs, AX, ALU.add))
            link(dve.tensor_copy(order_of[0:1, :], order_f[0:1, 0:NT]))
            bf, cn = bucket_f[0:1, :], chunk_no[0:1, :]
            link(dve.tensor_scalar(bf, cn, first_b[0:1, NT:NB], order_f[0:1, NT - 1:NT], ALU.is_ge, ALU.mult))
            with dve.Fori(1, NT) as b:
                link.enter(b - 1, 3)
                dve.tensor_scalar(from_first, cn, first_b[0:1, bass.ds(b, 1)], iota_b[0:1, bass.ds(b, 1)],
                                  ALU.is_ge, ALU.mult)
                link(dve.tensor_scalar(from_end, cn, end_b[0:1, bass.ds(b, 1)], iota_b[0:1, bass.ds(b, 1)],
                                       ALU.is_ge, ALU.mult))
                link(dve.tensor_tensor(bf, bf, from_first, ALU.add))
                link(dve.tensor_tensor(bf, bf, from_end, ALU.subtract))
                link.leave(NT - 1)
            link(dve.tensor_copy(bucket_of[0:1, :], bf))

            def evacuate(ph, take):
                with dve.Fori(0, TI) as i:
                    for j in range(TU):
                        dve.wait_ge(s_prod[ph], 1 + TU * i + j + 1)
                        take(i, j).then_inc(s_evac[ph], 1)
                dve.wait_ge(s_evac[ph], 1 + NT)

            roots = [0]

            def root(v):
                roots[0] += 1
                dve.sem_inc(s_var, 1)
                dve.wait_ge(s_root, roots[0])
                link(dve.reciprocal(v, v))

            def batch_norm(k, gamma, beta):
                link(dve.tensor_scalar(Y3[:, NT - 1, :], Y3[:, NT - 1, :], pmask, None, ALU.mult))
                dve.sem_inc(s_y, 1)
                dve.wait_ge(s_sum, 2 * k + 1)
                link(dve.tensor_scalar(mean_b, ps[:, 4, 0:D], 1.0 / N, None, ALU.mult))
                link(dve.tensor_tensor(Y3, Y3, over_tiles(mean_b), ALU.subtract))
                link(dve.tensor_scalar(Y3[:, NT - 1, :], Y3[:, NT - 1, :], pmask, None, ALU.mult))
                dve.sem_inc(s_dev, 1)
                dve.wait_ge(s_sum, 2 * k + 2)
                link(dve.tensor_scalar(scale_b, ps[:, 5, 0:D], 1.0 / N, EPS, ALU.mult, ALU.add))
                root(scale_b)
                link(dve.tensor_tensor(scale_b, scale_b, gamma, ALU.mult))
                link(dve.tensor_tensor(Y3, Y3, over_tiles(scale_b), ALU.mult))
                link(dve.tensor_tensor(Y3, Y3, over_tiles(beta), ALU.add))

            def layer_norm(v):
                with dve.Fori(0, TI) as i:
                    link.enter(i, 1)
                    for j in range(TU):
                        ins = dve.bn_stats(tile_at(stats, TU * i + j, 6), tile_at(v, TU * i + j))
                    link(ins)
                    link.leave(TI)
                mean_e, sq_e, mean_o, sq_o = (stats[:, :, n] for n in (1, 2, 4, 5))
                mean, var = mv[:, :, 0], mv[:, :, 1]
                link(dve.tensor_tensor(mean, mean_e, mean_o, ALU.add))
                link(dve.tensor_tensor(mean_e, mean_e, mean_o, ALU.subtract))
                link(dve.tensor_scalar(mean, mean, 0.5, None, ALU.mult))
                link(dve.tensor_tensor(var, sq_e, sq_o, ALU.add))
                link(dve.tensor_tensor(mean_e, mean_e, mean_e, ALU.mult))
                link(dve.scalar_tensor_tensor(var, mean_e, D / 4.0, var, ALU.mult, ALU.add))
                link(dve.tensor_scalar(var, var, 1.0 / D, EPS, ALU.mult, ALU.add))
                root(mv[:, :, 1])
                with dve.Fori(0, TI) as i:
                    link.enter(i, 1)
                    for j in range(TU):
                        t = TU * i + j
                        ins = dve.tensor_scalar(tile_at(v, t), tile_at(v, t), mv[:, bass.ds(t, 1), 0],
                                                mv[:, bass.ds(t, 1), 1], ALU.subtract, ALU.mult)
                    link(ins)
                    link.leave(TI)

            def sums_trip(order, i, with_types=False, beside=None):
                def one_hot(j):
                    c = NCH * order + U * i + j
                    dve.wait_ge(s_mm, U + c - OHS + 1)
                    if with_types:
                        dve.tensor_scalar(g[:, j, D:D + R2], col[:, 0:R2], edges_f[:, 3, bass.ds(U * i + j, 1)],
                                          None, ALU.is_equal)
                    dve.tensor_scalar(oh[:, j % OHS, :], col[:, :], edges_f[:, 2, bass.ds(U * i + j, 1)],
                                      None, ALU.is_equal).then_inc(s_oh, 1)

                buckets = buckets_of(mybir.EngineType.DVE, i)
                one_hot(0)
                one_hot(1)
                for j in range(U):
                    if j + 2 < U:
                        one_hot(j + 2)
                    c = NCH * order + U * i + j
                    t = buckets[j]
                    dve.wait_ge(s_mm, U + c + 1)
                    dve.wait_ge(s_add, U + c)
                    if with_types:
                        dve.tensor_tensor(tile_at(counts, t, R2), tile_at(counts, t, R2),
                                          ps[:, j % BANKS, D:D + R2], ALU.add)
                    dve.tensor_tensor(tile_at(A, t), tile_at(A, t), ps[:, j % BANKS, 0:D], ALU.add)\
                        .then_inc(s_add, 1)
                    if beside:
                        beside(j)

            def sums(order):
                with dve.Fori(0, CI) as i:
                    sums_trip(order, i)
                dve.wait_ge(s_add, U + NCH * (order + 1))

            dve.wait_ge(s_rows0, 16 * 7)
            evacuate(0, lambda i, j: dve.tensor_tensor(tile_at(Y3, TU * i + j), ps[:, j % 2, 0:D], B1, ALU.add))
            batch_norm(0, G1, BETA1)
            dve.sem_inc(s_h, 1)

            def take1(i, j):
                dve.tensor_tensor(tile_at(A, TU * i + j), ps[:, 2 + j % 2, 0:D], BR, ALU.add)
                dve.wait_ge(s_out0[j % 2], 16 * (1 + ((TU + 1) // 2 if j % 2 == 0 else TU // 2) * i + j // 2))
                return dve.tensor_copy(out0[:, j % 2, :], ps[:, j % 2, 0:D])

            evacuate(1, take1)
            for b in range(2):
                dve.wait_ge(s_out0[b], 16 * (1 + out_uses[b]))
            dve.wait_ge(s_planes, 4)
            sums(0)
            evacuate(2, lambda i, j: dve.tensor_tensor(tile_at(Y3, TU * i + j), ps[:, j % 2, 0:D], B2, ALU.add))
            batch_norm(1, G2, BETA2)
            link(dve.scalar_tensor_tensor(X[:, :, :], X[:, :, :], 2.0, Y3, ALU.mult, ALU.add))
            layer_norm(X)
            dve.sem_inc(s_x, 1)

            dve.wait_ge(s_rel_out[1], 16)
            def take_rel(i, j):
                for q in (0, 2):
                    dve.wait_ge(s_rel_mm, 4 * (TU * i + j) + q + 1)
                    if q == 0:
                        dve.wait_ge(s_rel_out[j % 2], 16 * (
                            1 + ((TU + 1) // 2 if j % 2 == 0 else TU // 2) * i + j // 2))
                    dve.tensor_copy(rel_out[:, j % 2, 2 * q:2 * q + 2, :].rearrange("p r d -> p (r d)"),
                                    ps[:, q, :]).then_inc(s_rel_dve, 1)
                dve.wait_ge(s_prod[3], 1 + TU * i + j + 1)
                return dve.tensor_tensor(tile_at(A, TU * i + j), ps[:, 4, 0:D], bias1[:, 0, :], ALU.add)

            with dve.Fori(0, TI) as i:
                for j in range(TU):
                    take_rel(i, j).then_inc(s_evac[3], 1)
            dve.wait_ge(s_evac[3], 1 + NT)
            for layer in range(1, L1):
                def take_root(t):
                    bucket = bucket_by_size(mybir.EngineType.DVE, t)
                    dve.wait_ge(s_prod[3 + layer], 1 + t + 1)
                    dve.tensor_tensor(tile_at(A, bucket), ps[:, 6, 0:D], bias1[:, layer, :], ALU.add)\
                        .then_inc(s_evac[3 + layer], 1)

                def trip(i, t):
                    sums_trip(layer, i)
                    if t is not None:
                        take_root(t)

                beside_sweep(dve, trip, take_root)
                dve.wait_ge(s_evac[3 + layer], 1 + NT)
            sums(L1)
            link(dve.scalar_tensor_tensor(X[:, :, :], A2, 0.0, X[:, :, :], ALU.max, ALU.add))
            layer_norm(X)
            link(dve.memset(A2, 0.0))
            link(dve.memset(counts, 0.0))
            link(dve.memset(cstage[:, R2:RB], 1.0))
            link(dve.memset(rel_gates, 0.0))
            dve.sem_inc(s_x, 1)
            steps_t, steps_u = 7, 4

            def gru_steps(j, t, u, bt, bu):
                if u is not None and j == 0:
                    link(dve.bn_aggr(mv1, stats1))
                    dve.tensor_scalar(mv1[:, 1:2], mv1[:, 1:2], EPS, None, ALU.add).then_inc(s_var1, 1)
                if u is not None and j == 2:
                    dve.wait_ge(s_root1, u + 1)
                    link(dve.reciprocal(mv1[:, 1:2], mv1[:, 1:2]))
                    dve.tensor_scalar(tile_at(X, bu), tile_at(X, bu), mv1[:, 0:1], mv1[:, 1:2],
                                      ALU.subtract, ALU.mult).then_inc(s_norm, 1)
                if u is not None and j == 10:
                    features = ps[:, 7, D:2 * D]
                    dve.wait_ge(s_prod[7], 1 + u + 1)
                    dve.tensor_scalar(tile_at(A, bu), features, 1.0, None, ALU.mult)
                    link(dve.tensor_tensor(att_tmp.rearrange("p (s d) -> p s d", s=2),
                                           features.rearrange("p (o d) -> p o d", o=1).broadcast_to([P, 2, D]),
                                           att_st, ALU.mult))
                    dve.sem_inc(s_evac[7], 1)
                    link(dve.tensor_reduce(tile_at(node_l, bu, 2 * H), att_tmp.rearrange("p (h f) -> p h f", f=F),
                                           AX, ALU.add))
                    dve.tensor_scalar(A[:, bass.ds(bu, 1), D:W3].rearrange("p o h -> p (o h)"), tile_at(node_l, bu, H),
                                      1.0, None, ALU.mult).then_inc(s_att_row, 1)
                if t is not None and j == 12:
                    dve.wait_ge(s_prod[6], 1 + t + 1)
                    link(dve.tensor_tensor(hn, ps[:, 5, D:2 * D], b_hn, ALU.add))
                    dve.wait_ge(s_gates, 1 + t + 1)
                    link(dve.tensor_tensor(hn, hn, gates[:, 0:D], ALU.mult))
                    dve.tensor_tensor(inn, ps[:, 5, 0:D], hn, ALU.add).then_inc(s_cand, 1)
                if t is not None and j == 14:
                    dve.wait_ge(s_tanh, t + 1)
                    link(dve.tensor_tensor(hn, tile_at(X, bt), inn, ALU.subtract))
                    link(dve.tensor_tensor(hn, hn, gates[:, D:2 * D], ALU.mult))
                    link(dve.tensor_tensor(hn, hn, inn, ALU.add))
                    link(dve.tensor_tensor(tile_at(X, bt), tile_at(X, bt), hn, ALU.add))
                if t is not None and j == 15:
                    link(dve.bn_stats(stats1, tile_at(X, bt)))

            def gru_buckets(t, u):
                return [None if v is None else bucket_by_size(mybir.EngineType.DVE, v) for v in (t, u)]

            def gru_trip(i, t, u):
                bt, bu = gru_buckets(t, u)
                if u is not None:
                    link.enter(i - READY - 1, steps_t + steps_u)
                sums_trip(4, i, True, lambda j: gru_steps(j, t, u, bt, bu))
                if u is not None:
                    link.leave(CI - READY - 1)

            def gru_hook(j, t, u):
                if j == 0:
                    tail[:] = gru_buckets(t, u)
                gru_steps(j, t, u, *tail)

            tail = []
            dve.wait_ge(s_w2, 96)
            dve.wait_ge(s_w3, 96)
            beside_gru(dve, gru_trip, gru_hook)
            dve.wait_ge(s_add, U + NCH * 5)
            dve.wait_ge(s_att_row, NT)
            dve.sem_inc(s_logit, 1)
            link(dve.tensor_copy(max_l, src_l))
            def first_pass(i, due, steps):
                buckets = lagged_buckets(mybir.EngineType.DVE, i, 5)
                for k in range(steps):
                    if due(k, 0):
                        c = U * i + k
                        dve.wait_ge(s_spread, U + c - RING2 + 1)
                        dve.tensor_scalar(miss[:, k % RING2, :], col[:, :], edges_f[:, 2, bass.ds(c, 1)], -1.0,
                                          ALU.is_equal, ALU.add).then_inc(s_miss, 1)
                    if due(k, 1):
                        c, j = U * i + k - 1, (k - 1) % U
                        dve.wait_ge(s_g[j], 16 * (CI * 5 + (i if k >= 1 else i - 1) + 1))
                        dve.wait_ge(s_spread, U + c - RING + 1)
                        dve.tensor_scalar(diag[:, j % RING, H - 1, :], ident[:, :], g[:, j, H - 1:H], None, ALU.mult)\
                            .then_inc(s_diag_dve, 1)
                    if due(k, 4):
                        c, j = U * i + k - 4, (k - 4) % U
                        dve.wait_ge(s_spread, U + c + 1)
                        dve.wait_ge(s_maxed, U + c - RING + 1)
                        dve.tensor_reduce(red[:, j % RING, :], ps[:, j % 8, :].rearrange("p (h e) -> p h e", h=H),
                                          AX, ALU.max).then_inc(s_red, 1)
                    if due(k, 5):
                        c, j = U * i + k - 5, (k - 5) % U
                        t = buckets[k]
                        dve.wait_ge(s_red, U + c + 1)
                        dve.wait_ge(s_maxed, U + c)
                        dve.tensor_tensor(tile_at(max_l, t, H), tile_at(max_l, t, H), red[:, j % RING, :], ALU.max)\
                            .then_inc(s_maxed, 1)

            trips(dve, first_pass)
            dve.wait_ge(s_maxed, U + NCH)

            link(dve.tensor_tensor(max_l, max_l, dst_l, ALU.add))
            link(dve.scalar_tensor_tensor(m_l, max_l, 0.2, max_l, ALU.mult, ALU.max))
            link(dve.tensor_tensor(t_l, src_l, dst_l, ALU.add))
            link(dve.scalar_tensor_tensor(t_l, t_l, 0.2, t_l, ALU.mult, ALU.max))
            link(dve.tensor_tensor(t_l, t_l, m_l, ALU.subtract))
            dve.sem_inc(s_shift, 1)
            dve.wait_ge(s_self, 1)
            dve.wait_ge(s_att_out, 16)
            link(dve.tensor_copy(A[:, :, D:W3], ex_l))
            a4 = A2.rearrange("p t (h f) -> p t h f", h=H)
            link(dve.memset(g[:, :, W3:W3 + H], 0.0))

            def by_head(v):
                return v.rearrange("p t (h o) -> p t h o", o=1).broadcast_to([P, NT, H, F])

            link(dve.tensor_tensor(a4, a4, by_head(ex_l), ALU.mult))
            dve.sem_inc(s_acc0, 1)
            def second_pass(i, due, steps):
                buckets = lagged_buckets(mybir.EngineType.DVE, i, 10)
                for k in range(steps):
                    if due(k, 0):
                        c = U * i + k
                        dve.wait_ge(s_mm3, U + c - U + 1)
                        dve.tensor_scalar(ohb[:, k, :], col[:, :], edges_f[:, 2, bass.ds(c, 1)], None,
                                          ALU.is_equal).then_inc(s_ohb, 1)
                    if due(k, 3):
                        c, j, s = U * i + k - 3, (k - 3) % U, (k - 3) % RING
                        dve.wait_ge(s_g[j], 16 * (CI * 6 + (i if k >= 3 else i - 1) + 1))
                        dve.wait_ge(s_dm, U + c + 1)
                        dve.tensor_tensor(lg[:, s, 0:2 * H], ps[:, 6 + s % 2, 0:2 * H], g[:, j, D:D + 2 * H], ALU.add)\
                            .then_inc(s_l0, 1)
                    if due(k, 4):
                        c, s = U * i + k - 4, (k - 4) % RING
                        dve.wait_ge(s_l0, U + c + 1)
                        dve.scalar_tensor_tensor(lg[:, s, 2 * H:3 * H], lg[:, s, 0:H], 0.2, lg[:, s, 0:H],
                                                 ALU.mult, ALU.max).then_inc(s_l1, 1)
                    if due(k, 5):
                        c, s = U * i + k - 5, (k - 5) % RING
                        dve.wait_ge(s_l1, c + 1)
                        dve.wait_ge(s_ex, U + c - RING + 1)
                        dve.tensor_tensor(lg[:, s, 3 * H:4 * H], lg[:, s, 2 * H:3 * H], lg[:, s, H:2 * H],
                                          ALU.subtract).then_inc(s_e, 1)
                    if due(k, 8):
                        c, j, r = U * i + k - 8, (k - 8) % U, (k - 8) % RING2
                        dve.wait_ge(s_ex, U + c + 1)
                        ex = wrow[:, r, D + HA:W3].rearrange("p (h o) -> p h o", o=1).broadcast_to([P, H - HA, F])
                        dve.tensor_tensor(wrow[:, r, HA * F:D].rearrange("p (h f) -> p h f", f=F),
                                          g[:, j, HA * F:D].rearrange("p (h f) -> p h f", f=F), ex, ALU.mult)\
                            .then_inc(s_wr, 1)
                    if due(k, 10):
                        c, j, t = U * i + k - 10, (k - 10) % U, buckets[k]
                        dve.wait_ge(s_mm3, U + c + 1)
                        dve.wait_ge(s_add3, U + c)
                        dve.tensor_tensor(tile_at(A, t, W3), tile_at(A, t, W3), ps[:, j % BANKS, 0:W3], ALU.add)\
                            .then_inc(s_add3, 1)

            trips(dve, second_pass)
            dve.wait_ge(s_add3, U + NCH)
            link(dve.tensor_scalar(A[:, :, D:W3], A[:, :, D:W3], 1e-16, None, ALU.add))
            link(dve.reciprocal(ex_l, A[:, :, D:W3]))
            link(dve.tensor_tensor(a4, a4, by_head(ex_l), ALU.mult))
            link(dve.tensor_tensor(A2, A2, over_tiles(bias3), ALU.add))
            link(dve.tensor_tensor(A2, A2, X[:, :, :], ALU.add))
            layer_norm(A2)
            link(dve.tensor_tensor(A2, A2, over_tiles(gamma3), ALU.mult))
            link(dve.tensor_tensor(A2, A2, over_tiles(beta3), ALU.add))
            link(dve.scalar_tensor_tensor(X[:, :, :], A2, 0.0, X[:, :, :], ALU.max, ALU.add))
            layer_norm(X)
            dve.sem_inc(s_x, 1)


_INS = ["x", "src", "dst", "edge_type_16", "edge_type_8"] + [f"L0_gnn_{n}" for n in (
    "w1", "b1", "g1", "beta1", "wr", "br", "wroot", "w2", "b2", "g2", "beta2")] + [
    "L1_gnn_W_rel", "L1_gnn_W_root", "L1_gnn_bias"] + [f"L2_gnn_{n}" for n in (
        "relvectors", "w_ih", "w_hh", "b_ih", "b_hh")] + [f"L3_gnn_{n}" for n in (
            "W", "att_src", "att_dst", "bias", "ln_gamma", "ln_beta")]


def kernel(**inputs):
    import numpy as np
    import concourse.bacc as bacc
    from concourse.bass_utils import run_bass_kernel_spmd

    nc = bacc.Bacc("TRN2", target_bir_lowering=False, num_devices=1)
    arrays, args = {}, {}
    for name in _INS:
        v = np.ascontiguousarray(inputs[name])
        arrays[f"in_{name}"] = v
        args[name] = nc.dram_tensor(f"in_{name}", v.shape, mybir.dt.from_np(v.dtype), kind="ExternalInput").ap()
    out = nc.dram_tensor("out", (N, D), F32, kind="ExternalOutput").ap()
    program(nc, args, out)
    r = run_bass_kernel_spmd(nc, [arrays], core_ids=[0])
    return r.results[0]["out"]
```

```python
from contextlib import ExitStack

import concourse.bass as bass
from concourse import mybir

F32 = mybir.dt.float32
BF16 = mybir.dt.bfloat16
I32 = mybir.dt.int32
ALU = mybir.AluOpType
ACT = mybir.ActivationFunctionType
AX = mybir.AxisListType.X

P = 128
N, D, E = 6250, 256, 100000
NT = -(-N // P)
NP = NT * P
LAST = N - (NT - 1) * P
EC = -(-E // P)
ELAST = E - (P - 1) * EC
TU = 7
TI = NT // TU
U = 16
HALF = U // 2
MAXCH = (P * EC + (NT + 1) * (P - 1)) // P
CI = -(-MAXCH // U)
NCH = CI * U
NB = NT + 1
SU = 16
SI = EC // SU
SREST = EC - SI * SU
R1, L1 = 8, 3
R2 = 16
RB = R2 + 2
H, F = 4, 64
G3 = 3 * D
KD = D // P
W3 = D + H
EPS = 1e-5
BIG = float(2 ** 100)
BANKS = 4
OHS = 8
AHEAD = 6
RING = 4
RING2 = 8
LAGS = 10
HA = 2
NPH = 8
READY = 4
assert NT == TU * TI and NCH == U * CI
assert all(U * min(t + READY, CI) * NT >= (t + 1) * NCH for t in range(NT)) and CI - READY <= NT


class Link:

    def __init__(self, eng, sem):
        self.eng, self.sem, self.base, self.n = eng, sem, 0, 0

    def __call__(self, ins):
        self.n += 1
        ins.then_inc(self.sem, 1)
        self.eng.wait_ge(self.sem, self.base + self.n)

    def begin(self, ins):
        self.n += 1
        ins.then_inc(self.sem, 1)

    def ended(self, but=0):
        self.eng.wait_ge(self.sem, self.base + self.n - but)

    def enter(self, i, per_trip):
        self.outer, self.per_trip = self.base + self.n, per_trip
        self.base, self.n = self.outer + per_trip * i, 0

    def leave(self, trips):
        assert self.n == self.per_trip, self.n
        self.base, self.n = self.outer + self.per_trip * trips, 0


def program(nc, a, out):
    ctx = ExitStack()
    with ctx:
        def sb(name, shape, dt=F32):
            return ctx.enter_context(nc.sbuf_tensor(name, shape, dt))

        def sem(name):
            return ctx.enter_context(nc.semaphore(name))

        def dram(name, shape, dt=F32):
            return nc.dram_tensor(name, shape, dt, kind="Internal").ap()

        slots_d = dram("slots_d", [P * NCH, 4], I32)
        rows_d = dram("rows_d", [NP, D])
        rel_d = [dram(f"rel_d{k}", [R1 * NP, D]) for k in range(2)]
        att_d = dram("att_d", [NP, W3])
        src_logit_d = dram("src_logit_d", [NP, H])

        X = sb("X", [P, NT, D])
        A = sb("A", [P, NT, D + R2])
        Y = sb("Y", [P, NT * D])
        Y3 = Y[:, :].rearrange("p (t d) -> p t d", d=D)
        edges = sb("edges", [P, 4, NCH], I32)
        edges_f = edges[:, :, :].bitcast(F32)
        blank = edges[:, :, :].rearrange("p w c -> p (w c)").rearrange("p (c w) -> p c w", w=4)
        g = sb("g", [P, U, D + R2])
        gflat = g[:, :, :].rearrange("p u d -> p (u d)")
        bucket_of = sb("bucket_of", [1, NCH], I32)
        order_of = sb("order_of", [1, NT], I32)
        wt = sb("wt", [P, 4, KD, D])
        rows0 = sb("rows0", [P, 7, D])
        col = sb("col", [P, P])
        ident = sb("ident", [P, P])
        ones = sb("ones", [P, P])
        big_ident = sb("big_ident", [P, H, P], BF16)
        stage = sb("stage", [P, 2, D])
        turned = sb("turned", [P, 2, D])
        oh = sb("oh", [P, OHS // 2, P])
        idx = sb("idx", [P, U], I32)
        small = sb("small", [P, 64])
        ps = ctx.enter_context(nc.psum_tensor("ps", [P, 8, 512], F32))

        aflat = A[:, :, :].rearrange("p t d -> p (t d)")

        def tmp(k, dt=F32):
            v = aflat[:, k * EC:(k + 1) * EC]
            return v if dt == F32 else v.bitcast(dt)

        payload = gflat[:, 0:4 * EC].rearrange("p (e w) -> p e w", w=4).bitcast(I32)
        payload_f = gflat[:, 0:4 * EC].rearrange("p (e w) -> p e w", w=4)
        loaded = gflat[:, 0:4 * NCH].rearrange("p (c w) -> p c w", w=4).bitcast(I32)
        slot_row = gflat[:, 4 * EC:5 * EC].bitcast(I32)
        at0 = 5 * EC
        sc_idx = gflat[:, at0:at0 + SU].bitcast(I32)
        sc_pay = gflat[:, at0 + SU:at0 + 5 * SU].rearrange("p (u w) -> p u w", w=4).bitcast(I32)
        iota_b = aflat[:, 10 * EC:10 * EC + NB]
        cnt_b, before_b, tot_b, nch_b, end_b, base_b, first_b, key_b, rank_b, order_f = (
            aflat[:, 10 * EC + 64 * k:10 * EC + 64 * k + NB] for k in range(1, 11))
        upper = aflat[:, 10 * EC + 704:10 * EC + 704 + P]
        chunk_no = aflat[:, 12 * EC:12 * EC + NCH]
        bucket_f = aflat[:, 13 * EC + 64:13 * EC + 64 + NCH]
        pairs = aflat[:, 0:NB * NB].rearrange("p (b c) -> p b c", b=NB)
        from_first, from_end = (aflat[0:1, k * NCH:(k + 1) * NCH] for k in range(2))
        pmask = small[:, 60:61]
        prow = small[:, 61:62]

        nat0 = Y[:, 0:4 * KD * D].rearrange("p (w b d) -> p w b d", w=4, b=KD)
        wrel = [Y[:, b * KD * R1 * D:(b + 1) * KD * R1 * D].rearrange(
            "p (k r d) -> p k r d", k=KD, r=R1) for b in range(2)]
        o1 = 2 * KD * R1 * D
        wroot1 = Y[:, o1:o1 + L1 * KD * D].rearrange("p (l k d) -> p l k d", l=L1, k=KD)
        bias1 = Y[:, o1 + L1 * KD * D:o1 + L1 * KD * D + L1 * D].rearrange("p (l d) -> p l d", l=L1)
        rel_out = gflat[:, 0:2 * R1 * D].rearrange("p (s r d) -> p s r d", s=2, r=R1)
        quarter = wt[:, :, :, :].rearrange("p w k d -> p w (k d)")
        nb2 = G3 // P
        nat2 = Y[:, 0:2 * nb2 * D].rearrange("p (w b d) -> p w b d", w=2, b=nb2)
        o2 = 2 * nb2 * D
        wt2 = Y[:, o2:o2 + 2 * KD * G3].rearrange("p (w k d) -> p w k d", w=2, k=KD)
        o2 += 2 * KD * G3
        b_hn = Y[:, o2:o2 + D]
        o2 += D
        relvec = Y[0:R2, o2:o2 + D]
        o2 += D
        cstage = Y[:, o2:o2 + RB]
        o2 += RB
        cturned = Y[0:RB, o2:o2 + P]
        o2 += P
        stage2 = Y[:, o2:o2 + D]
        o2 += D
        turned2 = Y[:, o2:o2 + D]
        o2 += D
        relvec_t = Y[:, o2:o2 + KD * R2].rearrange("p (k r) -> p k r", k=KD)
        o2 += KD * R2
        rel_gates = Y[0:RB, o2:o2 + G3]
        o2 += G3
        rflat = rows0[:, :, :].rearrange("p k d -> p (k d)")
        gates, hn, inn = rflat[:, 2 * D:4 * D], rflat[:, 4 * D:5 * D], rflat[:, 5 * D:6 * D]
        stats1, mv1 = small[:, 0:6], small[:, 8:10]
        assert o2 <= NT * D
        w3 = Y[:, 0:KD * D].rearrange("p (k d) -> p k d", k=KD)
        o3 = KD * D
        att_st = Y[:, o3:o3 + 2 * D].rearrange("p (s d) -> p s d", s=2)
        o3 += 2 * D
        bias3, gamma3, beta3 = (Y[:, o3 + k * D:o3 + (k + 1) * D] for k in range(3))
        o3 += 3 * D
        max_l, t_l, ex_l = (
            Y[:, o3 + k * NT * H:o3 + (k + 1) * NT * H].rearrange("p (t h) -> p t h", h=H) for k in range(3))
        o3 += 3 * NT * H
        node_l = Y[:, o3:o3 + NT * 3 * H].rearrange("p (t h) -> p t h", h=3 * H)
        o3 += NT * 3 * H
        src_l, dst_l, m_l = (node_l[:, :, k * H:(k + 1) * H] for k in range(3))
        assert o3 <= 2 * nb2 * D
        att_tmp = wt[:, 3].rearrange("p k d -> p (k d)")
        diag = Y[:, o3:o3 + RING * H * P].rearrange("p (s h e) -> p s h e", s=RING, h=H)
        o3 += RING * H * P
        miss = Y[:, o3:o3 + RING2 * P // 2].bitcast(BF16).rearrange("p (s n) -> p s n", s=RING2)
        o3 += RING2 * P // 2
        red = Y[:, o3:o3 + RING * H].rearrange("p (s h) -> p s h", s=RING)
        o3 += RING * H
        ohT = Y[:, o3:o3 + RING * P].rearrange("p (s e) -> p s e", s=RING)
        o3 += RING * P
        lg = Y[:, o3:o3 + RING * 4 * H].rearrange("p (s h) -> p s h", s=RING)
        o3 += RING * 4 * H
        wrow = Y[:, o3:o3 + RING2 * W3].rearrange("p (s d) -> p s d", s=RING2)
        o3 += RING2 * W3
        ohb = Y[:, o3:o3 + U * P].rearrange("p (s n) -> p s n", s=U)
        o3 += U * P
        assert o3 <= NT * D
        sflat = stage[:, :, :].rearrange("p s d -> p (s d)")
        stats = sflat[:, 0:NT * 6].rearrange("p (t s) -> p t s", s=6)
        mv = sflat[:, NT * 6:NT * 8].rearrange("p (t s) -> p t s", s=2)
        mean_b, scale_b = stage[:, 0, :], stage[:, 1, :]
        out0 = oh[:, :, :].rearrange("p (s q) n -> p s (q n)", s=2)

        s_dve = sem("s_dve")
        s_pool = sem("s_pool")
        s_const = sem("s_const")
        s_ident = sem("s_ident")
        s_edge_in = sem("s_edge_in")
        s_edge_pad = sem("s_edge_pad")
        s_x_pad = sem("s_x_pad")
        s_w0 = sem("s_w0")
        s_rows0 = sem("s_rows0")
        s_turn_w = sem("s_turn_w")
        s_wt = sem("s_wt")
        s_cnt = sem("s_cnt")
        s_tot = sem("s_tot")
        s_slot = sem("s_slot")
        s_blank = sem("s_blank")
        s_blank_d = sem("s_blank_d")
        s_sc = [sem(f"s_sc{k}") for k in range(2)]
        s_scat = sem("s_scat")
        s_edges = sem("s_edges")
        s_planes = sem("s_planes")
        s_stage = [sem(f"s_stage{k}") for k in range(NPH)]
        s_turn = [sem(f"s_turn{k}") for k in range(NPH)]
        s_turned = [sem(f"s_turned{k}") for k in range(NPH)]
        s_prod = [sem(f"s_prod{k}") for k in range(NPH)]
        s_evac = [sem(f"s_evac{k}") for k in range(NPH)]
        s_y = sem("s_y")
        s_sum = sem("s_sum")
        s_dev = sem("s_dev")
        s_sq = sem("s_sq")
        s_sq_used = sem("s_sq_used")
        s_h = sem("s_h")
        s_out0 = [sem(f"s_out0{k}") for k in range(2)]
        s_table = sem("s_table")
        s_var = sem("s_var")
        s_root = sem("s_root")
        s_acc0 = sem("s_acc0")
        s_x = sem("s_x")
        s_idx = [sem(f"s_idx{k}") for k in range(2)]
        s_g = [sem(f"s_g{k}") for k in range(U)]
        s_issue = sem("s_issue")
        s_oh = sem("s_oh")
        s_mm = sem("s_mm")
        s_add = sem("s_add")
        s_wrel = [sem(f"s_wrel{k}") for k in range(L1)]
        s_rel_mm = sem("s_rel_mm")
        s_rel_dve = sem("s_rel_dve")
        s_rel_act = sem("s_rel_act")
        s_rel_out = [sem(f"s_rel_out{k}") for k in range(2)]
        s_quarter_mm = sem("s_quarter_mm")
        s_quarter = sem("s_quarter")
        s_quarter_out = [sem(f"s_quarter_out{k}") for k in range(4)]
        s_w2 = sem("s_w2")
        s_turn_w2 = sem("s_turn_w2")
        s_gru_w = sem("s_gru_w")
        s_gates = sem("s_gates")
        s_cand = sem("s_cand")
        s_tanh = sem("s_tanh")
        s_stat_begun = sem("s_stat_begun")
        s_var1 = sem("s_var1")
        s_root1 = sem("s_root1")
        s_norm = sem("s_norm")
        s_w3 = sem("s_w3")
        s_att_row = sem("s_att_row")
        s_att_out = sem("s_att_out")
        s_logit = sem("s_logit")
        s_diag = sem("s_diag")
        s_diag_dve = sem("s_diag_dve")
        s_miss = sem("s_miss")
        s_spread = sem("s_spread")
        s_red = sem("s_red")
        s_maxed = sem("s_maxed")
        s_shift = sem("s_shift")
        s_self = sem("s_self")
        s_ohb = sem("s_ohb")
        s_oht = sem("s_oht")
        s_ohts = sem("s_ohts")
        s_dm = sem("s_dm")
        s_l0 = sem("s_l0")
        s_l1 = sem("s_l1")
        s_e = sem("s_e")
        s_ex = sem("s_ex")
        s_wr = sem("s_wr")
        s_wr_act = sem("s_wr_act")
        s_mm3 = sem("s_mm3")
        s_add3 = sem("s_add3")
        s_out = sem("s_out")

        block = ctx.enter_context(nc.Block())
        edge_in = [a["dst"], a["src"], a["edge_type_8"], a["edge_type_16"]]
        vec0 = ["L0_gnn_b1", "L0_gnn_g1", "L0_gnn_beta1", "L0_gnn_br", "L0_gnn_b2", "L0_gnn_g2", "L0_gnn_beta2"]
        mat0 = ["L0_gnn_w1", "L0_gnn_wr", "L0_gnn_wroot", "L0_gnn_w2"]
        B1, G1, BETA1, BR, B2, G2, BETA2 = (rows0[:, k, :] for k in range(7))
        A2 = A[:, :, 0:D]

        def one_hot_at(k):
            return oh[:, k, :] if k < OHS // 2 else rows0[:, (k - OHS // 2) // 2, (k % 2) * P:(k % 2 + 1) * P]

        def all_rows(v):
            return v.rearrange("(o d) -> o d", o=1).broadcast_to([P, v.shape[0]])

        def over_tiles(v):
            return v.rearrange("p (o d) -> p o d", o=1).broadcast_to([P, NT, D])

        def tile_at(v, t, width=D):
            return v[:, bass.ds(t, 1), 0:width].rearrange("p o d -> p (o d)")

        def node_rows(table):
            return table.rearrange("(t p) d -> p t d", p=P)

        def before(j):
            return j if j == 0 else j - 1

        out_uses = [TI * ((TU + 1) // 2), TI * (TU // 2)]

        def buckets_of(engine, i):
            _, values = nc.values_load_multi_w_load_instructions(
                bucket_of[0:1, bass.ds(U * i, U)], engines=(engine,), min_val=0, max_val=NT - 1,
                skip_runtime_bounds_check_because="a bucket's number counts which of NT - 1 ends lie before a chunk")
            return values

        def bucket_by_size(engine, t):
            _, values = nc.values_load_multi_w_load_instructions(
                order_of[0:1, bass.ds(t, 1)], engines=(engine,), min_val=0, max_val=NT - 1,
                skip_runtime_bounds_check_because="the buckets' numbers in another order")
            return values[0]

        def beside_sweep(eng, trip, dense):
            with eng.Fori(0, READY) as i:
                trip(i, None, None)
            trip(READY, 0, None)
            with eng.Fori(READY + 1, CI) as i:
                trip(i, i - READY, i - READY - 1)
            for v in range(CI - READY, NT + 1):
                dense(v if v < NT else None, v - 1)

        def beside_gru(eng, trip, hook):
            with eng.Fori(0, READY) as i:
                trip(i, None, None, None)
            trip(READY, 0, None, None)
            trip(READY + 1, 1, 0, None)
            with eng.Fori(READY + 2, CI) as i:
                trip(i, i - READY, i - READY - 1, i - READY - 2)
            for v in range(CI - READY, NT + 2):
                for j in range(U):
                    hook(j, v if v < NT else None, v - 1 if v < NT + 1 else None, v - 2)

        def trips(eng, trip):
            trip(0, lambda k, lag: k >= lag, U)
            with eng.Fori(1, CI) as i:
                trip(i, lambda k, lag: True, U)
            trip(CI, lambda k, lag: k < lag, LAGS)

        def lagged_buckets(engine, i, lag):
            first, last = isinstance(i, int) and i == 0, isinstance(i, int) and i == CI
            at, n = (0, U - lag) if first else (U * i - lag, lag if last else U)
            _, values = nc.values_load_multi_w_load_instructions(
                bucket_of[0:1, bass.ds(at, n)], engines=(engine,), min_val=0, max_val=NT - 1,
                skip_runtime_bounds_check_because="a bucket's number counts which of NT - 1 ends lie before a chunk")
            return (0,) * lag + tuple(values) if first else values

        @block.sync
        def _(sp):
            sp.wait_ge(s_edge_pad, 4)
            for k, v in enumerate(edge_in):
                sp.dma_start(tmp(k, I32)[0:P - 1, :], v[0:(P - 1) * EC].rearrange("(p e) -> p e", e=EC))\
                    .then_inc(s_edge_in, 16)
                sp.dma_start(tmp(k, I32)[P - 1:P, 0:ELAST], v[(P - 1) * EC:E].rearrange("(o e) -> o e", o=1))\
                    .then_inc(s_edge_in, 16)
            for k, n in enumerate(mat0):
                sp.dma_start(nat0[:, k], a[n].rearrange("(b p) d -> p b d", p=P)).then_inc(s_w0, 16)
            for k, n in enumerate(vec0):
                sp.dma_start(rows0[:, k, :], all_rows(a[n])).then_inc(s_rows0, 16)
            sp.wait_ge(s_x_pad, 1)
            sp.dma_start(X[:, 0:NT - 1, :], node_rows(a["x"][0:(NT - 1) * P, :])).then_inc(s_out0[0], 16)
            sp.dma_start(X[0:LAST, NT - 1, :], a["x"][(NT - 1) * P:N, :]).then_inc(s_out0[1], 16)
            sp.wait_ge(s_blank, 1)
            sp.dma_start(slots_d.rearrange("(p c) w -> p c w", p=P), blank).then_inc(s_blank_d, 16)
            with sp.Fori(0, TI) as i:
                for j in range(TU):
                    sp.wait_ge(s_evac[1], 1 + TU * i + j + 1)
                    sp.dma_start(rows_d[bass.ds((TU * i + j) * P, P), :], out0[:, j % 2, :])\
                        .then_inc(s_out0[j % 2], 16)
            def sweep_indices(order, word):
                with sp.Fori(0, CI) as i:
                    for h in range(2):
                        for j in range(HALF * h, HALF * (h + 1)):
                            sp.wait_ge(s_g[j], 16 * (CI * order + i))
                        sp.dma_start(idx[:, HALF * h:HALF * (h + 1)],
                                     edges[:, word, bass.ds(U * i + HALF * h, HALF)]).then_inc(s_idx[h], 16)

            sp.wait_ge(s_planes, 4)
            with sp.Fori(0, CI) as i:
                for h in range(2):
                    sp.wait_ge(s_mm, U * i + HALF * (h + 1))
                    sp.dma_start(idx[:, HALF * h:HALF * (h + 1)],
                                 edges[:, 0, bass.ds(U * i + HALF * h, HALF)]).then_inc(s_idx[h], 16)
            sp.wait_ge(s_x, 1)
            sp.dma_start(wroot1, a["L1_gnn_W_root"].rearrange("l (k p) d -> p l k d", p=P)).then_inc(s_rel_out[0], 16)
            sp.dma_start(bias1, a["L1_gnn_bias"].rearrange("(o l) d -> o l d", o=1).broadcast_to([P, L1, D]))\
                .then_inc(s_rel_out[1], 16)

            def load_wrel(layer):
                for k in range(KD):
                    sp.dma_start(wrel[layer % 2][:, k], a["L1_gnn_W_rel"][layer, :, k * P:(k + 1) * P, :]
                                 .rearrange("r p d -> p r d")).then_inc(s_wrel[layer], 16)

            load_wrel(0)
            load_wrel(1)
            with sp.Fori(0, TI) as i:
                for j in range(TU):
                    done = 2 * (TU * i + j + 1)
                    sp.wait_ge(s_rel_dve, 1 + done)
                    sp.wait_ge(s_rel_act, 1 + done)
                    sp.dma_start(rel_d[0].rearrange("(r n) d -> n r d", r=R1)[bass.ds((TU * i + j) * P, P), :, :],
                                 rel_out[:, j % 2]).then_inc(s_rel_out[j % 2], 16)
            sp.wait_ge(s_prod[3], 1 + NT)
            load_wrel(2)
            for layer in range(L1):
                sweep_indices(1 + layer, 1)
            sp.wait_ge(s_x, 2)
            sp.dma_start(node_rows(rows_d), X[:, :, :]).then_inc(s_table, 16)
            for k, n in enumerate(["L2_gnn_w_ih", "L2_gnn_w_hh"]):
                sp.dma_start(nat2[:, k], a[n].rearrange("(b p) d -> p b d", p=P)).then_inc(s_w2, 16)
            sp.dma_start(rel_gates[R2:R2 + 1, :], a["L2_gnn_b_ih"].rearrange("(o d) -> o d", o=1)).then_inc(s_w2, 16)
            sp.dma_start(rel_gates[R2 + 1:RB, 0:2 * D], a["L2_gnn_b_hh"][0:2 * D].rearrange("(o d) -> o d", o=1))\
                .then_inc(s_w2, 16)
            sp.dma_start(b_hn, all_rows(a["L2_gnn_b_hh"][2 * D:G3])).then_inc(s_w2, 16)
            sp.dma_start(relvec, a["L2_gnn_relvectors"]).then_inc(s_w2, 16)
            sp.wait_ge(s_turn_w2, 2 * KD)
            sp.dma_start(w3, a["L3_gnn_W"].rearrange("(k p) d -> p k d", p=P)).then_inc(s_w3, 16)
            for k, n in enumerate(["L3_gnn_att_src", "L3_gnn_att_dst"]):
                sp.dma_start(att_st[:, k, :], all_rows(a[n].rearrange("h f -> (h f)"))).then_inc(s_w3, 16)
            for v, n in ((bias3, "L3_gnn_bias"), (gamma3, "L3_gnn_ln_gamma"), (beta3, "L3_gnn_ln_beta")):
                sp.dma_start(v, all_rows(a[n])).then_inc(s_w3, 16)
            sweep_indices(4, 0)
            sp.wait_ge(s_logit, 1)
            sp.dma_start(node_rows(src_logit_d), src_l).then_inc(s_table, 16)
            sweep_indices(5, 0)
            sweep_indices(6, 0)
            sp.wait_ge(s_x, 3)
            sp.dma_start(node_rows(out[0:(NT - 1) * P, :]), X[:, 0:NT - 1, :]).then_inc(s_out, 16)
            sp.dma_start(out[(NT - 1) * P:N, :], X[0:LAST, NT - 1, :]).then_inc(s_out, 16)
            sp.wait_ge(s_out, 32)

        @block.gpsimd
        def _(pool):
            link = Link(pool, s_pool)
            pool.memset(tmp(0, I32), NT * P).then_inc(s_edge_pad, 1)
            for k in range(1, 4):
                pool.memset(tmp(k, I32), 0).then_inc(s_edge_pad, 1)
            pool.iota(col[:, :], pattern=[[1, P]], base=0, channel_multiplier=0,
                      allow_small_or_imprecise_dtypes=True).then_inc(s_const, 1)
            pool.iota(prow, pattern=[[1, 1]], base=0, channel_multiplier=1,
                      allow_small_or_imprecise_dtypes=True).then_inc(s_const, 1)
            pool.iota(iota_b, pattern=[[1, NB]], base=0, channel_multiplier=0,
                      allow_small_or_imprecise_dtypes=True).then_inc(s_const, 1)
            pool.iota(chunk_no, pattern=[[1, NCH]], base=0, channel_multiplier=0,
                      allow_small_or_imprecise_dtypes=True).then_inc(s_const, 1)
            pool.memset(ones[:, :], 1.0).then_inc(s_const, 1)
            pool.memset(X[:, NT - 1, :], 0.0).then_inc(s_x_pad, 1)
            link(pool.memset(blank, 0))
            pool.memset(blank.bitcast(F32)[:, :, 2:3], float(P)).then_inc(s_blank, 1)

            pool.wait_ge(s_slot, 1)
            pool.wait_ge(s_blank_d, 16)

            def scatter(k, s):
                pool.indirect_dma_start(
                    out=slots_d, out_offset=bass.IndirectOffsetOnAxis(ap=sc_idx[:, k:k + 1], axis=0),
                    in_=sc_pay[:, k, :], in_offset=None).then_inc(s, 16)

            half = SU // 2

            def stage_edges(at, h):
                link(pool.tensor_copy(sc_idx[:, half * h:half * (h + 1)], slot_row[:, bass.ds(at, half)]))
                link(pool.tensor_copy(sc_pay[:, half * h:half * (h + 1), :], payload[:, bass.ds(at, half), :]))
                pool.sem_inc(s_issue, 1)
                for k in range(half * h, half * (h + 1)):
                    scatter(k, s_sc[h])

            stage_edges(0, 0)
            stage_edges(half, 1)
            with pool.Fori(1, SI) as i:
                link.enter(i - 1, 4)
                for h in range(2):
                    pool.wait_ge(s_sc[h], 16 * half * i)
                    stage_edges(SU * i + half * h, h)
                link.leave(SI - 1)
            for h in range(2):
                pool.wait_ge(s_sc[h], 16 * half * SI)
            link(pool.tensor_copy(sc_idx[:, 0:SREST], slot_row[:, SU * SI:EC]))
            link(pool.tensor_copy(sc_pay[:, 0:SREST, :], payload[:, SU * SI:EC, :]))
            for k in range(SREST):
                scatter(k, s_scat)
            pool.wait_ge(s_scat, 16 * SREST)
            pool.dma_start(loaded, slots_d.rearrange("(p c) w -> p c w", p=P)).then_inc(s_edges, 16)

            def gathers(order, table, width, free, ahead):
                with pool.Fori(0, CI) as i:
                    for j in range(U):
                        if j % HALF == 0:
                            pool.wait_ge(s_idx[j // HALF], 16 * (CI * order + i + 1))
                        pool.wait_ge(free, ahead + U * i + j + 1)
                        pool.sem_inc(s_issue, 1)
                        pool.indirect_dma_start(
                            out=g[:, j, 0:width], out_offset=None, in_=table,
                            in_offset=bass.IndirectOffsetOnAxis(ap=idx[:, j:j + 1], axis=0)).then_inc(s_g[j], 16)

            for b in range(2):
                pool.wait_ge(s_out0[b], 16 * (1 + out_uses[b]))
            gathers(0, rows_d, D, s_mm, 0)
            for b in range(2):
                pool.wait_ge(s_rel_out[b], 16 * (1 + out_uses[b]))
            gathers(1, rel_d[0], D, s_mm, NCH)
            for layer in range(1, L1):
                for q in range(4):
                    pool.wait_ge(s_quarter_out[q], 16 * (1 + NT * layer))
                gathers(1 + layer, rel_d[layer % 2], D, s_mm, NCH * (1 + layer))
            pool.wait_ge(s_table, 16)
            gathers(4, rows_d, D, s_mm, NCH * 4)
            pool.wait_ge(s_table, 32)
            gathers(5, src_logit_d, H, s_spread, 0)
            pool.wait_ge(s_att_out, 16)
            pool.wait_ge(s_spread, U + NCH)
            gathers(6, att_d, W3, s_mm3, 0)

        @block.scalar
        def _(act):
            def copy(o, v):
                return act.activation(o, v, ACT.Copy)

            act.sem_inc(s_ohts, U)
            act.sem_inc(s_ex, U)
            act.sem_inc(s_quarter, 2)
            act.sem_inc(s_gates, 1)
            for s in s_turned + [s_rel_act]:
                act.sem_inc(s, 1)
            for s in s_quarter_out:
                act.sem_inc(s, 16)

            for k in range(4):
                act.wait_ge(s_turn_w, k + 1)
                copy(wt[:, k].rearrange("p k (b o) -> p k b o", b=KD),
                     ps[:, k, :].rearrange("p (b k o) -> p k b o", b=KD, k=KD)).then_inc(s_wt, 1)

            def turn_tiles(ph, staged, extra=None, begin=0):
                def put(i, j):
                    act.wait_ge(s_turn[ph], 1 + TU * i + before(j))
                    staged(j % 2, TU * i + j).then_inc(s_stage[ph], 1)

                with act.Fori(0, TI) as i:
                    put(i, 0)
                    for j in range(TU):
                        if j + 1 < TU:
                            put(i, j + 1)
                        act.wait_ge(s_turn[ph], 1 + TU * i + j + 1)
                        act.wait_ge(s_prod[ph], 1 + TU * i + before(j))
                        copy(turned[:, j % 2, :], ps[:, 6 + j % 2, 0:D]).then_inc(s_turned[ph], 1)
                        if extra:
                            extra(i, j)

            roots = [0]

            def root(v):
                roots[0] += 1
                act.wait_ge(s_var, roots[0])
                act.activation(v, v, ACT.Sqrt).then_inc(s_root, 1)

            def squares(k):
                with act.Fori(0, TI) as i:
                    for j in range(TU):
                        act.wait_ge(s_sq_used, 1 + NT * k + TU * i + before(j))
                        act.activation(turned[:, j % 2, :], tile_at(Y3, TU * i + j), ACT.Square).then_inc(s_sq, 1)

            for b in range(2):
                act.wait_ge(s_out0[b], 16)
            turn_tiles(0, lambda b, t: copy(stage[:, b, :], tile_at(X, t)))
            act.wait_ge(s_dev, 1)
            squares(0)
            root(scale_b)
            act.wait_ge(s_h, 1)
            turn_tiles(1, lambda b, t: copy(stage[:, b, :], tile_at(Y3, t)))
            act.wait_ge(s_edges, 16)
            for w in range(4):
                act.copy(edges[:, w, :], loaded[:, :, w]).then_inc(s_planes, 1)
            def gelu_tile(v):
                bucket = bucket_by_size(mybir.EngineType.Activation, v)
                act.wait_ge(s_turn[2], 1 + v)
                act.activation(stage[:, 0, :], tile_at(A, bucket), ACT.Gelu).then_inc(s_stage[2], 1)
                act.wait_ge(s_turn[2], 1 + v + 1)
                act.wait_ge(s_prod[2], 1 + v)
                copy(turned[:, 0, :], ps[:, 7, 0:D]).then_inc(s_turned[2], 1)

            with act.Fori(READY, CI) as i:
                act.wait_ge(s_add, U + U * i)
                gelu_tile(i - READY)
            act.wait_ge(s_add, U + NCH)
            for v in range(CI - READY, NT):
                gelu_tile(v)
            act.wait_ge(s_dev, 2)
            squares(1)
            root(scale_b)
            root(mv[:, :, 1])

            act.wait_ge(s_x, 1)

            def rel_rows(i, j):
                for q in (1, 3):
                    act.wait_ge(s_rel_mm, 4 * (TU * i + j) + q + 1)
                    if q == 1:
                        act.wait_ge(s_rel_out[j % 2], 16 * (
                            1 + ((TU + 1) // 2 if j % 2 == 0 else TU // 2) * i + j // 2))
                    copy(rel_out[:, j % 2, 2 * q:2 * q + 2, :].rearrange("p r d -> p (r d)"), ps[:, q, :])\
                        .then_inc(s_rel_act, 1)

            turn_tiles(3, lambda b, t: copy(stage[:, b, :], tile_at(X, t)), rel_rows)
            act.wait_ge(s_prod[2], 1 + NT)
            for layer in range(1, L1):
                table = rel_d[layer % 2].rearrange("(r n) d -> n r d", r=R1)

                def rel_tile(v):
                    ph, first = 3 + layer, 4 * (NT * (layer - 1) + v)
                    bucket = bucket_by_size(mybir.EngineType.Activation, v)
                    act.wait_ge(s_turn[ph], 1 + v)
                    act.activation(stage[:, 0, :], tile_at(A, bucket), ACT.Relu).then_inc(s_stage[ph], 1)
                    act.wait_ge(s_turn[ph], 1 + v + 1)
                    act.wait_ge(s_prod[ph], 1 + v)
                    copy(turned[:, 0, :], ps[:, 7, 0:D]).then_inc(s_turned[ph], 1)
                    for q in range(4):
                        act.wait_ge(s_quarter_mm, first + q + 1)
                        act.wait_ge(s_quarter_out[q], 16 * (1 + NT * (layer - 1) + v))
                        copy(quarter[:, q, :], ps[:, 4 + q % 2, :]).then_inc(s_quarter, 1)
                        act.wait_ge(s_quarter, 2 + first + q + 1)
                        act.dma_start(table[bass.ds(bucket * P, P), 2 * q:2 * q + 2, :],
                                      quarter[:, q, :].rearrange("p (r d) -> p r d", r=2)).then_inc(s_quarter_out[q], 16)

                with act.Fori(READY, CI) as i:
                    act.wait_ge(s_add, U + NCH * layer + U * i)
                    rel_tile(i - READY)
                act.wait_ge(s_add, U + NCH * (layer + 1))
                for v in range(CI - READY, NT):
                    rel_tile(v)
            root(mv[:, :, 1])
            for k in range(2):
                for h in range(KD):
                    act.wait_ge(s_turn_w2, KD * k + h + 1)
                    copy(wt2[:, k, h, 0:512], ps[:, 2 * h, :])
                    copy(wt2[:, k, h, 512:G3], ps[:, 2 * h + 1, 0:G3 - 512]).then_inc(s_gru_w, 1)
            act.wait_ge(s_turn_w2, 2 * KD + 1)
            copy(relvec_t, ps[:, 4, 0:KD * R2].rearrange("p (k r) -> p k r", k=KD)).then_inc(s_gru_w, 1)
            act.wait_ge(s_turn_w2, 2 * KD + 2)
            copy(rel_gates[0:R2, 0:512], ps[0:R2, 5, :])
            copy(rel_gates[0:R2, 512:G3], ps[0:R2, 6, 0:G3 - 512]).then_inc(s_gru_w, 1)

            def gru_tile(v, t, u):
                if u is not None:
                    last = bucket_by_size(mybir.EngineType.Activation, u)
                    act.wait_ge(s_norm, u + 1)
                    act.wait_ge(s_turn[7], 1 + u)
                    copy(stage[:, 1, :], tile_at(X, last)).then_inc(s_stage[7], 1)
                if t is not None:
                    act.wait_ge(s_prod[6], 1 + t + 1)
                    act.activation(gates, ps[:, 4, :], ACT.Sigmoid).then_inc(s_gates, 1)
                if u is not None:
                    act.wait_ge(s_turn[7], 1 + u + 1)
                    act.wait_ge(s_prod[7], 1 + u)
                    copy(turned[:, 1, :], ps[:, 7, 0:D]).then_inc(s_turned[7], 1)
                if v is not None:
                    bucket = bucket_by_size(mybir.EngineType.Activation, v)
                    act.wait_ge(s_turn[6], 1 + v)
                    copy(stage[:, 0, :], tile_at(A, bucket))
                    copy(cstage[:, 0:R2], A[:, bass.ds(bucket, 1), D:D + R2].rearrange("p o r -> p (o r)"))
                    copy(stage2, tile_at(X, bucket)).then_inc(s_stage[6], 1)
                if t is not None:
                    act.wait_ge(s_cand, 1 + t + 1)
                    act.activation(inn, inn, ACT.Tanh).then_inc(s_tanh, 1)
                if v is not None:
                    act.wait_ge(s_turn[6], 1 + v + 1)
                    act.wait_ge(s_prod[6], 1 + v)
                    copy(turned[:, 0, :], ps[:, 6, 0:D])
                    copy(turned2, ps[:, 6, D:2 * D])
                    copy(cturned, ps[0:RB, 7, 0:P]).then_inc(s_turned[6], 1)
                if t is not None:
                    act.wait_ge(s_var1, t + 1)
                    act.activation(mv1[:, 1:2], mv1[:, 1:2], ACT.Sqrt).then_inc(s_root1, 1)

            act.wait_ge(s_add, U + NCH * 4 + U * READY)
            gru_tile(0, None, None)
            act.wait_ge(s_add, U + NCH * 4 + U * (READY + 1))
            gru_tile(1, 0, None)
            with act.Fori(READY + 2, CI) as i:
                act.wait_ge(s_add, U + NCH * 4 + U * i)
                gru_tile(i - READY, i - READY - 1, i - READY - 2)
            act.wait_ge(s_add, U + NCH * 5)
            for v in range(CI - READY, NT + 2):
                gru_tile(v if v < NT else None, v - 1 if v < NT + 1 else None, v - 2)

            act.wait_ge(s_logit, 1)
            act.dma_start(node_rows(att_d), A[:, :, 0:W3]).then_inc(s_att_out, 16)
            with act.Fori(0, CI) as i:
                for j in range(U):
                    act.wait_ge(s_g[j], 16 * (CI * 5 + i + 1))
                    act.wait_ge(s_spread, U + U * i + j - RING + 1)
                    for h in range(H - 1):
                        ins = act.activation(diag[:, j % RING, h, :], ident[:, :], ACT.Copy, scale=g[:, j, h:h + 1])
                    ins.then_inc(s_diag, 1)
            act.wait_ge(s_shift, 1)
            act.activation(ex_l, t_l, ACT.Exp).then_inc(s_self, 1)

            def second_pass(i, due, steps):
                for k in range(steps):
                    if due(k, 0):
                        c, s = U * i + k, k % RING
                        act.wait_ge(s_oht, c + 1)
                        act.wait_ge(s_dm, U + c - RING + 1)
                        copy(ohT[:, s, :], ps[:, 4 + k % 2, 0:P]).then_inc(s_ohts, 1)
                    if due(k, 6):
                        c, s, r = U * i + k - 6, (k - 6) % RING, (k - 6) % RING2
                        act.wait_ge(s_e, U + c + 1)
                        act.wait_ge(s_mm3, U + c - RING2 + 1)
                        act.activation(wrow[:, r, D:W3], lg[:, s, 3 * H:4 * H], ACT.Exp).then_inc(s_ex, 1)
                    if due(k, 7):
                        c, j, r = U * i + k - 7, (k - 7) % U, (k - 7) % RING2
                        act.wait_ge(s_ex, U + c + 1)
                        for h in range(HA):
                            ins = act.activation(wrow[:, r, h * F:(h + 1) * F], g[:, j, h * F:(h + 1) * F], ACT.Copy,
                                                 scale=wrow[:, r, D + h:D + h + 1])
                        ins.then_inc(s_wr_act, 1)

            trips(act, second_pass)
            root(mv[:, :, 1])
            root(mv[:, :, 1])

        @block.tensor
        def _(pe):
            pe.sem_inc(s_mm, U)
            pe.sem_inc(s_spread, U)
            pe.sem_inc(s_dm, U)
            pe.sem_inc(s_mm3, U)
            for s in s_turn + s_prod + [s_sq_used]:
                pe.sem_inc(s, 1)

            pe.wait_ge(s_ident, 1)
            pe.wait_ge(s_w0, 64)
            for w in range(4):
                for b in range(KD):
                    for k in range(KD):
                        at = (b * KD + k) * P
                        ins = pe.transpose(ps[:, w, at:at + P], nat0[:, w, b, k * P:(k + 1) * P], ident[:, :])
                ins.then_inc(s_turn_w, 1)

            def turn_tiles(ph, products):
                def turn(i, j):
                    pe.wait_ge(s_stage[ph], TU * i + j + 1)
                    pe.wait_ge(s_turned[ph], 1 + TU * i + before(j))
                    for k in range(KD):
                        ins = pe.transpose(ps[:, 6 + j % 2, k * P:(k + 1) * P], stage[:, j % 2, k * P:(k + 1) * P],
                                           ident[:, :])
                    ins.then_inc(s_turn[ph], 1)

                with pe.Fori(0, TI) as i:
                    turn(i, 0)
                    for j in range(TU):
                        if j + 1 < TU:
                            turn(i, j + 1)
                        pe.wait_ge(s_turned[ph], 1 + TU * i + j + 1)
                        products(i, j)

            def product(o, b, w):
                for k in range(KD):
                    ins = pe.matmul(o, turned[:, b, k * P:(k + 1) * P], w[:, k, :], start=(k == 0), stop=(k == KD - 1))
                return ins

            def one_product(ph, w):
                def products(i, j):
                    pe.wait_ge(s_evac[ph], 1 + TU * i + before(j))
                    product(ps[:, j % 2, 0:D], j % 2, wt[:, w]).then_inc(s_prod[ph], 1)
                turn_tiles(ph, products)

            def sum_nodes(k):
                pe.wait_ge(s_y, k + 1)
                pe.matmul(ps[:, 4, 0:D], ones[:, :], Y3[:, 0, :], start=True, stop=False, skip_group_check=True)
                with pe.Fori(0, (NT - 1) // 8) as i:
                    for j in range(8):
                        ins = pe.matmul(ps[:, 4, 0:D], ones[:, :], tile_at(Y3, 8 * i + j + 1), start=False,
                                        stop=(j == 7), skip_group_check=True)
                pe.drain().then_inc(s_sum, 1)
                pe.wait_ge(s_sq, NT * k + 1)
                pe.matmul(ps[:, 5, 0:D], ones[:, :], turned[:, 0, :], start=True, stop=False,
                          skip_group_check=True).then_inc(s_sq_used, 1)
                for j in range(1, TU):
                    pe.wait_ge(s_sq, NT * k + j + 1)
                    pe.matmul(ps[:, 5, 0:D], ones[:, :], turned[:, j % 2, :], start=False, stop=(j == TU - 1),
                              skip_group_check=True).then_inc(s_sq_used, 1)
                with pe.Fori(1, TI) as i:
                    for j in range(TU):
                        pe.wait_ge(s_sq, NT * k + TU * i + j + 1)
                        pe.matmul(ps[:, 5, 0:D], ones[:, :], turned[:, j % 2, :], start=False, stop=(j == TU - 1),
                                  skip_group_check=True).then_inc(s_sq_used, 1)
                pe.drain().then_inc(s_sum, 1)

            def sum_chunk(order, width, i, j):
                c = NCH * order + U * i + j
                pe.wait_ge(s_oh, c + 1)
                pe.wait_ge(s_g[j], 16 * (CI * order + i + 1))
                pe.wait_ge(s_add, U + c - BANKS + 1)
                pe.matmul(ps[:, j % BANKS, 0:width], one_hot_at(j % OHS), g[:, j, 0:width],
                          start=True, stop=True).then_inc(s_mm, 1)

            def sums(order, width):
                with pe.Fori(0, CI) as i:
                    for j in range(U):
                        sum_chunk(order, width, i, j)

            pe.wait_ge(s_cnt, 1)
            pe.matmul(ps[:, 5, 0:NB], upper, cnt_b, start=True, stop=True)
            pe.matmul(ps[:, 5, 64:64 + NB], ones[:, :], cnt_b, start=True, stop=True).then_inc(s_tot, 1)

            pe.wait_ge(s_wt, 4)
            one_product(0, 0)
            sum_nodes(0)

            def two_products(i, j):
                pe.wait_ge(s_evac[1], 1 + TU * i + before(j))
                product(ps[:, j % 2, 0:D], j % 2, wt[:, 1])
                product(ps[:, 2 + j % 2, 0:D], j % 2, wt[:, 2]).then_inc(s_prod[1], 1)

            turn_tiles(1, two_products)
            pe.wait_ge(s_evac[1], 1 + NT)
            def last_steps(j, v, t):
                if v is not None and j == 2:
                    pe.wait_ge(s_stage[2], v + 1)
                    pe.wait_ge(s_turned[2], 1 + v)
                    for k in range(KD):
                        ins = pe.transpose(ps[:, 7, k * P:(k + 1) * P], stage[:, 0, k * P:(k + 1) * P], ident[:, :])
                    ins.then_inc(s_turn[2], 1)
                if v is not None and j == 8:
                    pe.wait_ge(s_turned[2], 1 + v + 1)
                    pe.wait_ge(s_evac[2], 1 + v)
                    product(ps[:, 6, 0:D], 0, wt[:, 3]).then_inc(s_prod[2], 1)

            def last_trip(i, v, t):
                for j in range(U):
                    sum_chunk(0, D, i, j)
                    last_steps(j, v, t)

            def last_dense(v, t):
                for j in range(U):
                    last_steps(j, v, t)

            beside_sweep(pe, last_trip, last_dense)
            sum_nodes(1)

            pe.wait_ge(s_rel_out[0], 16)
            relations = [v.rearrange("p k r d -> p k (r d)") for v in wrel]

            def rel_products(i, j):
                for q in range(4):
                    if q % 2:
                        pe.wait_ge(s_rel_act, 1 + 2 * (TU * i + j))
                    else:
                        pe.wait_ge(s_rel_dve, 1 + 2 * (TU * i + j))
                    for k in range(KD):
                        ins = pe.matmul(ps[:, q, :], turned[:, j % 2, k * P:(k + 1) * P],
                                        relations[0][:, k, q * 512:(q + 1) * 512], start=(k == 0), stop=(k == KD - 1))
                    ins.then_inc(s_rel_mm, 1)
                pe.wait_ge(s_evac[3], 1 + TU * i + j)
                product(ps[:, 4, 0:D], j % 2, wroot1[:, 0]).then_inc(s_prod[3], 1)

            pe.wait_ge(s_wrel[0], 32)
            turn_tiles(3, rel_products)
            pe.wait_ge(s_rel_act, 1 + 2 * NT)
            pe.wait_ge(s_rel_dve, 1 + 2 * NT)
            pe.wait_ge(s_evac[3], 1 + NT)
            for layer in range(1, L1):
                w, ph = relations[layer % 2], 3 + layer

                def rel_turn(t):
                    pe.wait_ge(s_stage[ph], t + 1)
                    pe.wait_ge(s_turned[ph], 1 + t)
                    for k in range(KD):
                        ins = pe.transpose(ps[:, 7, k * P:(k + 1) * P], stage[:, 0, k * P:(k + 1) * P], ident[:, :])
                    ins.then_inc(s_turn[ph], 1)

                def rel_quarter(t, q):
                    if q == 0:
                        pe.wait_ge(s_turned[ph], 1 + t + 1)
                    pe.wait_ge(s_quarter, 4 * (NT * (layer - 1) + t) + q + 1)
                    for k in range(KD):
                        ins = pe.matmul(ps[:, 4 + q % 2, :], turned[:, 0, k * P:(k + 1) * P],
                                        w[:, k, q * 512:(q + 1) * 512], start=(k == 0), stop=(k == KD - 1))
                    ins.then_inc(s_quarter_mm, 1)

                def rel_root(t):
                    pe.wait_ge(s_evac[ph], 1 + t)
                    product(ps[:, 6, 0:D], 0, wroot1[:, layer]).then_inc(s_prod[ph], 1)

                def steps(j, v, t):
                    if v is not None and j == 2:
                        rel_turn(v)
                    if v is not None and j in (5, 8, 11, U - 1):
                        rel_quarter(v, (5, 8, 11, U - 1).index(j))
                    if v is not None and j == U - 1:
                        rel_root(v)

                def trip(i, v, t):
                    for j in range(U):
                        sum_chunk(layer, D, i, j)
                        steps(j, v, t)

                def dense(v, t):
                    for j in range(U):
                        steps(j, v, t)

                pe.wait_ge(s_wrel[layer], 32)
                beside_sweep(pe, trip, dense)
                pe.wait_ge(s_evac[ph], 1 + NT)
            sums(L1, D)
            pe.wait_ge(s_add, U + NCH * (1 + L1))

            pe.wait_ge(s_w2, 96)
            for w in range(2):
                for k in range(KD):
                    if w:
                        pe.wait_ge(s_gru_w, k + 1)
                    for b in range(nb2):
                        ins = pe.transpose(ps[:, 2 * k + b // 4, b % 4 * P:(b % 4 + 1) * P],
                                           nat2[:, w, b, k * P:(k + 1) * P], ident[:, :])
                    ins.then_inc(s_turn_w2, 1)
            for k in range(KD):
                ins = pe.transpose(ps[:, 4, k * R2:(k + 1) * R2], relvec[:, k * P:(k + 1) * P], ident[0:R2, 0:R2])
            ins.then_inc(s_turn_w2, 1)
            pe.wait_ge(s_gru_w, 2 * KD + 1)
            for o, lo, hi in ((ps[0:R2, 5, :], 0, 512), (ps[0:R2, 6, 0:G3 - 512], 512, G3)):
                for k in range(KD):
                    ins = pe.matmul(o, relvec_t[:, k, :], wt2[:, 0, k, lo:hi], start=(k == 0), stop=(k == KD - 1))
            ins.then_inc(s_turn_w2, 1)
            pe.wait_ge(s_gru_w, 2 * KD + 2)
            pe.wait_ge(s_w3, 96)

            def gru_steps(j, v, t, u):
                rz, inp, hid = ps[:, 4, :], ps[:, 5, 0:D], ps[:, 5, D:2 * D]
                if t is not None and j == 1:
                    pe.wait_ge(s_cand, 1 + t)
                    pe.matmul(rz, cturned, rel_gates[:, 0:2 * D], start=False, stop=True)
                    for k in range(KD):
                        pe.matmul(inp, turned[:, 0, k * P:(k + 1) * P], wt2[:, 0, k, 2 * D:G3], start=(k == 0), stop=False)
                    pe.matmul(inp, cturned, rel_gates[:, 2 * D:G3], start=False, stop=True)
                if t is not None and j == 3:
                    for k in range(KD):
                        ins = pe.matmul(hid, turned2[:, k * P:(k + 1) * P], wt2[:, 1, k, 2 * D:G3],
                                        start=(k == 0), stop=(k == KD - 1))
                    ins.then_inc(s_prod[6], 1)
                if u is not None and j == 6:
                    pe.wait_ge(s_stage[7], u + 1)
                    if t is not None:
                        pe.wait_ge(s_turned[6], 1 + t + 1)
                    for k in range(KD):
                        ins = pe.transpose(ps[:, 7, k * P:(k + 1) * P], stage[:, 1, k * P:(k + 1) * P], ident[:, :])
                    ins.then_inc(s_turn[7], 1)
                if u is not None and j == 8:
                    pe.wait_ge(s_turned[7], 1 + u + 1)
                    product(ps[:, 7, D:2 * D], 1, w3).then_inc(s_prod[7], 1)
                if v is not None and j == 12:
                    pe.wait_ge(s_stage[6], v + 1)
                    pe.wait_ge(s_turned[6], 1 + v)
                    if u is not None:
                        pe.wait_ge(s_evac[7], 1 + u + 1)
                    for w, at in ((stage[:, 0, :], 0), (stage2, D)):
                        for k in range(KD):
                            pe.transpose(ps[:, 6, at + k * P:at + (k + 1) * P], w[:, k * P:(k + 1) * P], ident[:, :])
                    pe.transpose(ps[0:RB, 7, 0:P], cstage, ident[:, :]).then_inc(s_turn[6], 1)
                if v is not None and j == U - 1:
                    pe.wait_ge(s_turned[6], 1 + v + 1)
                    pe.wait_ge(s_gates, 1 + v)
                    for k in range(KD):
                        x_k, h_k = turned[:, 0, k * P:(k + 1) * P], turned2[:, k * P:(k + 1) * P]
                        pe.matmul(rz, x_k, wt2[:, 0, k, 0:2 * D], start=(k == 0), stop=False)
                        pe.matmul(rz, h_k, wt2[:, 1, k, 0:2 * D], start=False, stop=False)

            def gru_trip(i, v, t, u):
                for j in range(U):
                    sum_chunk(4, D + R2, i, j)
                    gru_steps(j, v, t, u)

            beside_gru(pe, gru_trip, gru_steps)
            pe.wait_ge(s_add, U + NCH * 5)
            pe.wait_ge(s_evac[7], 1 + NT)
            with pe.Fori(0, CI) as i:
                for j in range(U):
                    c = U * i + j
                    pe.wait_ge(s_diag, c + 1)
                    pe.wait_ge(s_diag_dve, c + 1)
                    pe.wait_ge(s_miss, c + 1)
                    pe.wait_ge(s_red, U + c - 8 + 1)
                    o = ps[:, j % 8, :]
                    pe.matmul(o, ones[:, :], diag[:, j % RING].rearrange("p h e -> p (h e)"), start=True, stop=False)
                    pe.matmul(o, miss[:, j % RING2, :], big_ident[:, :, :].rearrange("p h e -> p (h e)"),
                              start=False, stop=True).then_inc(s_spread, 1)
            pe.wait_ge(s_self, 1)
            pe.wait_ge(s_acc0, 1)

            def second_pass(i, due, steps):
                buckets = lagged_buckets(mybir.EngineType.PE, i, 2)
                for k in range(steps):
                    if due(k, 9):
                        c, j, r = U * i + k - 9, (k - 9) % U, (k - 9) % RING2
                        pe.wait_ge(s_wr, c + 1)
                        pe.wait_ge(s_wr_act, c + 1)
                        pe.wait_ge(s_add3, U + c - BANKS + 1)
                        pe.matmul(ps[:, j % BANKS, 0:W3], ohb[:, j, :], wrow[:, r, :], start=True, stop=True)\
                            .then_inc(s_mm3, 1)
                    if due(k, 0):
                        c = U * i + k
                        pe.wait_ge(s_ohb, c + 1)
                        pe.wait_ge(s_ohts, U + c - 2 + 1)
                        pe.transpose(ps[:, 4 + k % 2, 0:P], ohb[:, k, :], ident[:, :]).then_inc(s_oht, 1)
                    if due(k, 2):
                        c, s = U * i + k - 2, (k - 2) % RING
                        pe.wait_ge(s_ohts, U + c + 1)
                        pe.wait_ge(s_l0, U + c - 2 + 1)
                        pe.matmul(ps[:, 6 + k % 2, 0:2 * H], ohT[:, s, :], node_l[:, bass.ds(buckets[k], 1), H:3 * H].rearrange("p o h -> p (o h)"),
                                  start=True, stop=True).then_inc(s_dm, 1)

            trips(pe, second_pass)

        @block.vector
        def _(dve):
            link = Link(dve, s_dve)
            dve.sem_inc(s_add, U)
            dve.sem_inc(s_red, U)
            dve.sem_inc(s_e, U)
            dve.sem_inc(s_cand, 1)
            dve.sem_inc(s_l0, U)
            dve.sem_inc(s_add3, U)
            dve.sem_inc(s_maxed, U)
            for s in s_evac + [s_rel_dve]:
                dve.sem_inc(s, 1)

            dve.wait_ge(s_const, 5)
            dve.tensor_scalar(upper, col[:, :], prow, None, ALU.is_gt)
            dve.tensor_scalar(pmask, prow, float(LAST), None, ALU.is_lt)
            link(dve.tensor_scalar(ident[:, :], col[:, :], prow, None, ALU.is_equal))
            for h in range(H):
                ins = dve.tensor_scalar(big_ident[:, h, :], ident[:, :], BIG, None, ALU.mult)
            ins.then_inc(s_ident, 1)

            dst_i, src_i, rel_i, typ_i, int_w = (tmp(k, I32) for k in range(5))
            bucket, node, work, rank, pos = (tmp(k) for k in range(5, 10))
            dve.wait_ge(s_edge_in, 16 * 8)
            link(dve.tensor_scalar(int_w, dst_i, 7, None, ALU.logical_shift_right))
            link(dve.tensor_copy(bucket, int_w))
            link(dve.tensor_copy(node, dst_i))
            link(dve.scalar_tensor_tensor(node, bucket, -float(P), node, ALU.mult, ALU.add))
            link(dve.tensor_scalar(work, bucket, float(NT), float(P), ALU.is_equal, ALU.mult))
            link(dve.tensor_tensor(payload_f[:, :, 2], node, work, ALU.add))
            link(dve.tensor_copy(payload[:, :, 0], src_i))
            link(dve.tensor_copy(payload_f[:, :, 3], typ_i))
            link(dve.tensor_copy(node, rel_i))
            link(dve.tensor_copy(work, src_i))
            link(dve.scalar_tensor_tensor(payload[:, :, 1], node, float(NP), work, ALU.mult, ALU.add))
            link(dve.memset(pos, 0.0))
            mine, ranks = (work, tmp(0)), (rank, tmp(1))
            with dve.Fori(0, NB // 2) as b:
                link.enter(b, 10)
                for k in range(2):
                    if k:
                        link.ended(1)
                    link.begin(dve.tensor_scalar(mine[k], bucket, iota_b[:, bass.ds(2 * b + k, 1)], None, ALU.is_equal))
                for k in range(2):
                    link.ended(1)
                    link.begin(dve.tensor_tensor_scan(ranks[k], mine[k], mine[k], 0.0, ALU.add, ALU.max))
                link.ended(1)
                for k in range(2):
                    link.begin(dve.tensor_scalar(cnt_b[:, bass.ds(2 * b + k, 1)], ranks[k][:, EC - 1:EC], 1.0, None,
                                                 ALU.mult))
                    link.begin(dve.tensor_tensor(mine[k], ranks[k], mine[k], ALU.mult))
                    if k == 0:
                        link.ended(2)
                link.ended(2)
                link.begin(dve.tensor_tensor(pos, pos, mine[0], ALU.add))
                link.ended()
                link.begin(dve.tensor_tensor(pos, pos, mine[1], ALU.add))
                link.leave(NB // 2)
            link.ended()
            dve.sem_inc(s_cnt, 1)
            dve.wait_ge(s_tot, 1)
            before_p, total_p = ps[:, 5, 0:NB], ps[:, 5, 64:64 + NB]

            def by_bucket(v):
                return v.rearrange("p (b o) -> p b o", o=1).broadcast_to([P, NB, NB])

            def by_other(v):
                return v.rearrange("p (o b) -> p o b", o=1).broadcast_to([P, NB, NB])

            int_b, chunks_i = before_b.bitcast(I32), tot_b.bitcast(I32)
            link(dve.tensor_scalar(int_b, total_p, float(P - 1), None, ALU.add))
            link(dve.tensor_scalar(chunks_i, int_b, 7, None, ALU.logical_shift_right))
            link(dve.tensor_copy(nch_b, chunks_i))
            link(dve.scalar_tensor_tensor(key_b, nch_b, 64.0, iota_b, ALU.mult, ALU.add))
            link(dve.memset(key_b[:, NT:NB], 64.0 * (NCH + 1)))
            link(dve.tensor_tensor(pairs, by_other(key_b), by_bucket(key_b), ALU.is_lt))
            link(dve.tensor_reduce(rank_b, pairs, AX, ALU.add))
            link(dve.tensor_tensor(pairs, pairs, by_other(nch_b), ALU.mult))
            link(dve.tensor_reduce(first_b, pairs, AX, ALU.add))
            link(dve.tensor_tensor(end_b, first_b, nch_b, ALU.add))
            link(dve.tensor_scalar(base_b, first_b, float(P), -1.0, ALU.mult, ALU.add))
            link(dve.tensor_tensor(base_b, base_b, before_p, ALU.add))
            with dve.Fori(0, NB // 2) as b:
                link.enter(b, 4)
                for k in range(2):
                    if k:
                        link.ended(1)
                    link.begin(dve.tensor_scalar(mine[k], bucket, iota_b[:, bass.ds(2 * b + k, 1)],
                                                 base_b[:, bass.ds(2 * b + k, 1)], ALU.is_equal, ALU.mult))
                for k in range(2):
                    link.ended(1 - k)
                    link.begin(dve.tensor_tensor(pos, pos, mine[k], ALU.add))
                link.leave(NB // 2)
            link.ended()
            link(dve.tensor_copy(int_w, pos))
            link(dve.tensor_scalar(dst_i, int_w, P - 1, None, ALU.bitwise_and))
            link(dve.tensor_scalar(src_i, int_w, 7, None, ALU.logical_shift_right))
            link(dve.tensor_copy(node, dst_i))
            link(dve.tensor_copy(work, src_i))
            dve.scalar_tensor_tensor(slot_row, node, float(NCH), work, ALU.mult, ALU.add).then_inc(s_slot, 1)
            link(dve.tensor_tensor(pairs, by_other(rank_b), by_bucket(iota_b), ALU.is_equal))
            link(dve.tensor_tensor(pairs, pairs, by_other(iota_b), ALU.mult))
            link(dve.tensor_reduce(order_f, pairs, AX, ALU.add))
            link(dve.tensor_copy(order_of[0:1, :], order_f[0:1, 0:NT]))
            bf, cn = bucket_f[0:1, :], chunk_no[0:1, :]
            link(dve.tensor_scalar(bf, cn, first_b[0:1, NT:NB], order_f[0:1, NT - 1:NT], ALU.is_ge, ALU.mult))
            with dve.Fori(1, NT) as b:
                link.enter(b - 1, 3)
                dve.tensor_scalar(from_first, cn, first_b[0:1, bass.ds(b, 1)], iota_b[0:1, bass.ds(b, 1)],
                                  ALU.is_ge, ALU.mult)
                link(dve.tensor_scalar(from_end, cn, end_b[0:1, bass.ds(b, 1)], iota_b[0:1, bass.ds(b, 1)],
                                       ALU.is_ge, ALU.mult))
                link(dve.tensor_tensor(bf, bf, from_first, ALU.add))
                link(dve.tensor_tensor(bf, bf, from_end, ALU.subtract))
                link.leave(NT - 1)
            link(dve.tensor_copy(bucket_of[0:1, :], bf))

            def evacuate(ph, take):
                with dve.Fori(0, TI) as i:
                    for j in range(TU):
                        dve.wait_ge(s_prod[ph], 1 + TU * i + j + 1)
                        take(i, j).then_inc(s_evac[ph], 1)
                dve.wait_ge(s_evac[ph], 1 + NT)

            roots = [0]

            def root(v):
                roots[0] += 1
                dve.sem_inc(s_var, 1)
                dve.wait_ge(s_root, roots[0])
                link(dve.reciprocal(v, v))

            def batch_norm(k, gamma, beta):
                link(dve.tensor_scalar(Y3[:, NT - 1, :], Y3[:, NT - 1, :], pmask, None, ALU.mult))
                dve.sem_inc(s_y, 1)
                dve.wait_ge(s_sum, 2 * k + 1)
                link(dve.tensor_scalar(mean_b, ps[:, 4, 0:D], 1.0 / N, None, ALU.mult))
                link(dve.tensor_tensor(Y3, Y3, over_tiles(mean_b), ALU.subtract))
                link(dve.tensor_scalar(Y3[:, NT - 1, :], Y3[:, NT - 1, :], pmask, None, ALU.mult))
                dve.sem_inc(s_dev, 1)
                dve.wait_ge(s_sum, 2 * k + 2)
                link(dve.tensor_scalar(scale_b, ps[:, 5, 0:D], 1.0 / N, EPS, ALU.mult, ALU.add))
                root(scale_b)
                link(dve.tensor_tensor(scale_b, scale_b, gamma, ALU.mult))
                link(dve.tensor_tensor(Y3, Y3, over_tiles(scale_b), ALU.mult))
                link(dve.tensor_tensor(Y3, Y3, over_tiles(beta), ALU.add))

            def layer_norm(v):
                with dve.Fori(0, TI) as i:
                    link.enter(i, 1)
                    for j in range(TU):
                        ins = dve.bn_stats(tile_at(stats, TU * i + j, 6), tile_at(v, TU * i + j))
                    link(ins)
                    link.leave(TI)
                mean_e, sq_e, mean_o, sq_o = (stats[:, :, n] for n in (1, 2, 4, 5))
                mean, var = mv[:, :, 0], mv[:, :, 1]
                link(dve.tensor_tensor(mean, mean_e, mean_o, ALU.add))
                link(dve.tensor_tensor(mean_e, mean_e, mean_o, ALU.subtract))
                link(dve.tensor_scalar(mean, mean, 0.5, None, ALU.mult))
                link(dve.tensor_tensor(var, sq_e, sq_o, ALU.add))
                link(dve.tensor_tensor(mean_e, mean_e, mean_e, ALU.mult))
                link(dve.scalar_tensor_tensor(var, mean_e, D / 4.0, var, ALU.mult, ALU.add))
                link(dve.tensor_scalar(var, var, 1.0 / D, EPS, ALU.mult, ALU.add))
                root(mv[:, :, 1])
                with dve.Fori(0, TI) as i:
                    link.enter(i, 1)
                    for j in range(TU):
                        t = TU * i + j
                        ins = dve.tensor_scalar(tile_at(v, t), tile_at(v, t), mv[:, bass.ds(t, 1), 0],
                                                mv[:, bass.ds(t, 1), 1], ALU.subtract, ALU.mult)
                    link(ins)
                    link.leave(TI)

            def sums_trip(order, i, with_types=False, beside=None):
                def one_hot(j):
                    c = NCH * order + U * i + j
                    dve.wait_ge(s_mm, U + c - OHS + 1)
                    if with_types:
                        dve.tensor_scalar(g[:, j, D:D + R2], col[:, 0:R2], edges_f[:, 3, bass.ds(U * i + j, 1)],
                                          None, ALU.is_equal)
                    dve.tensor_scalar(one_hot_at(j % OHS), col[:, :], edges_f[:, 2, bass.ds(U * i + j, 1)],
                                      None, ALU.is_equal).then_inc(s_oh, 1)

                for j in range(AHEAD):
                    one_hot(j)
                buckets = buckets_of(mybir.EngineType.DVE, i)
                for j in range(U):
                    if j + AHEAD < U:
                        one_hot(j + AHEAD)
                    c = NCH * order + U * i + j
                    t = buckets[j]
                    dve.wait_ge(s_mm, U + c + 1)
                    dve.wait_ge(s_add, U + c)
                    width = D + R2 if with_types else D
                    dve.tensor_tensor(tile_at(A, t, width), tile_at(A, t, width), ps[:, j % BANKS, 0:width], ALU.add)\
                        .then_inc(s_add, 1)
                    if beside:
                        beside(j)

            def sums(order):
                with dve.Fori(0, CI) as i:
                    sums_trip(order, i)
                dve.wait_ge(s_add, U + NCH * (order + 1))

            dve.wait_ge(s_rows0, 16 * 7)
            evacuate(0, lambda i, j: dve.tensor_tensor(tile_at(Y3, TU * i + j), ps[:, j % 2, 0:D], B1, ALU.add))
            batch_norm(0, G1, BETA1)
            dve.sem_inc(s_h, 1)

            def take1(i, j):
                dve.tensor_tensor(tile_at(A, TU * i + j), ps[:, 2 + j % 2, 0:D], BR, ALU.add)
                dve.wait_ge(s_out0[j % 2], 16 * (1 + ((TU + 1) // 2 if j % 2 == 0 else TU // 2) * i + j // 2))
                return dve.tensor_copy(out0[:, j % 2, :], ps[:, j % 2, 0:D])

            evacuate(1, take1)
            for b in range(2):
                dve.wait_ge(s_out0[b], 16 * (1 + out_uses[b]))
            dve.wait_ge(s_planes, 4)
            def take_last(t):
                bucket = bucket_by_size(mybir.EngineType.DVE, t)
                dve.wait_ge(s_prod[2], 1 + t + 1)
                dve.tensor_tensor(tile_at(Y3, bucket), ps[:, 6, 0:D], B2, ALU.add).then_inc(s_evac[2], 1)

            def last_trip(i, v, t):
                sums_trip(0, i, beside=lambda j: take_last(t) if t is not None and j == 4 else None)

            beside_sweep(dve, last_trip, lambda v, t: take_last(t))
            dve.wait_ge(s_evac[2], 1 + NT)
            batch_norm(1, G2, BETA2)
            link(dve.scalar_tensor_tensor(X[:, :, :], X[:, :, :], 2.0, Y3, ALU.mult, ALU.add))
            layer_norm(X)
            dve.sem_inc(s_x, 1)

            dve.wait_ge(s_rel_out[1], 16)
            def take_rel(i, j):
                for q in (0, 2):
                    dve.wait_ge(s_rel_mm, 4 * (TU * i + j) + q + 1)
                    if q == 0:
                        dve.wait_ge(s_rel_out[j % 2], 16 * (
                            1 + ((TU + 1) // 2 if j % 2 == 0 else TU // 2) * i + j // 2))
                    dve.tensor_copy(rel_out[:, j % 2, 2 * q:2 * q + 2, :].rearrange("p r d -> p (r d)"),
                                    ps[:, q, :]).then_inc(s_rel_dve, 1)
                dve.wait_ge(s_prod[3], 1 + TU * i + j + 1)
                return dve.tensor_tensor(tile_at(A, TU * i + j), ps[:, 4, 0:D], bias1[:, 0, :], ALU.add)

            with dve.Fori(0, TI) as i:
                for j in range(TU):
                    take_rel(i, j).then_inc(s_evac[3], 1)
            dve.wait_ge(s_evac[3], 1 + NT)
            for layer in range(1, L1):
                def take_root(t):
                    bucket = bucket_by_size(mybir.EngineType.DVE, t)
                    dve.wait_ge(s_prod[3 + layer], 1 + t + 1)
                    dve.tensor_tensor(tile_at(A, bucket), ps[:, 6, 0:D], bias1[:, layer, :], ALU.add)\
                        .then_inc(s_evac[3 + layer], 1)

                def trip(i, v, t):
                    sums_trip(layer, i, beside=lambda j: take_root(t) if t is not None and j == 4 else None)

                beside_sweep(dve, trip, lambda v, t: take_root(t))
                dve.wait_ge(s_evac[3 + layer], 1 + NT)
            sums(L1)
            link(dve.scalar_tensor_tensor(X[:, :, :], A2, 0.0, X[:, :, :], ALU.max, ALU.add))
            layer_norm(X)
            link(dve.memset(A[:, :, :], 0.0))
            link(dve.memset(cstage[:, R2:RB], 1.0))
            link(dve.memset(rel_gates, 0.0))
            dve.sem_inc(s_x, 1)
            steps_t, steps_u = 8, 3

            def gru_steps(j, t, u, bt, bu):
                if t is not None or u is not None:
                    link.ended()
                if u is not None:
                    features = ps[:, 7, D:2 * D]
                    if j == 2:
                        dve.wait_ge(s_root1, u + 1)
                        link.begin(dve.reciprocal(mv1[:, 1:2], mv1[:, 1:2]))
                    if j == 3:
                        dve.tensor_scalar(tile_at(X, bu), tile_at(X, bu), mv1[:, 0:1], mv1[:, 1:2],
                                          ALU.subtract, ALU.mult).then_inc(s_norm, 1)
                    if j == 9:
                        dve.wait_ge(s_prod[7], 1 + u + 1)
                        dve.tensor_scalar(tile_at(A, bu), features, 1.0, None, ALU.mult)
                        link.begin(dve.tensor_tensor(
                            att_tmp.rearrange("p (s d) -> p s d", s=2),
                            features.rearrange("p (o d) -> p o d", o=1).broadcast_to([P, 2, D]), att_st, ALU.mult))
                    if j == 10:
                        dve.sem_inc(s_evac[7], 1)
                        link.begin(dve.tensor_reduce(tile_at(node_l, bu, 2 * H),
                                                     att_tmp.rearrange("p (h f) -> p h f", f=F), AX, ALU.add))
                    if j == 11:
                        dve.tensor_scalar(A[:, bass.ds(bu, 1), D:W3].rearrange("p o h -> p (o h)"),
                                          tile_at(node_l, bu, H), 1.0, None, ALU.mult).then_inc(s_att_row, 1)
                if t is not None:
                    if j == 5:
                        dve.wait_ge(s_prod[6], 1 + t + 1)
                        link.begin(dve.tensor_tensor(hn, ps[:, 5, D:2 * D], b_hn, ALU.add))
                    if j == 6:
                        dve.wait_ge(s_gates, 1 + t + 1)
                        link.begin(dve.tensor_tensor(hn, hn, gates[:, 0:D], ALU.mult))
                    if j == 7:
                        dve.tensor_tensor(inn, ps[:, 5, 0:D], hn, ALU.add).then_inc(s_cand, 1)
                    if j == 10:
                        dve.wait_ge(s_tanh, t + 1)
                        link.begin(dve.tensor_tensor(hn, tile_at(X, bt), inn, ALU.subtract))
                    if j == 11:
                        link.begin(dve.tensor_tensor(hn, hn, gates[:, D:2 * D], ALU.mult))
                    if j == 12:
                        link.begin(dve.tensor_tensor(hn, hn, inn, ALU.add))
                    if j == 13:
                        link.begin(dve.tensor_tensor(tile_at(X, bt), tile_at(X, bt), hn, ALU.add))
                    if j == 14:
                        dve.sem_inc(s_stat_begun, 1)
                        link.begin(dve.bn_stats(stats1, tile_at(X, bt)))
                    if j == 15:
                        dve.sem_inc(s_stat_begun, 1)
                        link(dve.bn_aggr(mv1, stats1))
                        dve.tensor_scalar(mv1[:, 1:2], mv1[:, 1:2], EPS, None, ALU.add).then_inc(s_var1, 1)

            def gru_buckets(t, u):
                return [None if v is None else bucket_by_size(mybir.EngineType.DVE, v) for v in (t, u)]

            def gru_trip(i, v, t, u):
                bt, bu = gru_buckets(t, u)
                if u is not None:
                    link.enter(i - READY - 2, steps_t + steps_u)
                sums_trip(4, i, True, lambda j: gru_steps(j, t, u, bt, bu))
                if u is not None:
                    link.leave(CI - READY - 2)

            def gru_hook(j, v, t, u):
                if j == 0:
                    tail[:] = gru_buckets(t, u)
                gru_steps(j, t, u, *tail)

            tail = []
            dve.wait_ge(s_w2, 96)
            dve.wait_ge(s_w3, 96)
            beside_gru(dve, gru_trip, gru_hook)
            dve.wait_ge(s_add, U + NCH * 5)
            dve.wait_ge(s_att_row, NT)
            dve.sem_inc(s_logit, 1)
            link(dve.tensor_copy(max_l, src_l))
            def first_pass(i, due, steps):
                buckets = lagged_buckets(mybir.EngineType.DVE, i, 5)
                for k in range(steps):
                    if due(k, 0):
                        c = U * i + k
                        dve.wait_ge(s_spread, U + c - RING2 + 1)
                        dve.tensor_scalar(miss[:, k % RING2, :], col[:, :], edges_f[:, 2, bass.ds(c, 1)], -1.0,
                                          ALU.is_equal, ALU.add).then_inc(s_miss, 1)
                    if due(k, 1):
                        c, j = U * i + k - 1, (k - 1) % U
                        dve.wait_ge(s_g[j], 16 * (CI * 5 + (i if k >= 1 else i - 1) + 1))
                        dve.wait_ge(s_spread, U + c - RING + 1)
                        dve.tensor_scalar(diag[:, j % RING, H - 1, :], ident[:, :], g[:, j, H - 1:H], None, ALU.mult)\
                            .then_inc(s_diag_dve, 1)
                    if due(k, 4):
                        c, j = U * i + k - 4, (k - 4) % U
                        dve.wait_ge(s_spread, U + c + 1)
                        dve.wait_ge(s_maxed, U + c - RING + 1)
                        dve.tensor_reduce(red[:, j % RING, :], ps[:, j % 8, :].rearrange("p (h e) -> p h e", h=H),
                                          AX, ALU.max).then_inc(s_red, 1)
                    if due(k, 5):
                        c, j = U * i + k - 5, (k - 5) % U
                        t = buckets[k]
                        dve.wait_ge(s_red, U + c + 1)
                        dve.wait_ge(s_maxed, U + c)
                        dve.tensor_tensor(tile_at(max_l, t, H), tile_at(max_l, t, H), red[:, j % RING, :], ALU.max)\
                            .then_inc(s_maxed, 1)

            trips(dve, first_pass)
            dve.wait_ge(s_maxed, U + NCH)

            link(dve.tensor_tensor(max_l, max_l, dst_l, ALU.add))
            link(dve.scalar_tensor_tensor(m_l, max_l, 0.2, max_l, ALU.mult, ALU.max))
            link(dve.tensor_tensor(t_l, src_l, dst_l, ALU.add))
            link(dve.scalar_tensor_tensor(t_l, t_l, 0.2, t_l, ALU.mult, ALU.max))
            link(dve.tensor_tensor(t_l, t_l, m_l, ALU.subtract))
            dve.sem_inc(s_shift, 1)
            dve.wait_ge(s_self, 1)
            dve.wait_ge(s_att_out, 16)
            link(dve.tensor_copy(A[:, :, D:W3], ex_l))
            a4 = A2.rearrange("p t (h f) -> p t h f", h=H)
            link(dve.memset(g[:, :, W3:W3 + H], 0.0))

            def by_head(v):
                return v.rearrange("p t (h o) -> p t h o", o=1).broadcast_to([P, NT, H, F])

            link(dve.tensor_tensor(a4, a4, by_head(ex_l), ALU.mult))
            dve.sem_inc(s_acc0, 1)
            def second_pass(i, due, steps):
                buckets = lagged_buckets(mybir.EngineType.DVE, i, 10)
                for k in range(steps):
                    if due(k, 0):
                        c = U * i + k
                        dve.wait_ge(s_mm3, U + c - U + 1)
                        dve.tensor_scalar(ohb[:, k, :], col[:, :], edges_f[:, 2, bass.ds(c, 1)], None,
                                          ALU.is_equal).then_inc(s_ohb, 1)
                    if due(k, 3):
                        c, j, s = U * i + k - 3, (k - 3) % U, (k - 3) % RING
                        dve.wait_ge(s_g[j], 16 * (CI * 6 + (i if k >= 3 else i - 1) + 1))
                        dve.wait_ge(s_dm, U + c + 1)
                        dve.tensor_tensor(lg[:, s, 0:2 * H], ps[:, 6 + s % 2, 0:2 * H], g[:, j, D:D + 2 * H], ALU.add)\
                            .then_inc(s_l0, 1)
                    if due(k, 4):
                        c, s = U * i + k - 4, (k - 4) % RING
                        dve.wait_ge(s_l0, U + c + 1)
                        dve.scalar_tensor_tensor(lg[:, s, 2 * H:3 * H], lg[:, s, 0:H], 0.2, lg[:, s, 0:H],
                                                 ALU.mult, ALU.max).then_inc(s_l1, 1)
                    if due(k, 5):
                        c, s = U * i + k - 5, (k - 5) % RING
                        dve.wait_ge(s_l1, c + 1)
                        dve.wait_ge(s_ex, U + c - RING + 1)
                        dve.tensor_tensor(lg[:, s, 3 * H:4 * H], lg[:, s, 2 * H:3 * H], lg[:, s, H:2 * H],
                                          ALU.subtract).then_inc(s_e, 1)
                    if due(k, 8):
                        c, j, r = U * i + k - 8, (k - 8) % U, (k - 8) % RING2
                        dve.wait_ge(s_ex, U + c + 1)
                        ex = wrow[:, r, D + HA:W3].rearrange("p (h o) -> p h o", o=1).broadcast_to([P, H - HA, F])
                        dve.tensor_tensor(wrow[:, r, HA * F:D].rearrange("p (h f) -> p h f", f=F),
                                          g[:, j, HA * F:D].rearrange("p (h f) -> p h f", f=F), ex, ALU.mult)\
                            .then_inc(s_wr, 1)
                    if due(k, 10):
                        c, j, t = U * i + k - 10, (k - 10) % U, buckets[k]
                        dve.wait_ge(s_mm3, U + c + 1)
                        dve.wait_ge(s_add3, U + c)
                        dve.tensor_tensor(tile_at(A, t, W3), tile_at(A, t, W3), ps[:, j % BANKS, 0:W3], ALU.add)\
                            .then_inc(s_add3, 1)

            trips(dve, second_pass)
            dve.wait_ge(s_add3, U + NCH)
            link(dve.tensor_scalar(A[:, :, D:W3], A[:, :, D:W3], 1e-16, None, ALU.add))
            link(dve.reciprocal(ex_l, A[:, :, D:W3]))
            link(dve.tensor_tensor(a4, a4, by_head(ex_l), ALU.mult))
            link(dve.tensor_tensor(A2, A2, over_tiles(bias3), ALU.add))
            link(dve.tensor_tensor(A2, A2, X[:, :, :], ALU.add))
            layer_norm(A2)
            link(dve.tensor_tensor(A2, A2, over_tiles(gamma3), ALU.mult))
            link(dve.tensor_tensor(A2, A2, over_tiles(beta3), ALU.add))
            link(dve.scalar_tensor_tensor(X[:, :, :], A2, 0.0, X[:, :, :], ALU.max, ALU.add))
            layer_norm(X)
            dve.sem_inc(s_x, 1)


_INS = ["x", "src", "dst", "edge_type_16", "edge_type_8"] + [f"L0_gnn_{n}" for n in (
    "w1", "b1", "g1", "beta1", "wr", "br", "wroot", "w2", "b2", "g2", "beta2")] + [
    "L1_gnn_W_rel", "L1_gnn_W_root", "L1_gnn_bias"] + [f"L2_gnn_{n}" for n in (
        "relvectors", "w_ih", "w_hh", "b_ih", "b_hh")] + [f"L3_gnn_{n}" for n in (
            "W", "att_src", "att_dst", "bias", "ln_gamma", "ln_beta")]


def kernel(**inputs):
    import numpy as np
    import concourse.bacc as bacc
    from concourse.bass_utils import run_bass_kernel_spmd

    nc = bacc.Bacc("TRN2", target_bir_lowering=False, num_devices=1)
    arrays, args = {}, {}
    for name in _INS:
        v = np.ascontiguousarray(inputs[name])
        arrays[f"in_{name}"] = v
        args[name] = nc.dram_tensor(f"in_{name}", v.shape, mybir.dt.from_np(v.dtype), kind="ExternalInput").ap()
    out = nc.dram_tensor("out", (N, D), F32, kind="ExternalOutput").ap()
    program(nc, args, out)
    r = run_bass_kernel_spmd(nc, [arrays], core_ids=[0])
    return r.results[0]["out"]
```
